# Optimizing a Trainium2 kernel written in Bass

```python
import numpy as np
import jax
import jax.numpy as jnp

def _softmax(x, axis=-1):
    return jax.nn.softmax(x, axis=axis)

def _gelu(x):
    return jax.nn.gelu(x, approximate=True)

def _silu(x):
    return jax.nn.silu(x)

def _sigmoid(x):
    return jax.nn.sigmoid(x)

def _layernorm(x, axis=-1, eps=1e-05):
    m = jnp.mean(x, axis=axis, keepdims=True)
    v = jnp.var(x, axis=axis, keepdims=True)
    return (x - m) / jnp.sqrt(v + eps)

def _scatter_add(tgt, idx, src, axis=0):
    return tgt.at[idx].add(src)

def _segment_sum(src, seg, n):
    return jax.ops.segment_sum(src, seg, n)
kernel_name = 'mk_perceiver_d1_seqx_r2_d1a2cd'

def setup_inputs(seed: int=0):
    np.random.seed(seed)
    _w = jnp.asarray

    def _rec_inputs():
        import jax
        import jax.numpy as jnp
        _rk = jax.random.key(seed)
        x = -0.0002928 + 1 * jax.random.normal(jax.random.fold_in(_rk, 1), (8, 128, 512), jnp.float32)
        _lenS = 128 - jax.random.randint(jax.random.fold_in(_rk, 7), (8,), 0, max(1, 128 // 4) + 1, jnp.int32)
        _lenS2 = 2048 - jax.random.randint(jax.random.fold_in(_rk, 8), (8,), 0, max(1, 2048 // 4) + 1, jnp.int32)
        _ctx_1024P = jax.random.normal(jax.random.fold_in(_rk, 11), (8, 16, 512), jnp.float32)
        _ctx_1024c = jax.random.dirichlet(jax.random.fold_in(_rk, 511), 0.3 * jnp.ones((16,), jnp.float32), (8, 2048))
        _ctx_1024t = jnp.einsum('bsk,bkd->bsd', _ctx_1024c, _ctx_1024P)
        _ctx_1024t = _ctx_1024t * jax.lax.rsqrt(jnp.mean(jnp.square(_ctx_1024t)) + 1e-12) * 0.953939
        ctx_1024 = 4.13588e-05 + 0.999923 * (_ctx_1024t + 0.3 * jax.random.normal(jax.random.fold_in(_rk, 611), (8, 2048, 512), jnp.float32))
        return (x, ctx_1024)
    x, ctx_1024 = _rec_inputs()

    def _L0_xattn_setup():
        import jax, jax.numpy as jnp
        import numpy as np
        D_MODEL = 512
        N_HEADS = 16
        D_HEAD = D_MODEL // N_HEADS
        key = jax.random.key(seed)
        ks = jax.random.split(key, 6)
        query = jax.random.normal(ks[0], (2, 1024, D_MODEL), dtype=jnp.float32)
        context = jax.random.normal(ks[1], (2, 2048, D_MODEL), dtype=jnp.float32)
        s = 1.0 / np.sqrt(D_MODEL)
        Wq = jax.random.normal(ks[2], (D_MODEL, D_MODEL), dtype=jnp.float32) * s
        Wk = jax.random.normal(ks[3], (D_MODEL, D_MODEL), dtype=jnp.float32) * s
        Wv = jax.random.normal(ks[4], (D_MODEL, D_MODEL), dtype=jnp.float32) * s
        Wo = jax.random.normal(ks[5], (D_MODEL, D_MODEL), dtype=jnp.float32) * s
        return {'query': query, 'context': context, 'Wq': Wq, 'Wk': Wk, 'Wv': Wv, 'Wo': Wo}
    _L0_xattn_all = _L0_xattn_setup()
    _L0_xattn_in = {k: v for k, v in _L0_xattn_all.items() if k in ('Wq', 'Wk', 'Wv', 'Wo')}
    del _L0_xattn_all

    def _L0_attn_setup():
        import jax, jax.numpy as jnp
        import numpy as np
        import math
        E = 512
        H = 16
        HD = E // H
        NBITS = 8

        def fake_quant(x, n_bits=NBITS):
            qmax = 2.0 ** (n_bits - 1) - 1.0
            qmin = -2.0 ** (n_bits - 1)
            scale = jnp.maximum(jnp.max(jnp.abs(x)) / qmax, 1e-08)
            xq = jnp.round(jnp.clip(x / scale, qmin, qmax)) * scale
            return x + jax.lax.stop_gradient(xq - x)
        key = jax.random.key(seed)
        ks = jax.random.split(key, 7)
        L, B = (1024, 2)
        query = jax.random.normal(ks[0], (L, B, E), dtype=jnp.float32)
        k_in = jax.random.normal(ks[1], (L, B, E), dtype=jnp.float32)
        v_in = jax.random.normal(ks[2], (L, B, E), dtype=jnp.float32)
        in_w = jax.random.normal(ks[3], (3 * E, E), dtype=jnp.float32) * (1.0 / math.sqrt(E))
        in_b = jax.random.normal(ks[4], (3 * E,), dtype=jnp.float32) * 0.01
        out_w = jax.random.normal(ks[5], (E, E), dtype=jnp.float32) * (1.0 / math.sqrt(E))
        out_b = jax.random.normal(ks[6], (E,), dtype=jnp.float32) * 0.01
        return {'query': query, 'key': k_in, 'value': v_in, 'in_w': in_w, 'in_b': in_b, 'out_w': out_w, 'out_b': out_b}
    _L0_attn_all = _L0_attn_setup()
    _L0_attn_in = {k: v for k, v in _L0_attn_all.items() if k in ('key', 'value', 'in_w', 'in_b', 'out_w', 'out_b')}
    del _L0_attn_all

    def _L0_ffn_setup():
        import jax, jax.numpy as jnp
        import numpy as np
        NUM_EXPERTS = 8
        TOP_K = 2
        CAP_RATIO = 1.25
        INIT_STD = 0.02
        key = jax.random.key(seed)
        k1, k2, k3, k4 = jax.random.split(key, 4)
        B, T, H, F = (4, 1024, 512, 2048)
        x = jax.random.normal(k1, (B, T, H), jnp.float32)
        router_w = jax.random.normal(k2, (NUM_EXPERTS, H), jnp.float32) * INIT_STD
        w1 = jax.random.normal(k3, (NUM_EXPERTS, H, F), jnp.float32) * INIT_STD
        w2 = jax.random.normal(k4, (NUM_EXPERTS, F, H), jnp.float32) * INIT_STD
        return {'x': x, 'router_w': router_w, 'w1': w1, 'w2': w2}
    _L0_ffn_all = _L0_ffn_setup()
    _L0_ffn_in = {k: v for k, v in _L0_ffn_all.items() if k in ('router_w', 'w1', 'w2')}
    del _L0_ffn_all
    return {'x': x, 'ctx_1024': ctx_1024, 'L0_xattn_Wq': _L0_xattn_in['Wq'], 'L0_xattn_Wk': _L0_xattn_in['Wk'], 'L0_xattn_Wv': _L0_xattn_in['Wv'], 'L0_xattn_Wo': _L0_xattn_in['Wo'], 'L0_attn_key': _L0_attn_in['key'], 'L0_attn_value': _L0_attn_in['value'], 'L0_attn_in_w': _L0_attn_in['in_w'], 'L0_attn_in_b': _L0_attn_in['in_b'], 'L0_attn_out_w': _L0_attn_in['out_w'], 'L0_attn_out_b': _L0_attn_in['out_b'], 'L0_ffn_router_w': _L0_ffn_in['router_w'], 'L0_ffn_w1': _L0_ffn_in['w1'], 'L0_ffn_w2': _L0_ffn_in['w2']}

def reference(x, ctx_1024, L0_xattn_Wq, L0_xattn_Wk, L0_xattn_Wv, L0_xattn_Wo, L0_attn_key, L0_attn_value, L0_attn_in_w, L0_attn_in_b, L0_attn_out_w, L0_attn_out_b, L0_ffn_router_w, L0_ffn_w1, L0_ffn_w2):
    import jax
    import jax.numpy as jnp

    def _L0_xattn_ref(query, context, Wq, Wk, Wv, Wo):
        import jax, jax.numpy as jnp
        import numpy as np
        D_MODEL = 512
        N_HEADS = 16
        D_HEAD = D_MODEL // N_HEADS
        B, T_q, D = query.shape
        T_c = context.shape[1]
        Q = (query @ Wq.T).reshape(B, T_q, N_HEADS, D_HEAD)
        K = (context @ Wk.T).reshape(B, T_c, N_HEADS, D_HEAD)
        V = (context @ Wv.T).reshape(B, T_c, N_HEADS, D_HEAD)
        scale = jnp.sqrt(jnp.asarray(D_HEAD, dtype=query.dtype))
        scores = jnp.einsum('bqhd,bkhd->bhqk', Q, K) / scale
        attn = jax.nn.softmax(scores, axis=-1)
        out = jnp.einsum('bhqk,bkhd->bqhd', attn, V).reshape(B, T_q, D)
        return out @ Wo.T

    def _L0_attn_ref(query, key, value, in_w, in_b, out_w, out_b):
        import jax, jax.numpy as jnp
        import numpy as np
        import math
        E = 512
        H = 16
        HD = E // H
        NBITS = 8

        def fake_quant(x, n_bits=NBITS):
            qmax = 2.0 ** (n_bits - 1) - 1.0
            qmin = -2.0 ** (n_bits - 1)
            scale = jnp.maximum(jnp.max(jnp.abs(x)) / qmax, 1e-08)
            xq = jnp.round(jnp.clip(x / scale, qmin, qmax)) * scale
            return x + jax.lax.stop_gradient(xq - x)
        L, B, _ = query.shape
        Wi = fake_quant(in_w)
        Wo = fake_quant(out_w)
        X = jnp.einsum('lbe,fe->lbf', query, Wi) + in_b
        X = fake_quant(X)
        Q, K, V = jnp.split(X, 3, axis=-1)
        q = Q.reshape(L, B * H, HD).transpose(1, 0, 2)
        k = K.reshape(L, B * H, HD).transpose(1, 0, 2)
        v = V.reshape(L, B * H, HD).transpose(1, 0, 2)
        q = q / math.sqrt(HD)
        q = fake_quant(q)
        attn = jnp.einsum('bqd,bkd->bqk', q, k)
        attn = jax.nn.softmax(attn, axis=-1)
        heads = jnp.einsum('bqk,bkd->bqd', attn, v)
        heads = fake_quant(heads)
        heads_r = heads.transpose(1, 0, 2).reshape(L * B, E)
        y = heads_r @ Wo.T + out_b
        y = y.reshape(L, B, E)
        return fake_quant(y)

    def _L0_ffn_ref(x, router_w, w1, w2):
        import jax, jax.numpy as jnp
        import numpy as np
        NUM_EXPERTS = 8
        TOP_K = 2
        CAP_RATIO = 1.25
        INIT_STD = 0.02
        B, T, H = x.shape
        E, K = (NUM_EXPERTS, TOP_K)
        xf = x.reshape(-1, H)
        N = xf.shape[0]
        P = N * K
        capacity = int(CAP_RATio * N * K / E) + 1 if False else int(CAP_RATIO * N * K / E) + 1
        logits = xf @ router_w.T
        probs = jax.nn.softmax(logits, axis=-1)
        k_probs, k_idx = jax.lax.top_k(probs, K)
        k_probs = k_probs / jnp.sum(k_probs, axis=-1, keepdims=True)
        flat_e = k_idx.reshape(-1)
        onehot = jax.nn.one_hot(flat_e, E, dtype=jnp.int32)
        rank = jnp.take_along_axis(jnp.cumsum(onehot, axis=0) - 1, flat_e[:, None], axis=1)[:, 0]
        keep = rank < capacity
        slot = jnp.minimum(rank, capacity - 1)
        token_id = jnp.arange(P) // K
        dispatched = jnp.where(keep[:, None], xf[token_id], 0.0)
        buf = jnp.zeros((E, capacity, H), x.dtype).at[flat_e, slot].add(dispatched)
        h = jax.nn.silu(jnp.einsum('ech,ehf->ecf', buf, w1))
        out_buf = jnp.einsum('ecf,efh->ech', h, w2)
        pair_out = out_buf[flat_e, slot] * keep[:, None].astype(x.dtype)
        combined = jnp.sum(pair_out.reshape(N, K, H) * k_probs[..., None], axis=1)
        return combined.reshape(B, T, H) + x
    x = x + _L0_xattn_ref(_layernorm(x, axis=-1), ctx_1024, L0_xattn_Wq, L0_xattn_Wk, L0_xattn_Wv, L0_xattn_Wo)
    x = x + _L0_attn_ref(_layernorm(x, axis=-1), L0_attn_key, L0_attn_value, L0_attn_in_w, L0_attn_in_b, L0_attn_out_w, L0_attn_out_b)
    x = x + _L0_ffn_ref(_layernorm(x, axis=-1), L0_ffn_router_w, L0_ffn_w1, L0_ffn_w2)
    return x

_drawn_inputs = setup_inputs


def setup_inputs(seed=0):
    import zlib

    import numpy as np

    out = dict(_drawn_inputs(seed))
    spreads = {}
    factors = {'L0_attn_in_b': 3.93, 'L0_attn_out_b': 5.219}
    for name, (base, spread) in spreads.items():
        noise = np.random.default_rng([zlib.crc32(name.encode()), seed]).standard_normal(out[name].shape)
        drawn = base * np.exp(spread * noise) if base else spread * noise
        out[name] = jnp.asarray(drawn.astype(out[name].dtype))
    for name, factor in factors.items():
        out[name] = (out[name] * factor).astype(out[name].dtype)
    return out
```

```python
import concourse.bass as bass
from concourse import mybir
from contextlib import ExitStack
from math import sqrt

f32 = mybir.dt.float32
f16 = mybir.dt.float16
i32 = mybir.dt.int32
u32 = mybir.dt.uint32
ALU = mybir.AluOpType
ACT = mybir.ActivationFunctionType
AX = mybir.AxisListType

P = 128
B, T, D = 8, 128, 512
S = 2048
H, HD = 16, 32
EC = D // P
GH = P // HD
G = H // GH
KB = S // 512
KC = S // P
UNITS = 8
WSCALE = 1024.0
EPS = 1e-5
QK = 3 * HD
QKM = QK + 1


def mm_terms(hi_l, lo_l, hi_r, lo_r):
    return ((hi_l, hi_r), (lo_l, hi_r), (hi_l, lo_r))


class Steps:

    def __init__(self, eng, sem, base=0):
        self.eng, self.sem, self.base, self.n = eng, sem, base, 0

    def did(self, instruction):
        instruction.then_inc(self.sem, 1)
        self.n += 1

    def wait(self):
        self.eng.wait_ge(self.sem, self.base + self.n)


def wait_each(eng, *waits):
    for _, value in waits:
        if not isinstance(value, int):
            eng.compute_val(value)
    for sem, value in waits:
        eng.wait_ge(sem, value)


def cross_attention(nc, x, ctxT, wqT, wkT, wvT, woT, x1, ident, ident16, ones, ones16):
    with ExitStack() as c:
        def sb(name, shape, dt):
            return c.enter_context(nc.sbuf_tensor(name, shape, dt))

        def sem(name):
            return c.enter_context(nc.semaphore(name))

        stage = sb("stage", [P, 2, 2, 512], f32)
        ctx_hi = sb("ctx_hi", [P, KB, EC, 512], f16)
        ctx_lo = sb("ctx_lo", [P, KB, EC, 512], f16)
        w_hi = sb("w_hi", [P, 3, EC, D], f16)
        w_lo = sb("w_lo", [P, 3, EC, D], f16)
        wo = sb("wo_sb", [P, EC, D], f32)
        v_sb = sb("v_sb", [P, 2, KC, 256], f32)
        k_hi = sb("k_hi", [P, S], f16)
        k_lo = sb("k_lo", [P, S], f16)
        ks = sb("ks", [P, 2, GH, S], f16)
        q_hi = sb("q_hi", [P, G, T], f16)
        q_lo = sb("q_lo", [P, G, T], f16)
        qs = sb("qs", [P, H, T], f16)
        xn = sb("xn", [P, D], f32)
        xt_hi = sb("xt_hi", [P, EC, T], f16)
        xt_lo = sb("xt_lo", [P, EC, T], f16)
        probs = sb("probs", [P, 4, 1024], f32)
        acc_v = sb("acc_v", [P, 1024], f32)
        acc_g = sb("acc_g", [P, 1024], f32)
        mx = sb("mx", [P, GH, 2], f32)
        nm = sb("nm", [P, GH], f32)
        diag = sb("diag", [P, GH, T], f16)
        rden = sb("rden", [P, T], f32)
        ot = sb("ot", [P, G, T], f32)
        st = sb("st", [P, B, 6], f32)
        mv = sb("mv", [P, B, 2], f32)
        var = sb("var", [P, B], f32)
        rs = sb("rs", [P, B], f32)
        tmp = sb("tmp", [P, B], f32)

        proj = [c.enter_context(nc.psum_tensor(f"proj{i}", [P, 512], f32)) for i in range(2)]
        sc = [c.enter_context(nc.psum_tensor(f"sc{i}", [P, 1024], f32)) for i in range(2)]
        po = c.enter_context(nc.psum_tensor("po", [P, 512], f32))
        misc = c.enter_context(nc.psum_tensor("misc", [P, 512], f32))

        x_in = sem("x_in")
        wo_in = sem("wo_in")
        stage_in = [sem(f"stage_in{i}") for i in range(2)]
        stage_hi = sem("stage_hi")
        stage_lo = sem("stage_lo")
        rows_set = sem("rows_set")
        var_ready = sem("var_ready")
        std_ready = sem("std_ready")
        xn_ready = sem("xn_ready")
        xt_ready = sem("xt_ready")
        xt_split_hi = sem("xt_split_hi")
        xt_split_lo = sem("xt_split_lo")
        q_ready = sem("q_ready")
        q_split_hi = sem("q_split_hi")
        q_split_lo = sem("q_split_lo")
        qs_in = sem("qs_in")
        proj_ready = sem("proj_ready")
        proj_act = sem("proj_act")
        k_low = sem("k_low")
        ks_in = [sem(f"ks_in{i}") for i in range(2)]
        m_ready = sem("m_ready")
        m_read = sem("m_read")
        diag_ready = sem("diag_ready")
        row_ready = sem("row_ready")
        row_set = sem("row_set")
        s_ready = sem("s_ready")
        e_ready = sem("e_ready")
        pv_done = sem("pv_done")
        sum_v = sem("sum_v")
        sum_g = sem("sum_g")
        group_done = sem("group_done")
        ot_ready = sem("ot_ready")
        o_ready = sem("o_ready")
        x1_ready = sem("x1_ready")
        v_step = sem("v_step")

        STAGE_W = 6
        W_ORDER = (2, 1, 0)
        ctx_v = ctxT.rearrange("b (c p) s -> b p c s", p=P)

        def use_k(b, g, kb):
            return 8 + 32 * b + 8 + 4 * g + kb

        def use_v(b, half, n):
            return 8 + 32 * b + n if half else 32 * b + n

        def stage_at(b, s):
            return STAGE_W + 8 * b + s

        def wait_k_stacked(eng, b, g):
            if isinstance(b, int) and b == 0 and g == 0:
                return
            n = 2 * b + (g - 1) // 2 + 1 if g else 2 * b
            eng.wait_ge(ks_in[(g - 1) % 2], 192 * n)

        with nc.Block() as block:

            @block.sync
            def _(sp):
                sp.dma_start(x1[:, :, :], x.rearrange("b p d -> p b d")).then_inc(x_in, 16)

                def load_ctx(b, s, first=False):
                    n = stage_at(b, s)
                    if not isinstance(b, int):
                        sp.compute_val(b * (D * S) * 4)
                    wait_each(sp, (stage_hi, n - 1), (stage_lo, n - 1))
                    src = ctx_v[bass.ds(b, 1), :, 2 * (s % 2):2 * (s % 2) + 2, 512 * (s // 2):512 * (s // 2) + 512]
                    sp.dma_start(stage[:, s % 2], src.rearrange("a p c s -> (a p) c s")).then_inc(stage_in[s % 2], 16)

                for n in range(STAGE_W):
                    w = (wqT, wkT, wvT)[W_ORDER[n // 2]].rearrange("(c p) d -> p c d", p=P)
                    if n >= 2:
                        sp.wait_ge(stage_hi, n - 1)
                        sp.wait_ge(stage_lo, n - 1)
                    sp.dma_start(stage[:, n % 2], w[:, 2 * (n % 2):2 * (n % 2) + 2, :]).then_inc(stage_in[n % 2], 16)
                for s in range(8):
                    load_ctx(0, s)
                sp.dma_start(wo[:, :, :], woT.rearrange("(c p) d -> p c d", p=P)).then_inc(wo_in, 16)

                def stack_q(b):
                    waits = [(q_split_hi, b + 1), (q_split_lo, b + 1)]
                    if not (isinstance(b, int) and b == 0):
                        waits.append((group_done, 4 * b))
                    wait_each(sp, *waits)
                    for row, part in ((0, q_hi), (HD, q_hi), (2 * HD, q_lo)):
                        for j in range(GH):
                            sp.dma_start(qs[row:row + HD, j:H:GH, :], part[HD * j:HD * j + HD, :, :]).then_inc(qs_in, 16)

                def stack_k(b, g):
                    waits = [(proj_act, use_k(b, g, KB - 1) + 1), (k_low, 16 * b + 4 * g + KB)]
                    if g >= 2 or not (isinstance(b, int) and b == 0):
                        waits.append((group_done, 4 * b + g - 1))
                    wait_each(sp, *waits)
                    for row, part in ((0, k_hi), (HD, k_lo), (2 * HD, k_hi)):
                        for j in range(GH):
                            sp.dma_start(ks[row:row + HD, g % 2, j, :], part[HD * j:HD * j + HD, :]).then_inc(ks_in[g % 2], 16)

                stack_q(0)

                def body(b, last):
                    for g in range(3):
                        stack_k(b, g)
                    if not last:
                        load_ctx(b + 1, 0)
                        load_ctx(b + 1, 1)
                    stack_k(b, 3)
                    if not last:
                        for s in range(2, 8):
                            load_ctx(b + 1, s)
                        stack_q(b + 1)

                body(0, False)
                with sp.Fori(1, B - 1) as b:
                    body(b, False)
                body(B - 1, True)

            @block.gpsimd
            def _(gp):
                gp.memset(ks[QK:P, :, :, :], 1.0).then_inc(rows_set, 1)

                def body(b):
                    for g in range(G):
                        e = 32 * b + UNITS * g
                        gp.wait_ge(e_ready, e + 4)
                        if not (isinstance(b, int) and b == 0 and g == 0):
                            gp.wait_ge(group_done, 4 * b + g)
                        gp.tensor_tensor(acc_g[:, :], probs[:, 2, :], probs[:, 3, :], ALU.add).then_inc(sum_g, 1)
                        gp.wait_ge(e_ready, e + 7)
                        gp.wait_ge(sum_g, 8 * b + 2 * g + 1)
                        gp.tensor_tensor(acc_g[:, :], acc_g[:, :], probs[:, 2, :], ALU.add).then_inc(sum_g, 1)

                body(0)
                with gp.Fori(1, B) as b:
                    body(b)

            @block.scalar
            def _(act):
                def split_hi(n, dst, scale):
                    act.activation(dst, stage[:, n % 2], ACT.Copy, scale=scale).then_inc(stage_hi, 1)

                act.wait_ge(var_ready, 1)
                act.activation(tmp[:, :], var[:, :], ACT.Sqrt).then_inc(std_ready, 1)
                for n in range(STAGE_W):
                    act.wait_ge(stage_in[n % 2], 16 * (n // 2 + 1))
                    split_hi(n, w_hi[:, W_ORDER[n // 2], 2 * (n % 2):2 * (n % 2) + 2, :], WSCALE)

                def split_ctx(b, s, first=False):
                    n = stage_at(b, s)
                    act.wait_ge(stage_in[s % 2], 16 * (3 + 4 * b + s // 2 + 1))
                    if not first:
                        act.wait_ge(proj_ready, use_k(b - 1, 3, s // 2) + 1)
                    split_hi(s, ctx_hi[:, s // 2, 2 * (s % 2):2 * (s % 2) + 2, :], 1.0)

                def copy_v(b, half, n):
                    u = use_v(b, half, n)
                    act.wait_ge(proj_ready, u + 1)
                    if half:
                        if not (isinstance(b, int) and b == 0):
                            act.wait_ge(pv_done, 32 * b)
                    elif not (isinstance(b, int) and b == 0):
                        act.wait_ge(pv_done, 32 * b - 16)
                    act.activation(v_sb[:, half, 2 * n:2 * n + 2, :],
                                   proj[n % 2][:, :].rearrange("p (c d) -> p c d", c=2),
                                   ACT.Copy, scale=1.0 / WSCALE).then_inc(proj_act, 1)

                def split_k(b, g, kb):
                    act.wait_ge(proj_ready, use_k(b, g, kb) + 1)
                    if kb == 0:
                        wait_k_stacked(act, b, g)
                    act.activation(k_hi[:, 512 * kb:512 * kb + 512], proj[kb % 2][:, :], ACT.Copy,
                                   scale=1.0 / WSCALE).then_inc(proj_act, 1)

                def set_row(b, g):
                    act.wait_ge(row_ready, 4 * b + g + 1)
                    act.activation(qs[QK:QKM, 4 * g:4 * g + 4, :],
                                   misc[QK:QKM, :].rearrange("p (j t) -> p j t", j=GH), ACT.Copy).then_inc(row_set, 1)

                def exp(b, g, u):
                    e = 32 * b + UNITS * g + u
                    act.wait_ge(s_ready, e + 1)
                    if not (isinstance(b, int) and b == 0 and g == 0 and u < 4):
                        act.wait_ge(pv_done, e - 3)
                        k = 4 * g + 16 * b
                        m = 2 * g + 8 * b
                        who, val = {0: (sum_v, k - 2), 1: (sum_v, k - 1), 2: (sum_g, m), 3: (sum_v, k),
                                    4: (sum_v, k + 1), 5: (sum_v, k + 1), 6: (sum_g, m + 1), 7: (sum_g, m + 1)}[u]
                        act.wait_ge(who, val)
                    act.activation(probs[:, u % 4, :], sc[u % 2][:, :], ACT.Exp, scale=1.0 / sqrt(HD)).then_inc(e_ready, 1)

                def split_xt(b):
                    act.wait_ge(xt_ready, b + 1)
                    act.activation(xt_hi[:, :, :], misc[:, :].rearrange("p (c t) -> p c t", c=EC), ACT.Copy).then_inc(xt_split_hi, 1)

                def split_q(b):
                    act.wait_ge(q_ready, b + 1)
                    if not (isinstance(b, int) and b == 0):
                        act.wait_ge(qs_in, 192 * b)
                    act.activation(q_hi[:, :, :], misc[:, :].rearrange("p (g t) -> p g t", g=G), ACT.Copy,
                                   scale=1.0 / WSCALE).then_inc(q_split_hi, 1)

                for s in range(8):
                    split_ctx(0, s, first=True)
                split_xt(0)
                split_q(0)
                for n in range(8):
                    copy_v(0, 0, n)

                def body(b, last):
                    for n in range(8):
                        copy_v(b, 1, n)
                    for kb in range(KB):
                        split_k(b, 0, kb)
                    for g in range(G):
                        if g < 3:
                            for kb in range(KB):
                                split_k(b, g + 1, kb)
                        elif not last:
                            split_xt(b + 1)
                            split_ctx(b + 1, 4)
                            copy_v(b + 1, 0, 0)
                            split_ctx(b + 1, 5)
                            copy_v(b + 1, 0, 1)
                            split_ctx(b + 1, 6)
                            split_q(b + 1)
                            split_ctx(b + 1, 7)
                            for n in range(2, 8):
                                copy_v(b + 1, 0, n)
                        set_row(b, g)
                        for u in range(UNITS):
                            exp(b, g, u)
                            if g == 2 and u % 2 == 1 and not last:
                                split_ctx(b + 1, u // 2)

                body(0, False)
                with act.Fori(1, B - 1) as b:
                    body(b, False)
                body(B - 1, True)

            @block.vector
            def _(dve):
                steps = Steps(dve, v_step)
                dve.wait_ge(x_in, 16)
                for b in range(B):
                    steps.did(dve.bn_stats(st[:, b, :], x1[:, b, :]))
                steps.wait()
                for b in range(B):
                    steps.did(dve.bn_aggr(mv[:, b, :], st[:, b, :]))
                steps.wait()
                dve.tensor_scalar(var[:, :], mv[:, :, 1], EPS, None, ALU.add).then_inc(var_ready, 1)
                dve.wait_ge(std_ready, 1)
                rsqrt_from_std(dve, steps, rs, tmp, var)
                LN_STEPS = steps.n

                def split_lo(n, hi, lo, scale):
                    dve.scalar_tensor_tensor(lo, stage[:, n % 2], scale, hi, ALU.mult, ALU.subtract).then_inc(stage_lo, 1)

                for n in range(STAGE_W):
                    dve.wait_ge(stage_hi, n + 1)
                    at = (slice(None), W_ORDER[n // 2], slice(2 * (n % 2), 2 * (n % 2) + 2))
                    split_lo(n, w_hi[at], w_lo[at], WSCALE)

                def split_ctx(b, s):
                    dve.wait_ge(stage_hi, stage_at(b, s) + 1)
                    at = (slice(None), s // 2, slice(2 * (s % 2), 2 * (s % 2) + 2))
                    split_lo(s, ctx_hi[at], ctx_lo[at], 1.0)

                def split_k(b, g, kb):
                    dve.wait_ge(proj_act, use_k(b, g, kb) + 1)
                    dve.scalar_tensor_tensor(k_lo[:, 512 * kb:512 * kb + 512], proj[kb % 2][:, :], 1.0 / WSCALE,
                                             k_hi[:, 512 * kb:512 * kb + 512], ALU.mult, ALU.subtract).then_inc(k_low, 1)

                def normalise(b):
                    if not (isinstance(b, int) and b == 0):
                        dve.wait_ge(xt_ready, b)
                    dve.tensor_scalar(xn[:, :], x1[:, bass.ds(b, 1), :].rearrange("p a d -> p (a d)"),
                                      mv[:, bass.ds(b, 1), 0], rs[:, bass.ds(b, 1)],
                                      ALU.subtract, ALU.mult).then_inc(xn_ready, 1)

                def split_xt(b):
                    dve.wait_ge(xt_split_hi, b + 1)
                    dve.tensor_tensor(xt_lo[:, :, :], misc[:, :].rearrange("p (c t) -> p c t", c=EC), xt_hi[:, :, :],
                                      ALU.subtract).then_inc(xt_split_lo, 1)

                def split_q(b):
                    dve.wait_ge(q_split_hi, b + 1)
                    dve.scalar_tensor_tensor(q_lo[:, :, :], misc[:, :].rearrange("p (g t) -> p g t", g=G), 1.0 / WSCALE,
                                             q_hi[:, :, :], ALU.mult, ALU.subtract).then_inc(q_split_lo, 1)

                def maximum(b, g, u):
                    dve.wait_ge(m_ready, 32 * b + UNITS * g + u + 1)
                    dve.reduce_max(mx[:, u // 2, u % 2:u % 2 + 1], sc[u % 2][:, :], AX.X).then_inc(m_read, 1)

                def maxima_to_diag(b, g, steps):
                    dve.wait_ge(m_read, 32 * b + UNITS * g + UNITS)
                    steps.did(dve.tensor_reduce(nm[:, :], mx[:, :, :], AX.X, ALU.max, negate=True))
                    steps.wait()
                    if not (isinstance(b, int) and b == 0 and g == 0):
                        dve.wait_ge(row_ready, 4 * b + g)
                    dve.tensor_tensor(diag[:, :, :], nm[:, :].unsqueeze(2).to_broadcast([P, GH, T]),
                                      ident16[:, :].unsqueeze(1).to_broadcast([P, GH, T]),
                                      ALU.mult).then_inc(diag_ready, 1)

                def add_probs(b, g, part):
                    e = 32 * b + UNITS * g
                    dve.wait_ge(e_ready, e + (2, 5, 6, 8)[part])
                    if part == 0:
                        if not (isinstance(b, int) and b == 0 and g == 0):
                            dve.wait_ge(group_done, 4 * b + g)
                        dve.tensor_tensor(acc_v[:, :], probs[:, 0, :], probs[:, 1, :], ALU.add).then_inc(sum_v, 1)
                    else:
                        dve.wait_ge(sum_v, 16 * b + 4 * g + part)
                        dve.tensor_tensor(acc_v[:, :], acc_v[:, :], probs[:, (0, 0, 1, 3)[part], :],
                                          ALU.add).then_inc(sum_v, 1)

                def finish_group(b, g, steps):
                    dve.wait_ge(group_done, 4 * b + g + 1)
                    steps.did(dve.reciprocal(rden[:, :], po[:, T:2 * T]))
                    steps.wait()
                    if g == 0 and not (isinstance(b, int) and b == 0):
                        dve.wait_ge(o_ready, b)
                    dve.tensor_tensor(ot[:, g, :], po[:, 0:T], rden[:, :], ALU.mult).then_inc(ot_ready, 1)

                normalise(0)
                for s in range(8):
                    split_ctx(0, s)
                split_xt(0)
                split_q(0)
                PER = 2 * G

                def body(b, last):
                    steps = Steps(dve, v_step, LN_STEPS + PER * b)
                    for kb in range(KB):
                        split_k(b, 0, kb)
                    if not last:
                        normalise(b + 1)
                    for g in range(G):
                        if g == 3 and not last:
                            split_xt(b + 1)
                        for u in range(UNITS):
                            maximum(b, g, u)
                            if g < 3 and u in (2, 5):
                                split_k(b, g + 1, u // 3)
                            if g == 3 and not last and u in (0, 1, 2, 4):
                                split_ctx(b + 1, {0: 4, 1: 5, 2: 6, 4: 7}[u])
                            if g == 3 and not last and u == 3:
                                split_q(b + 1)
                        maxima_to_diag(b, g, steps)
                        if g < 3:
                            split_k(b, g + 1, 2)
                            split_k(b, g + 1, 3)
                        for part in range(4):
                            add_probs(b, g, part)
                            if g == 2 and not last:
                                split_ctx(b + 1, part)
                        finish_group(b, g, steps)
                    dve.wait_ge(o_ready, b + 1)
                    x_b = x1[:, bass.ds(b, 1), :].rearrange("p a d -> p (a d)")
                    dve.tensor_tensor(x_b, misc[:, :], x_b, ALU.add).then_inc(x1_ready, 1)
                    assert steps.n == PER

                body(0, False)
                with dve.Fori(1, B - 1) as b:
                    body(b, False)
                body(B - 1, True)

            @block.tensor
            def _(pe):
                pe.wait_ge(rows_set, 1)

                def project_v(b, half, piece):
                    n, c = piece // 2, piece % 2
                    u = use_v(b, half, n)
                    out = proj[n % 2][:, 256 * c:256 * c + 256]
                    if c == 0:
                        if half or not (isinstance(b, int) and b == 0 and n < 2):
                            pe.wait_ge(proj_act, u - 1)
                        if not half and n < 2 and not (isinstance(b, int) and b == 0):
                            pe.wait_ge(k_low, 16 * b - 1 + n)
                        if not half and n % 2 == 0:
                            pe.wait_ge(stage_hi, stage_at(b, n + 2))
                            pe.wait_ge(stage_lo, stage_at(b, n + 2))
                    kb, at = piece // 4, P * (piece % 4)
                    wv = slice(256 * half, 256 * half + 256)
                    n_mm = 0
                    for x_part, w_part in mm_terms(ctx_hi, ctx_lo, w_hi, w_lo):
                        for e in range(EC):
                            last = pe.matmul(out, x_part[:, kb, e, at:at + P], w_part[:, 2, e, wv],
                                             start=n_mm == 0, stop=n_mm == 3 * EC - 1)
                            n_mm += 1
                    if c == 1:
                        last.then_inc(proj_ready, 1)

                def project_k(b, g, piece):
                    kb, term = piece // 3, piece % 3
                    u = use_k(b, g, kb)
                    if term == 0:
                        pe.wait_ge(proj_act, u - 1)
                        if g or kb >= 2:
                            pe.wait_ge(k_low, 16 * b + 4 * g + kb - 1)
                    w_part, x_part = mm_terms(w_hi, w_lo, ctx_hi, ctx_lo)[term]
                    for e in range(EC):
                        last = pe.matmul(proj[kb % 2][:, :], w_part[:, 1, e, P * g:P * g + P], x_part[:, kb, e, :],
                                         start=term == 0 and e == 0, stop=term == 2 and e == EC - 1)
                    if term == 2:
                        last.then_inc(proj_ready, 1)

                def scores_for_max(b, g, u):
                    w = 32 * b + UNITS * g + u
                    if u == 0:
                        pe.wait_ge(ks_in[g % 2], 192 * (2 * b + g // 2 + 1))
                    if g == 0 and u == 0:
                        pe.wait_ge(qs_in, 192 * (b + 1))
                    if u >= 2:
                        pe.wait_ge(m_read, w - 1)
                    elif not (isinstance(b, int) and b == 0 and g == 0):
                        pe.wait_ge(e_ready, w - 1)
                    j = u // 2
                    for i in range(2):
                        at = 1024 * (u % 2) + 512 * i
                        last = pe.matmul(sc[u % 2][:, 512 * i:512 * i + 512], qs[0:QK, 4 * g + j, :],
                                         ks[0:QK, g % 2, j, at:at + 512], start=True, stop=True)
                    last.then_inc(m_ready, 1)

                def maxima_to_row(b, g):
                    pe.wait_ge(diag_ready, 4 * b + g + 1)
                    if g == 3 and not (isinstance(b, int) and b == B - 1):
                        pe.wait_ge(q_split_lo, b + 2)
                    elif g:
                        pe.wait_ge(row_set, 4 * b + g)
                    elif not (isinstance(b, int) and b == 0):
                        pe.wait_ge(x1_ready, b)
                    pe.matmul(misc[QK:QKM, :], ones16[:, 0:1], diag[:, :, :].rearrange("p j t -> p (j t)"),
                              start=True, stop=True, tile_position=(0, QK)).then_inc(row_ready, 1)

                def scores_transposed(b, g, u):
                    w = 32 * b + UNITS * g + u
                    if u == 0:
                        pe.wait_ge(row_set, 4 * b + g + 1)
                    if u >= 2:
                        pe.wait_ge(e_ready, w - 1)
                    else:
                        pe.wait_ge(m_read, 32 * b + UNITS * g + UNITS - 1 + u)
                    for i in range(2):
                        ck = 2 * u + i
                        for j in range(GH):
                            last = pe.matmul(sc[u % 2][:, 512 * i + P * j:512 * i + P * j + P],
                                             ks[0:QKM, g % 2, j, P * ck:P * ck + P], qs[0:QKM, 4 * g + j, :],
                                             start=True, stop=True)
                    last.then_inc(s_ready, 1)

                def times_v(b, g, u):
                    w = 32 * b + UNITS * g + u
                    pe.wait_ge(e_ready, w + 1)
                    if u == 0:
                        if not (isinstance(b, int) and b == 0 and g == 0):
                            pe.wait_ge(ot_ready, 4 * b + g)
                    if u == 0 and g % 2 == 0:
                        pe.wait_ge(proj_act, use_v(b, g // 2, 7) + 1)
                    for i in range(2):
                        ck = 2 * u + i
                        for j in range(GH):
                            at = (4 * g + j) % 8 * HD
                            last = pe.matmul(po[HD * j:HD * j + HD, 0:T], v_sb[:, g // 2, ck, at:at + HD],
                                             probs[:, u % 4, 512 * i + P * j:512 * i + P * j + P],
                                             start=ck == 0, stop=ck == KC - 1, tile_position=(0, HD * j))
                    last.then_inc(pv_done, 1)

                def denominators(b, g):
                    pe.wait_ge(sum_v, 16 * b + 4 * g + 4)
                    pe.wait_ge(sum_g, 8 * b + 2 * g + 2)
                    parts = [(acc, 512 * i) for acc in (acc_v, acc_g) for i in range(2)]
                    for n, (acc, at) in enumerate(parts):
                        for j in range(GH):
                            last = pe.matmul(po[HD * j:HD * j + HD, T:2 * T], ones[:, 0:HD],
                                             acc[:, at + P * j:at + P * j + P], start=n == 0,
                                             stop=n == len(parts) - 1, tile_position=(0, HD * j))
                    last.then_inc(group_done, 1)

                def transpose_xn(b):
                    pe.wait_ge(xn_ready, b + 1)
                    if not (isinstance(b, int) and b == 0):
                        pe.wait_ge(row_set, 4 * b - 1)
                    for e in range(EC):
                        last = pe.transpose(misc[:, P * e:P * e + P], xn[:, P * e:P * e + P], ident[:, :])
                    last.then_inc(xt_ready, 1)

                def project_q(b):
                    pe.wait_ge(xt_split_lo, b + 1)
                    for g in range(G):
                        n_mm = 0
                        for w_part, x_part in mm_terms(w_hi, w_lo, xt_hi, xt_lo):
                            for e in range(EC):
                                last = pe.matmul(misc[:, P * g:P * g + P], w_part[:, 0, e, P * g:P * g + P],
                                                 x_part[:, e, :], start=n_mm == 0, stop=n_mm == 3 * EC - 1)
                                n_mm += 1
                    last.then_inc(q_ready, 1)

                def project_out(b):
                    pe.wait_ge(ot_ready, 4 * b + 4)
                    pe.wait_ge(row_set, 4 * b + 4)
                    for g in range(G):
                        last = pe.matmul(misc[:, :], ot[:, g, :], wo[:, g, :], start=g == 0, stop=g == G - 1)
                    last.then_inc(o_ready, 1)

                pe.wait_ge(stage_hi, STAGE_W)
                pe.wait_ge(stage_lo, STAGE_W)
                transpose_xn(0)
                project_q(0)
                for piece in range(16):
                    project_v(0, 0, piece)
                pe.wait_ge(wo_in, 16)

                def body(b, last):
                    for piece in range(16):
                        project_v(b, 1, piece)
                    for piece in range(12):
                        project_k(b, 0, piece)
                    for g in range(G):
                        if g == 3 and not last:
                            transpose_xn(b + 1)
                        for u in range(UNITS):
                            scores_for_max(b, g, u)
                            if g < 3:
                                project_k(b, g + 1, u)
                            elif not last:
                                project_v(b + 1, 0, u)
                            if g == 3 and u == 3 and not last:
                                project_q(b + 1)
                        for piece in range(UNITS, 12 if g < 3 else 16):
                            if g < 3:
                                project_k(b, g + 1, piece)
                            elif not last:
                                project_v(b + 1, 0, piece)
                        maxima_to_row(b, g)
                        for u in range(UNITS + 1):
                            if u < UNITS:
                                scores_transposed(b, g, u)
                            if u:
                                times_v(b, g, u - 1)
                        denominators(b, g)
                    project_out(b)

                body(0, False)
                with pe.Fori(1, B - 1) as b:
                    body(b, False)
                body(B - 1, True)


def rsqrt_from_std(dve, steps, rs, std, var):
    steps.did(dve.reciprocal(rs[:, :], std[:, :]))
    steps.wait()
    steps.did(dve.tensor_tensor(std[:, :], rs[:, :], rs[:, :], ALU.mult))
    steps.wait()
    steps.did(dve.tensor_tensor(std[:, :], std[:, :], var[:, :], ALU.mult))
    steps.wait()
    steps.did(dve.tensor_scalar(std[:, :], std[:, :], -0.5, 1.5, ALU.mult, ALU.add))
    steps.wait()
    steps.did(dve.tensor_tensor(rs[:, :], rs[:, :], std[:, :], ALU.mult))
    steps.wait()


def constants(nc, ident, ident16, ones, ones16):
    with ExitStack() as c:
        zeroed = c.enter_context(nc.semaphore("zeroed"))
        made = c.enter_context(nc.semaphore("made"))
        with nc.Block() as block:

            @block.gpsimd
            def _(gp):
                gp.memset(ones[:, :], 1.0).then_inc(made, 1)
                gp.memset(ones16[:, :], 1.0).then_inc(made, 1)
                gp.memset(ident[:, :], 0.0).then_inc(zeroed, 1)
                gp.wait_ge(zeroed, 1)
                gp.affine_select(out=ident[:, :], in_=ident[:, :], compare_op=ALU.not_equal, fill=1.0, base=0,
                                 pattern=[[-1, P]], channel_multiplier=1).then_inc(zeroed, 1)
                gp.wait_ge(zeroed, 2)
                gp.tensor_copy(ident16[:, :], ident[:, :]).then_inc(made, 1)
                gp.wait_ge(made, 3)


QMAX, QMIN, QFLOOR = 127.0, -128.0, 1e-8
ROUND = 1.5 * 2.0 ** 23


def quantised_self_attention(nc, wiT, in_b, qoT, out_b, x1, ident, ident16):
    E3 = 3 * D
    with ExitStack() as c:
        def sb(name, shape, dt):
            return c.enter_context(nc.sbuf_tensor(name, shape, dt))

        def sem(name):
            return c.enter_context(nc.semaphore(name))

        wi = sb("wi_f", [P, EC, E3], f32)
        wi_q = sb("wi_q", [P, EC, E3], f16)
        qo = sb("qo", [P, EC, D], f32)
        qo_q = sb("qo_q", [P, EC, D], f16)
        bi = sb("bi_sb", [P, E3], f32)
        bo = sb("bo_sb", [P, D], f32)
        xn = sb("xn2", [P, 2, D], f32)
        xt_hi = sb("xt2_hi", [P, 2, EC, T], f16)
        xt_lo = sb("xt2_lo", [P, 2, EC, T], f16)
        big = sb("big", [P, B, E3], f32)
        xq = sb("xq", [P, B, E3], f16)
        prod = sb("prod", [P, B, D], f32)
        scores = sb("scores2", [P, B, H, B], f32)
        row = sb("row", [P, B, H], f32)
        heads = big[:, :, 0:D]
        hq = xq[:, :, 0:D]
        y = big[:, :, D:2 * D]
        ht = sb("ht", [P, 2, EC, T], f16)
        st = sb("st2", [P, B, 6], f32)
        mv = sb("mv2", [P, B, 2], f32)
        var = sb("var2", [P, B], f32)
        std = sb("std2", [P, B], f32)
        rs = sb("rs2", [P, B], f32)
        part = sb("part", [P, 1], f32)
        wide = sb("wide", [P, P], f32)
        scale = {n: sb(f"scale_{n}", [P, 1], f32) for n in ("wi", "wo", "x", "q", "qx", "h", "how", "y", "tmp")}
        inv = {n: sb(f"inv_{n}", [P, 1], f32) for n in ("wi", "wo", "x", "q", "h", "y")}

        px = [c.enter_context(nc.psum_tensor(f"px{i}", [P, E3], f32)) for i in range(2)]
        pt = [c.enter_context(nc.psum_tensor(f"pt{i}", [P, 512], f32)) for i in range(2)]

        wi_in, wo_in, bias_in = sem("wi_in2"), sem("wo_in2"), sem("bias_in2")
        v_step = sem("v_step2")
        wide_ready = sem("wide_ready")
        wide_t = sem("wide_t")
        var_ready, std_ready = sem("var_ready2"), sem("std_ready2")
        xn_ready = sem("xn_ready2")
        xt_ready, xt_hi_ready, xt_lo_ready = sem("xt_ready2"), sem("xt_hi_ready2"), sem("xt_lo_ready2")
        x_ready, x_read = sem("x_ready2"), sem("x_read2")
        diff_ready, exp_ready = sem("diff_ready2"), sem("exp_ready2")
        hq_ready, ht_ready, ht_read, y_ready, y_read = (sem(n) for n in ("hq_ready", "ht_ready", "ht_read", "y_ready", "y_read"))

        with nc.Block() as block:

            @block.sync
            def _(sp):
                sp.dma_start(wi[:, :, :], wiT.rearrange("(c p) d -> p c d", p=P)).then_inc(wi_in, 16)
                sp.dma_start(qo[:, :, :], qoT.rearrange("(c p) d -> p c d", p=P)).then_inc(wo_in, 16)
                sp.dma_start(bi[:, :], in_b.rearrange("(a d) -> a d", a=1).to_broadcast([P, E3])).then_inc(bias_in, 16)
                sp.dma_start(bo[:, :], out_b.rearrange("(a d) -> a d", a=1).to_broadcast([P, D])).then_inc(bias_in, 16)

            @block.scalar
            def _(act):
                act.wait_ge(var_ready, 1)
                act.activation(std[:, :], var[:, :], ACT.Sqrt).then_inc(std_ready, 1)
                for t in range(B):
                    act.wait_ge(xt_ready, t + 1)
                    if t >= 2:
                        act.wait_ge(x_ready, t - 1)
                    act.activation(xt_hi[:, t % 2], pt[t % 2][:, :].rearrange("p (c t) -> p c t", c=EC),
                                   ACT.Copy).then_inc(xt_hi_ready, 1)
                act.wait_ge(diff_ready, 1)
                act.activation(scores[:, :, :, :], scores[:, :, :, :], ACT.Exp, scale=scale["qx"][:, :]).then_inc(exp_ready, 1)
                for t in range(B):
                    act.wait_ge(ht_ready, t + 1)
                    if t >= 2:
                        act.wait_ge(y_ready, t - 1)
                    act.activation(ht[:, t % 2], pt[t % 2][:, :].bitcast(f16)[:, 0:EC * T].rearrange("p (c t) -> p c t", c=EC),
                                   ACT.Copy).then_inc(ht_read, 1)

            @block.vector
            def _(dve):
                steps = Steps(dve, v_step)
                rounds = [0]

                def do(instruction):
                    steps.did(instruction)
                    steps.wait()

                def across_partitions():
                    steps.wait()
                    dve.tensor_copy(wide[:, :], part[:, :].to_broadcast([P, P])).then_inc(wide_ready, 1)
                    rounds[0] += 1
                    dve.wait_ge(wide_t, rounds[0])
                    do(dve.reduce_max(part[:, :], pt[0][:, 0:P], AX.X))

                def scale_from_max(name):
                    do(dve.tensor_scalar(scale[name][:, :], part[:, :], 1.0 / QMAX, QFLOOR, ALU.mult, ALU.max))
                    do(dve.reciprocal(inv[name][:, :], scale[name][:, :]))

                def quantise(ints, values, name):
                    do(dve.tensor_scalar(values, values, inv[name][:, :], ROUND, ALU.mult, ALU.add))
                    do(dve.tensor_scalar(ints, values, -ROUND, QMAX, ALU.add, ALU.min))
                    do(dve.tensor_scalar(ints, ints, QMIN, None, ALU.max))

                def absmax(out, in_, axis):
                    do(dve.tensor_reduce(out, in_, axis, ALU.max, apply_absolute_value=True))

                for t in range(B):
                    steps.did(dve.bn_stats(st[:, t, :], x1[:, t, :]))
                steps.wait()
                for t in range(B):
                    steps.did(dve.bn_aggr(mv[:, t, :], st[:, t, :]))
                steps.wait()
                dve.tensor_scalar(var[:, :], mv[:, :, 1], EPS, None, ALU.add).then_inc(var_ready, 1)
                dve.wait_ge(std_ready, 1)
                rsqrt_from_std(dve, steps, rs, std, var)

                def normalise(t):
                    dve.tensor_scalar(xn[:, t % 2, :], x1[:, t, :], mv[:, t, 0:1], rs[:, t:t + 1],
                                      ALU.subtract, ALU.mult).then_inc(xn_ready, 1)

                dve.wait_ge(wi_in, 16)
                absmax(part[:, :], wi[:, :, :], AX.XY)
                across_partitions()
                scale_from_max("wi")
                quantise(wi_q[:, :, :], wi[:, :, :], "wi")
                dve.wait_ge(wo_in, 16)
                absmax(part[:, :], qo[:, :, :], AX.XY)
                across_partitions()
                scale_from_max("wo")
                quantise(qo_q[:, :, :], qo[:, :, :], "wo")

                normalise(0)
                normalise(1)
                dve.wait_ge(bias_in, 32)
                for t in range(B):
                    dve.wait_ge(xt_hi_ready, t + 1)
                    dve.tensor_tensor(xt_lo[:, t % 2], pt[t % 2][:, :].rearrange("p (c t) -> p c t", c=EC),
                                      xt_hi[:, t % 2], ALU.subtract).then_inc(xt_lo_ready, 1)
                    if t + 2 < B:
                        dve.wait_ge(xt_ready, t + 1)
                        normalise(t + 2)
                    dve.wait_ge(x_ready, t + 1)
                    dve.scalar_tensor_tensor(big[:, t, :], px[t % 2][:, :], scale["wi"][:, :], bi[:, :],
                                             ALU.mult, ALU.add).then_inc(x_read, 1)
                dve.wait_ge(x_read, B)
                absmax(part[:, :], big[:, :, :], AX.XY)
                across_partitions()
                scale_from_max("x")
                quantise(xq[:, :, :], big[:, :, :], "x")

                q_int = xq[:, :, 0:D]
                q_val = big[:, :, 0:D]
                do(dve.tensor_scalar(q_val, q_int, scale["x"][:, :], 1.0 / sqrt(HD), ALU.mult, ALU.mult))
                absmax(part[:, :], q_val, AX.XY)
                across_partitions()
                scale_from_max("q")
                quantise(q_int, q_val, "q")
                do(dve.tensor_tensor(scale["qx"][:, :], scale["q"][:, :], scale["x"][:, :], ALU.mult))

                k_int, v_int = xq[:, :, D:2 * D], xq[:, :, 2 * D:3 * D]
                prod_khd = prod[:, :, :].rearrange("p k (h d) -> p k h d", h=H)
                base = steps.base + steps.n
                with dve.Fori(0, B) as q:
                    loop = Steps(dve, v_step, base + 2 * q)
                    loop.did(dve.tensor_tensor(prod[:, :, :], k_int, xq[:, bass.ds(q, 1), 0:D].to_broadcast([P, B, D]), ALU.mult))
                    loop.wait()
                    out = scores[:, bass.ds(q, 1), :, :].rearrange("p a h k -> p (a k) h")
                    loop.did(dve.tensor_reduce(out, prod_khd, AX.X, ALU.add))
                    loop.wait()
                steps.n += 2 * B
                s3 = scores[:, :, :, :].rearrange("p q h k -> p (q h) k")
                r2 = row[:, :, :].rearrange("p q h -> p (q h)")
                r3 = r2.unsqueeze(2).to_broadcast([P, B * H, B])
                do(dve.tensor_reduce(r2, s3, AX.X, ALU.max))
                dve.tensor_tensor(s3, s3, r3, ALU.subtract).then_inc(diff_ready, 1)
                dve.wait_ge(exp_ready, 1)
                do(dve.tensor_reduce(r2, s3, AX.X, ALU.add))
                do(dve.reciprocal(r2, r2))
                do(dve.tensor_tensor(s3, s3, r3, ALU.mult))
                v_khd = v_int.rearrange("p k (h d) -> p k h d", h=H)
                base = steps.base + steps.n
                with dve.Fori(0, B) as q:
                    loop = Steps(dve, v_step, base + 2 * q)
                    p_q = scores[:, bass.ds(q, 1), :, :].rearrange("p a h k -> p (a k) h").unsqueeze(3)
                    loop.did(dve.tensor_tensor(prod_khd, v_khd, p_q.to_broadcast([P, B, H, HD]), ALU.mult))
                    loop.wait()
                    out = heads[:, bass.ds(q, 1), :].rearrange("p a d -> p (a d)")
                    loop.did(dve.tensor_reduce(out, prod[:, :, :].rearrange("p k d -> p d k"), AX.X, ALU.add))
                    loop.wait()
                steps.n += 2 * B

                do(dve.tensor_scalar(heads, heads, scale["x"][:, :], None, ALU.mult))
                absmax(part[:, :], heads, AX.XY)
                across_partitions()
                scale_from_max("h")
                quantise(hq, heads, "h")
                dve.tensor_tensor(scale["how"][:, :], scale["h"][:, :], scale["wo"][:, :], ALU.mult).then_inc(hq_ready, 1)
                dve.wait_ge(hq_ready, 1)
                for t in range(B):
                    dve.wait_ge(y_ready, t + 1)
                    dve.scalar_tensor_tensor(y[:, t, :], px[t % 2][:, 0:D], scale["how"][:, :], bo[:, :],
                                             ALU.mult, ALU.add).then_inc(y_read, 1)
                dve.wait_ge(y_read, B)
                absmax(part[:, :], y, AX.XY)
                across_partitions()
                scale_from_max("y")
                quantise(hq, y, "y")
                do(dve.scalar_tensor_tensor(x1[:, :, :], hq, scale["y"][:, :], x1[:, :, :], ALU.mult, ALU.add))

            @block.tensor
            def _(pe):
                rounds = [0]

                def transpose_wide():
                    rounds[0] += 1
                    pe.wait_ge(wide_ready, rounds[0])
                    pe.transpose(pt[0][:, 0:P], wide[:, :], ident[:, :]).then_inc(wide_t, 1)

                transpose_wide()
                transpose_wide()

                def transpose_xn(t):
                    pe.wait_ge(xn_ready, t + 1)
                    if t >= 2:
                        pe.wait_ge(xt_lo_ready, t - 1)
                    for e in range(EC):
                        last = pe.transpose(pt[t % 2][:, P * e:P * e + P], xn[:, t % 2, P * e:P * e + P], ident[:, :])
                    last.then_inc(xt_ready, 1)

                transpose_xn(0)
                for t in range(B):
                    if t + 1 < B:
                        transpose_xn(t + 1)
                    pe.wait_ge(xt_lo_ready, t + 1)
                    if t >= 2:
                        pe.wait_ge(x_read, t - 1)
                    for n in range(3):
                        n_mm = 0
                        for x_part in (xt_hi, xt_lo):
                            for e in range(EC):
                                last = pe.matmul(px[t % 2][:, D * n:D * n + D], x_part[:, t % 2, e, :],
                                                 wi_q[:, e, D * n:D * n + D], start=n_mm == 0, stop=n_mm == 2 * EC - 1)
                                n_mm += 1
                    last.then_inc(x_ready, 1)
                transpose_wide()
                transpose_wide()
                transpose_wide()
                pe.wait_ge(hq_ready, 1)

                def transpose_heads(t):
                    if t >= 2:
                        pe.wait_ge(ht_read, t - 1)
                    for e in range(EC):
                        last = pe.transpose(pt[t % 2][:, :].bitcast(f16)[:, P * e:P * e + P], hq[:, t, P * e:P * e + P], ident16[:, :])
                    last.then_inc(ht_ready, 1)

                transpose_heads(0)
                for t in range(B):
                    if t + 1 < B:
                        transpose_heads(t + 1)
                    pe.wait_ge(ht_read, t + 1)
                    if t >= 2:
                        pe.wait_ge(y_read, t - 1)
                    for e in range(EC):
                        last = pe.matmul(px[t % 2][:, 0:D], ht[:, t % 2, e, :], qo_q[:, e, :], start=e == 0, stop=e == EC - 1)
                    last.then_inc(y_ready, 1)
                transpose_wide()


E_, F = 8, 2048
TOPK = 2
CAP = int(1.25 * B * T * TOPK / E_) + 1
FQ = F // 512
CT = -(-CAP // P)
ROWS = [min(P, CAP - P * i) for i in range(CT)]
DROPPED = 4096.0


def route(nc, rwT, x1, xn3, slot_i, gates, xbuf, ident, ident16):
    with ExitStack() as c:
        def sb(name, shape, dt):
            return c.enter_context(nc.sbuf_tensor(name, shape, dt))

        def sem(name):
            return c.enter_context(nc.semaphore(name))

        rw = sb("rw", [P, EC, E_], f32)
        zeros = sb("zeros", [P, D], f32)
        xt = sb("xt3", [P, 2, EC, T], f32)
        st = sb("st3", [P, B, 6], f32)
        mv = sb("mv3", [P, B, 2], f32)
        var = sb("var3", [P, B], f32)
        std = sb("std3", [P, B], f32)
        rs = sb("rs3", [P, B], f32)
        upper = sb("upper", [P, P], f16)
        ones_sq = sb("ones_sq", [P, P], f16)
        expert_i = sb("expert_i", [P, E_], i32)
        expert_f = sb("expert_f", [P, E_], f32)
        logits = sb("logits", [P, B, E_], f32)
        top = sb("top", [P, B, 8], f32)
        top_i = sb("top_i", [P, B, 8], u32)
        chosen = sb("chosen", [P, TOPK, B], f32)
        hot = sb("hot", [P, TOPK, B, E_], f32)
        both = sb("both", [P, B, E_], f16)
        before = sb("before", [P, B, E_], f16)
        rank_e = sb("rank_e", [P, B, E_], f32)
        masked = sb("masked", [P, TOPK, B, E_], f32)
        rank = sb("rank", [P, TOPK, B], f32)
        keep = sb("keep", [P, TOPK, B], f32)
        slot = sb("slot", [P, TOPK, B], f32)
        send = sb("send", [P, TOPK, B], f32)
        send_i = sb("send_i", [P, TOPK, B], i32)
        gap = sb("gap", [P, B], f32)
        e2 = sb("e2", [P, B], f32)

        pt = [c.enter_context(nc.psum_tensor(f"pt3_{i}", [P, 512], f32)) for i in range(2)]
        pl = c.enter_context(nc.psum_tensor("pl", [P, B * E_], f32))
        pr = c.enter_context(nc.psum_tensor("pr", [P, B * E_], f32))

        rw_in, zeroed, filled = sem("rw_in"), sem("zeroed3"), sem("filled")
        made = sem("made3")
        v_step = sem("v_step3")
        var_ready, std_ready = sem("var_ready3"), sem("std_ready3")
        xn_ready, xt_ready, xt_read, logit_ready = (sem(n) for n in ("xn_ready3", "xt_ready3", "xt_read3", "logit_ready"))
        before_ready = sem("before_ready")
        both_ready, rank_ready, gap_ready, exp_ready, send_ready, sent = (
            sem(n) for n in ("both_ready", "rank_ready", "gap_ready", "exp_ready3", "send_ready", "sent"))

        with nc.Block() as block:

            @block.sync
            def _(sp):
                sp.dma_start(rw[:, :, :], rwT.rearrange("(c p) e -> p c e", p=P)).then_inc(rw_in, 16)
                sp.wait_ge(zeroed, 1)
                rows = E_ * CAP
                for r in range(0, rows, P):
                    n = min(P, rows - r)
                    sp.dma_start(xbuf[r:r + n, :], zeros[0:n, :]).then_inc(filled, 16)

            @block.gpsimd
            def _(gp):
                gp.memset(zeros[:, :], 0.0).then_inc(zeroed, 1)
                gp.memset(ones_sq[:, :], 1.0).then_inc(made, 1)
                gp.iota(expert_i[:, :], [[1, E_]], base=0, channel_multiplier=0).then_inc(made, 1)
                gp.wait_ge(made, 2)
                gp.affine_select(out=upper[:, :], in_=ones_sq[:, :], compare_op=ALU.is_gt, fill=0.0, base=0,
                                 pattern=[[1, P]], channel_multiplier=-1).then_inc(made, 1)
                gp.wait_ge(send_ready, 1)
                gp.wait_ge(filled, 16 * (-(-E_ * CAP // P)))
                for t in range(B):
                    for k in range(TOPK):
                        gp.indirect_dma_start(xbuf, bass.IndirectOffsetOnAxis(ap=send_i[:, k, t:t + 1], axis=0),
                                              xn3[:, t, :], None, bounds_check=E_ * CAP - 1, oob_is_err=False).then_inc(sent, 16)
                gp.wait_ge(sent, 16 * B * TOPK)

            @block.scalar
            def _(act):
                act.wait_ge(var_ready, 1)
                act.activation(std[:, :], var[:, :], ACT.Sqrt).then_inc(std_ready, 1)
                for t in range(B):
                    act.wait_ge(xt_ready, t + 1)
                    if t >= 2:
                        act.wait_ge(logit_ready, t - 1)
                    act.activation(xt[:, t % 2], pt[t % 2][:, :].rearrange("p (c t) -> p c t", c=EC), ACT.Copy).then_inc(xt_read, 1)
                act.wait_ge(gap_ready, 1)
                act.activation(e2[:, :], gap[:, :], ACT.Exp).then_inc(exp_ready, 1)

            @block.vector
            def _(dve):
                steps = Steps(dve, v_step)

                def do(instruction):
                    steps.did(instruction)
                    steps.wait()

                for t in range(B):
                    steps.did(dve.bn_stats(st[:, t, :], x1[:, t, :]))
                steps.wait()
                for t in range(B):
                    steps.did(dve.bn_aggr(mv[:, t, :], st[:, t, :]))
                steps.wait()
                dve.tensor_scalar(var[:, :], mv[:, :, 1], EPS, None, ALU.add).then_inc(var_ready, 1)
                dve.wait_ge(std_ready, 1)
                rsqrt_from_std(dve, steps, rs, std, var)
                for t in range(B):
                    dve.tensor_scalar(xn3[:, t, :], x1[:, t, :], mv[:, t, 0:1], rs[:, t:t + 1],
                                      ALU.subtract, ALU.mult).then_inc(xn_ready, 1)
                dve.wait_ge(xn_ready, B)
                do(dve.tensor_tensor(x1[:, :, :], x1[:, :, :], xn3[:, :, :], ALU.add))
                dve.wait_ge(made, 3)
                do(dve.tensor_copy(expert_f[:, :], expert_i[:, :]))
                dve.wait_ge(logit_ready, B)
                do(dve.tensor_copy(logits[:, :, :], pl[:, :].rearrange("p (t e) -> p t e", t=B)))
                for t in range(B):
                    steps.did(dve.max(top[:, t, :], logits[:, t, :]))
                steps.wait()
                for t in range(B):
                    steps.did(dve.max_index(top_i[:, t, :], top[:, t, :], logits[:, t, :]))
                dve.tensor_tensor(gap[:, :], top[:, :, 1], top[:, :, 0], ALU.subtract).then_inc(gap_ready, 1)
                steps.wait()
                do(dve.tensor_copy(chosen[:, :, :].rearrange("p k t -> p t k"), top_i[:, :, 0:TOPK]))
                for k in range(TOPK):
                    steps.did(dve.tensor_tensor(hot[:, k], chosen[:, k, :].unsqueeze(2).to_broadcast([P, B, E_]),
                                                expert_f[:, :].unsqueeze(1).to_broadcast([P, B, E_]), ALU.is_equal))
                steps.wait()
                dve.tensor_tensor(both[:, :, :], hot[:, 0], hot[:, 1], ALU.add).then_inc(both_ready, 1)
                do(dve.memset(before[:, 0, :], 0.0))
                dve.wait_ge(both_ready, 1)
                for t in range(1, B):
                    dve.tensor_tensor(before[:, t, :], before[:, t - 1, :], both[:, t - 1, :], ALU.add).then_inc(before_ready, 1)
                    dve.wait_ge(before_ready, t)
                dve.wait_ge(exp_ready, 1)
                do(dve.tensor_scalar(gates[:, 0, :], e2[:, :], 1.0, None, ALU.add))
                do(dve.reciprocal(gates[:, 0, :], gates[:, 0, :]))
                do(dve.tensor_tensor(gates[:, 1, :], gates[:, 0, :], e2[:, :], ALU.mult))
                dve.wait_ge(rank_ready, 1)
                do(dve.tensor_copy(rank_e[:, :, :], pr[:, :].rearrange("p (t e) -> p t e", t=B)))
                for k in range(TOPK):
                    steps.did(dve.tensor_tensor(masked[:, k], hot[:, k], rank_e[:, :, :], ALU.mult))
                steps.wait()
                do(dve.tensor_reduce(rank[:, :, :], masked[:, :, :, :], AX.X, ALU.add))
                do(dve.tensor_scalar(keep[:, :, :], rank[:, :, :], float(CAP), None, ALU.is_lt))
                do(dve.tensor_scalar(slot[:, :, :], rank[:, :, :], float(CAP - 1), None, ALU.min))
                do(dve.scalar_tensor_tensor(slot[:, :, :], chosen[:, :, :], float(CAP), slot[:, :, :], ALU.mult, ALU.add))
                do(dve.tensor_scalar(send[:, :, :], keep[:, :, :], -DROPPED, DROPPED, ALU.mult, ALU.add))
                do(dve.tensor_tensor(send[:, :, :], send[:, :, :], slot[:, :, :], ALU.add))
                dve.tensor_copy(send_i[:, :, :], send[:, :, :]).then_inc(send_ready, 1)
                dve.tensor_copy(slot_i[:, :, :], slot[:, :, :])
                dve.tensor_tensor(gates[:, :, :], gates[:, :, :], keep[:, :, :], ALU.mult)

            @block.tensor
            def _(pe):
                pe.wait_ge(rw_in, 16)

                def transpose_xn(t):
                    pe.wait_ge(xn_ready, t + 1)
                    if t >= 2:
                        pe.wait_ge(xt_read, t - 1)
                    for e in range(EC):
                        last = pe.transpose(pt[t % 2][:, P * e:P * e + P], xn3[:, t, P * e:P * e + P], ident[:, :])
                    last.then_inc(xt_ready, 1)

                transpose_xn(0)
                for t in range(B):
                    if t + 1 < B:
                        transpose_xn(t + 1)
                    pe.wait_ge(xt_read, t + 1)
                    for e in range(EC):
                        last = pe.matmul(pl[:, E_ * t:E_ * t + E_], xt[:, t % 2, e, :], rw[:, e, :], start=e == 0, stop=e == EC - 1)
                    last.then_inc(logit_ready, 1)
                pe.wait_ge(both_ready, 1)
                pe.wait_ge(made, 3)
                pe.matmul(pr[:, :], upper[:, :], both[:, :, :].rearrange("p t e -> p (t e)"), start=True, stop=False)
                pe.wait_ge(before_ready, B - 1)
                pe.matmul(pr[:, :], ones_sq[:, :], before[:, :, :].rearrange("p t e -> p (t e)"),
                          start=False, stop=True).then_inc(rank_ready, 1)


def experts(nc, w1, w2, xbuf, obuf, ident):
    with ExitStack() as c:
        def sb(name, shape, dt):
            return c.enter_context(nc.sbuf_tensor(name, shape, dt))

        def sem(name):
            return c.enter_context(nc.semaphore(name))

        NST = 4
        stage = sb("stage_w", [P, NST, EC, 512], f32)
        w_hi = sb("w_hi3", [P, 8, EC, 512], f16)
        w_lo = sb("w_lo3", [P, 8, EC, 512], f16)
        xg = sb("xg", [P, CT, D], f32)
        xt_hi = sb("xt3_hi", [P, EC, CAP], f16)
        xt_lo = sb("xt3_lo", [P, EC, CAP], f16)
        hf = sb("hf", [P, 2, CAP], f32)
        h_hi = sb("h_hi", [P, 8, CAP], f16)
        h_lo = sb("h_lo", [P, 8, CAP], f16)
        o_sb = sb("o_sb", [P, CT, D], f32)

        ph = [c.enter_context(nc.psum_tensor(f"ph{i}", [P, 512], f32)) for i in range(2)]
        po = [c.enter_context(nc.psum_tensor(f"po3_{i}", [P, 512], f32)) for i in range(CT)]
        pt = [c.enter_context(nc.psum_tensor(f"ptx{i}", [P, 512], f32)) for i in range(3)]

        stage_in = [sem(f"w_in{i}") for i in range(NST)]
        stage_hi, stage_lo = sem("w_hi_ready"), sem("w_lo_ready")
        xg_in = sem("xg_in")
        xt_ready, xt_hi_ready, xt_lo_ready = sem("xg_t_ready"), sem("xg_hi_ready"), sem("xg_lo_ready")
        a_ready = sem("a_ready")
        a_done = sem("a_done")
        h_step, h_ready = sem("h_step"), sem("h_ready")
        b_done = sem("b_done")
        o_ready, o_stored = sem("o_sb_ready"), sem("o_stored")

        ORDER = [("a", 0), ("a", 1), ("b", 0), ("a", 2), ("b", 1), ("a", 3), ("b", 2), ("b", 3)]
        SLOT = {item: s for s, item in enumerate(ORDER)}

        def wait_used(eng, e, s):
            kind, q = ORDER[s]
            if kind == "a":
                eng.wait_ge(a_ready, 16 * (e - 1) + 4 * q + 4)
            else:
                eng.wait_ge(b_done, 4 * (e - 1) + q + 1)

        with nc.Block() as block:

            @block.sync
            def _(sp):
                def load(e, s, first=False):
                    kind, q = ORDER[s]
                    src = (w1 if kind == "a" else w2)[bass.ds(e, 1), :, :].rearrange("a r n -> (a r) n")
                    if kind == "a":
                        src = src.rearrange("(c p) f -> p c f", p=P)[:, :, 512 * q:512 * q + 512]
                    else:
                        src = src[512 * q:512 * q + 512, :].rearrange("(c p) h -> p c h", p=P)
                    if not isinstance(e, int):
                        sp.compute_val(e * (D * F) * 4)
                    if not first:
                        wait_each(sp, (stage_hi, 8 * e + s - NST + 1), (stage_lo, 8 * e + s - NST + 1))
                    sp.dma_start(stage[:, s % NST], src).then_inc(stage_in[s % NST], 16)

                for s in range(8):
                    load(0, s, first=s < NST)
                with sp.Fori(1, E_) as e:
                    for s in range(8):
                        load(e, s)

            @block.gpsimd
            def _(gp):
                def load_x(e):
                    for i in range(CT):
                        row = e * CAP + P * i
                        gp.dma_start(xg[0:ROWS[i], i, :], xbuf[bass.ds(row, ROWS[i]), :]).then_inc(xg_in, 16)

                def store(e):
                    gp.wait_ge(o_ready, CT * e + CT)
                    for i in range(CT):
                        row = e * CAP + P * i
                        gp.dma_start(obuf[bass.ds(row, ROWS[i]), :], o_sb[0:ROWS[i], i, :]).then_inc(o_stored, 16)

                load_x(0)

                def body(e):
                    gp.wait_ge(xt_ready, EC * e + EC)
                    load_x(e + 1)
                    store(e)

                body(0)
                with gp.Fori(1, E_ - 1) as e:
                    body(e)
                store(E_ - 1)
                gp.wait_ge(o_stored, 16 * CT * E_)

            @block.scalar
            def _(act):
                def split(e, s):
                    act.wait_ge(stage_in[s % NST], 16 * (2 * e + s // NST + 1))
                    if not (isinstance(e, int) and e == 0):
                        wait_used(act, e, s)
                    act.activation(w_hi[:, s], stage[:, s % NST], ACT.Copy, scale=WSCALE).then_inc(stage_hi, 1)

                def silu(e, q):
                    for f in range(4):
                        n = 16 * e + 4 * q + f
                        act.wait_ge(a_ready, n + 1)
                        if not (isinstance(e, int) and e == 0 and q == 0 and f < 2):
                            act.wait_ge(h_ready, n - 1)
                        act.activation(hf[:, f % 2, :], ph[f % 2][:, 0:CAP], ACT.Silu, scale=1.0 / WSCALE).then_inc(a_done, 1)

                def split_x(e, chunks):
                    for i in chunks:
                        act.wait_ge(xt_ready, EC * e + i + 1)
                        act.activation(xt_hi[:, i, :], pt[i % 3][:, 0:CAP], ACT.Copy).then_inc(xt_hi_ready, 1)

                for s in range(3):
                    split(0, s)
                split_x(0, range(EC))
                for s in range(3, 7):
                    split(0, s)

                def body(e, last):
                    silu(e, 0)
                    split(e, 7)
                    silu(e, 1)
                    if not last:
                        split(e + 1, 0)
                        split(e + 1, 1)
                    silu(e, 2)
                    if not last:
                        split(e + 1, 2)
                    silu(e, 3)
                    if not last:
                        for s in (3, 4, 5):
                            split(e + 1, s)
                        split_x(e + 1, range(EC))
                        split(e + 1, 6)

                body(0, False)
                with act.Fori(1, E_ - 1) as e:
                    body(e, False)
                body(E_ - 1, True)

            @block.vector
            def _(dve):
                def split(e, s):
                    dve.wait_ge(stage_hi, 8 * e + s + 1)
                    dve.scalar_tensor_tensor(w_lo[:, s], stage[:, s % NST], WSCALE, w_hi[:, s],
                                             ALU.mult, ALU.subtract).then_inc(stage_lo, 1)

                def split_h(e, q):
                    if not (isinstance(e, int) and e == 0 and q < 2):
                        dve.wait_ge(b_done, 4 * e + q - 1)
                    for f in range(4):
                        n = 16 * e + 4 * q + f
                        at = 4 * (q % 2) + f
                        dve.wait_ge(a_done, n + 1)
                        dve.tensor_copy(h_hi[:, at, :], hf[:, f % 2, :]).then_inc(h_step, 1)
                        dve.wait_ge(h_step, n + 1)
                        dve.tensor_tensor(h_lo[:, at, :], hf[:, f % 2, :], h_hi[:, at, :], ALU.subtract).then_inc(h_ready, 1)

                def split_x(e, chunks):
                    for i in chunks:
                        dve.wait_ge(xt_hi_ready, EC * e + i + 1)
                        dve.tensor_tensor(xt_lo[:, i, :], pt[i % 3][:, 0:CAP], xt_hi[:, i, :], ALU.subtract).then_inc(xt_lo_ready, 1)

                def read_out(e):
                    dve.wait_ge(b_done, 4 * e + 4)
                    if not (isinstance(e, int) and e == 0):
                        dve.wait_ge(o_stored, 16 * CT * e)
                    for i in range(CT):
                        dve.tensor_scalar(o_sb[0:ROWS[i], i, :], po[i][0:ROWS[i], :], 1.0 / WSCALE, None, ALU.mult).then_inc(o_ready, 1)

                for s in range(3):
                    split(0, s)
                split_x(0, range(EC))
                for s in range(3, 7):
                    split(0, s)

                def body(e, last):
                    split_h(e, 0)
                    split(e, 7)
                    split_h(e, 1)
                    if not last:
                        split(e + 1, 0)
                        split(e + 1, 1)
                    split_h(e, 2)
                    if not last:
                        split(e + 1, 2)
                    split_h(e, 3)
                    if not last:
                        for s in (3, 4, 5):
                            split(e + 1, s)
                        split_x(e + 1, range(EC))
                        split(e + 1, 6)
                    read_out(e)

                body(0, False)
                with dve.Fori(1, E_ - 1) as e:
                    body(e, False)
                body(E_ - 1, True)

            @block.tensor
            def _(pe):
                def wait_split(e, s):
                    wait_each(pe, (stage_hi, 8 * e + s + 1), (stage_lo, 8 * e + s + 1))

                def transpose_x(e, chunks):
                    for i in chunks:
                        if i == 0:
                            pe.wait_ge(xg_in, 16 * CT * (e + 1))
                            if not (isinstance(e, int) and e == 0):
                                pe.wait_ge(xt_lo_ready, EC * e)
                        if i == 3:
                            pe.wait_ge(xt_lo_ready, EC * e + 1)
                        for j in range(CT):
                            last = pe.transpose(pt[i % 3][:, P * j:P * j + ROWS[j]], xg[0:ROWS[j], j, P * i:P * i + P],
                                                ident[0:ROWS[j], 0:ROWS[j]])
                        last.then_inc(xt_ready, 1)

                def hidden(e, q):
                    wait_split(e, SLOT["a", q])
                    if q == 0:
                        pe.wait_ge(xt_lo_ready, EC * e + EC)
                    s = SLOT["a", q]
                    for f in range(4):
                        n = 16 * e + 4 * q + f
                        if not (isinstance(e, int) and e == 0 and q == 0 and f < 2):
                            pe.wait_ge(a_done, n - 1)
                        n_mm = 0
                        for w_part, x_part in mm_terms(w_hi, w_lo, xt_hi, xt_lo):
                            for i in range(EC):
                                last = pe.matmul(ph[f % 2][:, 0:CAP], w_part[:, s, i, P * f:P * f + P], x_part[:, i, :],
                                                 start=n_mm == 0, stop=n_mm == 3 * EC - 1)
                                n_mm += 1
                        last.then_inc(a_ready, 1)

                def output(e, q, chunks):
                    s = SLOT["b", q]
                    if 0 in chunks:
                        wait_split(e, s)
                        if q == 0 and not (isinstance(e, int) and e == 0):
                            pe.wait_ge(o_ready, CT * e)
                    for f in chunks:
                        pe.wait_ge(h_ready, 16 * e + 4 * q + f + 1)
                        at = 4 * (q % 2) + f
                        for i in range(CT):
                            rows = slice(P * i, P * i + ROWS[i])
                            for n, (h_part, w_part) in enumerate(mm_terms(h_hi, h_lo, w_hi, w_lo)):
                                last = pe.matmul(po[i][0:ROWS[i], :], h_part[:, at, rows], w_part[:, s, f, :],
                                                 start=q == 0 and f == 0 and n == 0, stop=q == FQ - 1 and f == 3 and n == 2)
                    if 3 in chunks:
                        last.then_inc(b_done, 1)

                transpose_x(0, range(EC))

                def body(e, last):
                    hidden(e, 0)
                    hidden(e, 1)
                    output(e, 0, range(4))
                    hidden(e, 2)
                    output(e, 1, range(4))
                    hidden(e, 3)
                    output(e, 2, range(4))
                    if not last:
                        transpose_x(e + 1, range(3))
                    output(e, 3, range(2))
                    if not last:
                        transpose_x(e + 1, range(3, 4))
                    output(e, 3, range(2, 4))

                body(0, False)
                with pe.Fori(1, E_ - 1) as e:
                    body(e, False)
                body(E_ - 1, True)


def combine(nc, x1, slot_i, gates, obuf, out):
    with ExitStack() as c:
        pair = c.enter_context(nc.sbuf_tensor("pair", [P, B, TOPK, D], f32))
        got = [c.enter_context(nc.semaphore(f"got{t}")) for t in range(B)]
        step, summed, stored = (c.enter_context(nc.semaphore(n)) for n in ("step5", "summed", "stored"))
        with nc.Block() as block:

            @block.gpsimd
            def _(gp):
                for t in range(B):
                    for k in range(TOPK):
                        gp.indirect_dma_start(pair[:, t, k, :], None, obuf,
                                              bass.IndirectOffsetOnAxis(ap=slot_i[:, k, t:t + 1], axis=0)).then_inc(got[t], 16)

            @block.vector
            def _(dve):
                for t in range(B):
                    dve.wait_ge(got[t], 16 * TOPK)
                    dve.scalar_tensor_tensor(x1[:, t, :], pair[:, t, 0, :], gates[:, 0, t:t + 1], x1[:, t, :],
                                             ALU.mult, ALU.add).then_inc(step, 1)
                    dve.wait_ge(step, t + 1)
                    dve.scalar_tensor_tensor(x1[:, t, :], pair[:, t, 1, :], gates[:, 1, t:t + 1], x1[:, t, :],
                                             ALU.mult, ALU.add).then_inc(summed, 1)

            @block.sync
            def _(sp):
                for t in range(B):
                    sp.wait_ge(summed, t + 1)
                    sp.dma_start(out[t], x1[:, t, :]).then_inc(stored, 16)
                sp.wait_ge(stored, 16 * B)


def build_block(nc, x, ctxT, wqT, wkT, wvT, woT, wiT, in_b, qoT, out_b, rwT, w1, w2, out):
    xbuf = nc.dram_tensor("xbuf", [E_ * CAP, D], f32).ap()
    obuf = nc.dram_tensor("obuf", [E_ * CAP, D], f32).ap()
    with ExitStack() as c:
        def sb(name, shape, dt):
            return c.enter_context(nc.sbuf_tensor(name, shape, dt))

        x1 = sb("x1", [P, B, D], f32)
        ident = sb("ident", [P, P], f32)
        ident16 = sb("ident16", [P, P], f16)
        ones = sb("ones", [P, HD], f32)
        ones16 = sb("ones16", [P, 1], f16)
        slot_i = sb("slot_i", [P, TOPK, B], i32)
        gates = sb("gates", [P, TOPK, B], f32)
        constants(nc, ident, ident16, ones, ones16)
        cross_attention(nc, x, ctxT, wqT, wkT, wvT, woT, x1, ident, ident16, ones, ones16)
        quantised_self_attention(nc, wiT, in_b, qoT, out_b, x1, ident, ident16)
        with nc.sbuf_tensor("xn3", [P, B, D], f32) as xn3:
            route(nc, rwT, x1, xn3, slot_i, gates, xbuf, ident, ident16)
        experts(nc, w1, w2, xbuf, obuf, ident)
        combine(nc, x1, slot_i, gates, obuf, out)


def kernel(x, ctx_1024, L0_xattn_Wq, L0_xattn_Wk, L0_xattn_Wv, L0_xattn_Wo, L0_attn_key, L0_attn_value,
           L0_attn_in_w, L0_attn_in_b, L0_attn_out_w, L0_attn_out_b, L0_ffn_router_w, L0_ffn_w1, L0_ffn_w2):
    import numpy as np
    import concourse.bacc as bacc
    from concourse.bass_utils import run_bass_kernel_spmd

    arrays = {
        "x": x, "ctxT": np.asarray(ctx_1024).transpose(0, 2, 1), "wqT": np.asarray(L0_xattn_Wq).T,
        "wkT": np.asarray(L0_xattn_Wk).T, "wvT": np.asarray(L0_xattn_Wv).T, "woT": np.asarray(L0_xattn_Wo).T,
        "wiT": np.asarray(L0_attn_in_w).T, "in_b": L0_attn_in_b, "qoT": np.asarray(L0_attn_out_w).T,
        "out_b": L0_attn_out_b, "rwT": np.asarray(L0_ffn_router_w).T, "w1": L0_ffn_w1, "w2": L0_ffn_w2,
    }
    arrays = {f"in_{n}": np.ascontiguousarray(a) for n, a in arrays.items()}
    nc = bacc.Bacc("TRN2", target_bir_lowering=False, num_devices=1)
    args = [nc.dram_tensor(n, a.shape, mybir.dt.from_np(a.dtype), kind="ExternalInput").ap() for n, a in arrays.items()]
    args.append(nc.dram_tensor("out_x", (B, T, D), f32, kind="ExternalOutput").ap())
    build_block(nc, *args)
    return run_bass_kernel_spmd(nc, [arrays], core_ids=[0]).results[0]["out_x"]
```

```python
import concourse.bass as bass
from concourse import mybir
from contextlib import ExitStack
from math import sqrt

f32 = mybir.dt.float32
f16 = mybir.dt.float16
i32 = mybir.dt.int32
u32 = mybir.dt.uint32
ALU = mybir.AluOpType
ACT = mybir.ActivationFunctionType
AX = mybir.AxisListType

P = 128
B, T, D = 8, 128, 512
S = 2048
H, HD = 16, 32
EC = D // P
GH = P // HD
G = H // GH
KB = S // 512
KC = S // P
UNITS = 8
WSCALE = 1024.0
EPS = 1e-5
QMAX, QFLOOR = 127.0, 1e-8
ROUND = 1.5 * 2.0 ** 23
QK = 3 * HD
WPIECES = 4 * EC
QKM = QK + 1


def mm_terms(hi_l, lo_l, hi_r, lo_r):
    return ((hi_l, hi_r), (lo_l, hi_r), (hi_l, lo_r))


class Steps:

    def __init__(self, eng, sem, base=0):
        self.eng, self.sem, self.base, self.n = eng, sem, base, 0

    def did(self, instruction):
        instruction.then_inc(self.sem, 1)
        self.n += 1

    def wait(self):
        self.eng.wait_ge(self.sem, self.base + self.n)


def wait_each(eng, *waits):
    for _, value in waits:
        if not isinstance(value, int):
            eng.compute_val(value)
    for sem, value in waits:
        eng.wait_ge(sem, value)


def cross_attention(nc, x, ctxT, wqT, wkT, wvT, woT, wiT, qoT, weights_q, wmax, wscale, x1, ident, ident16, ones, ones16):
    with ExitStack() as c:
        def sb(name, shape, dt):
            return c.enter_context(nc.sbuf_tensor(name, shape, dt))

        def sem(name):
            return c.enter_context(nc.semaphore(name))

        stage = sb("stage", [P, 2, 2, 512], f32)
        ctx_hi = sb("ctx_hi", [P, KB, EC, 512], f16)
        ctx_lo = sb("ctx_lo", [P, KB, EC, 512], f16)
        w_hi = sb("w_hi", [P, 3, EC, D], f16)
        w_lo = sb("w_lo", [P, 3, EC, D], f16)
        wo = sb("wo_sb", [P, EC, D], f32)
        v_sb = sb("v_sb", [P, 2, KC, 256], f32)
        k_hi = sb("k_hi", [P, S], f16)
        k_lo = sb("k_lo", [P, S], f16)
        ks = sb("ks", [P, 2, GH, S], f16)
        q_hi = sb("q_hi", [P, G, T], f16)
        q_lo = sb("q_lo", [P, G, T], f16)
        qs = sb("qs", [P, H, T], f16)
        xn = sb("xn", [P, D], f32)
        xt_hi = sb("xt_hi", [P, EC, T], f16)
        xt_lo = sb("xt_lo", [P, EC, T], f16)
        probs = sb("probs", [P, 4, 1024], f32)
        acc_v = sb("acc_v", [P, 1024], f32)
        acc_g = sb("acc_g", [P, 1024], f32)
        mx = sb("mx", [P, GH, 2], f32)
        nm = sb("nm", [P, GH], f32)
        diag = sb("diag", [P, GH, T], f16)
        rden = sb("rden", [P, T], f32)
        ot = sb("ot", [P, G, T], f32)
        st = sb("st", [P, B, 6], f32)
        mv = sb("mv", [P, B, 2], f32)
        var = sb("var", [P, B], f32)
        rs = sb("rs", [P, B], f32)
        tmp = sb("tmp", [P, B], f32)

        wq_f = sb("wq_f", [P, 2, 512], f32)
        wq_i = sb("wq_i", [P, 2, 512], f16)
        wq_max = sb("wq_max", [P, WPIECES], f32)
        wq_part = sb("wq_part", [P, 2], f32)
        wq_all = sb("wq_all", [P, P, 2], f32)
        wq_inv = sb("wq_inv", [P, 2], f32)

        proj = [c.enter_context(nc.psum_tensor(f"proj{i}", [P, 512], f32)) for i in range(2)]
        sc = [c.enter_context(nc.psum_tensor(f"sc{i}", [P, 1024], f32)) for i in range(2)]
        po = c.enter_context(nc.psum_tensor("po", [P, 512], f32))
        misc = c.enter_context(nc.psum_tensor("misc", [P, 512], f32))

        x_in = sem("x_in")
        wo_in = sem("wo_in")
        w_in = [sem(f"w_in{i}") for i in range(3)]
        w_hi_ready = sem("w_hi_ready")
        w_lo_ready = sem("w_lo_ready")
        stage_in = [sem(f"stage_in{i}") for i in range(2)]
        stage_hi = sem("stage_hi")
        stage_lo = sem("stage_lo")
        rows_set = sem("rows_set")
        var_ready = sem("var_ready")
        std_ready = sem("std_ready")
        xn_ready = sem("xn_ready")
        xt_ready = sem("xt_ready")
        xt_split_hi = sem("xt_split_hi")
        xt_split_lo = sem("xt_split_lo")
        q_ready = sem("q_ready")
        q_split_hi = sem("q_split_hi")
        q_split_lo = sem("q_split_lo")
        qs_in = sem("qs_in")
        proj_ready = sem("proj_ready")
        proj_act = sem("proj_act")
        k_low = sem("k_low")
        ks_in = [sem(f"ks_in{i}") for i in range(2)]
        m_ready = sem("m_ready")
        m_read = sem("m_read")
        diag_ready = sem("diag_ready")
        row_ready = sem("row_ready")
        row_set = sem("row_set")
        s_ready = sem("s_ready")
        e_ready = sem("e_ready")
        pv_done = sem("pv_done")
        sum_v = sem("sum_v")
        sum_g = sem("sum_g")
        group_done = sem("group_done")
        ot_ready = sem("ot_ready")
        o_ready = sem("o_ready")
        x1_ready = sem("x1_ready")
        v_step = sem("v_step")
        wq_in = [sem(f"wq_in{i}") for i in range(2)]
        wq_seen = sem("wq_seen")
        wq_step = sem("wq_step")
        wmax_ready, wmax_moved = sem("wmax_ready"), sem("wmax_moved")
        wq_scaled = sem("wq_scaled")
        wq_round, wq_int = sem("wq_round"), sem("wq_int")
        wq_out = [sem(f"wq_out{i}") for i in range(2)]

        ctx_v = ctxT.rearrange("b (c p) s -> b p c s", p=P)
        W_ORDER = (2, 1, 0)
        w_stage = [probs[:, 0:2, :], probs[:, 2:4, :], v_sb[:, 1, 0:8, :]]
        w_stage = [w.rearrange("p a n -> p (a n)").rearrange("p (c d) -> p c d", c=EC) for w in w_stage]

        USES = ([("k", 0, i) for i in range(KB)] + [("v", 1, i) for i in (0, 1, 2)]
                + [("k", 1, i) for i in range(KB)] + [("v", 1, 3)]
                + [("k", 2, i) for i in range(KB)] + [("v", 1, i) for i in (4, 5)]
                + [("k", 3, i) for i in range(KB)] + [("v", 1, i) for i in (6, 7)] + [("v", 0, i) for i in range(8)])
        FILL = {0: [(1, i) for i in (6, 7)], 1: [(1, i) for i in range(8, 12)],
                2: [(1, i) for i in range(12, 16)], 3: [(0, i) for i in range(10, 16)]}

        def weight_piece(n):
            third, e = n // EC, n % EC
            src = wiT[:, 512 * third:512 * third + 512] if third < 3 else qoT
            return src[P * e:P * e + P, :]

        def use_k(b, g, kb):
            return 8 + 32 * b + USES.index(("k", g, kb))

        def use_v(b, half, n):
            at = USES.index(("v", half, n))
            return 8 + 32 * b + at if half else 32 * b + at - 24

        def bank(use_in_body):
            return use_in_body % 2

        def first_batch(b):
            return isinstance(b, int) and b == 0

        def fill_after(g, unit, last):
            pieces = FILL[g] if not (last and g == 3) else []
            return pieces[0:2] if unit < 0 else pieces[2 + unit:3 + unit]

        def wait_k_stacked(eng, b, g):
            if isinstance(b, int) and b == 0 and g == 0:
                return
            n = 2 * b + (g - 1) // 2 + 1 if g else 2 * b
            eng.wait_ge(ks_in[(g - 1) % 2], 192 * n)

        with nc.Block() as block:

            @block.sync
            def _(sp):
                def load_w(i):
                    w = (wqT, wkT, wvT)[W_ORDER[i]].rearrange("(c p) d -> p c d", p=P)
                    sp.dma_start(w_stage[i], w).then_inc(w_in[i], 16)

                def load_ctx(b, s):
                    n = 8 * b + s
                    if not isinstance(b, int):
                        sp.compute_val(b * (D * S) * 4)
                    if not (first_batch(b) and s < 2):
                        wait_each(sp, (stage_hi, n - 1), (stage_lo, n - 1))
                    src = ctx_v[bass.ds(b, 1), :, 2 * (s % 2):2 * (s % 2) + 2, 512 * (s // 2):512 * (s // 2) + 512]
                    sp.dma_start(stage[:, s % 2], src.rearrange("a p c s -> (a p) c s")).then_inc(stage_in[s % 2], 16)

                def stack_q(b):
                    waits = [(q_split_hi, b + 1), (q_split_lo, b + 1)]
                    if not first_batch(b):
                        waits.append((s_ready, 32 * b))
                    wait_each(sp, *waits)
                    for row, part in ((0, q_hi), (HD, q_hi), (2 * HD, q_lo)):
                        for j in range(GH):
                            sp.dma_start(qs[row:row + HD, j:H:GH, :], part[HD * j:HD * j + HD, :, :]).then_inc(qs_in, 16)

                def stack_k(b, g):
                    waits = [(proj_act, use_k(b, g, KB - 1) + 1), (k_low, 16 * b + 4 * g + KB)]
                    if g >= 2 or not first_batch(b):
                        waits.append((s_ready, 8 * (4 * b + g - 1)))
                    wait_each(sp, *waits)
                    for row, part in ((0, k_hi), (HD, k_lo), (2 * HD, k_hi)):
                        for j in range(GH):
                            sp.dma_start(ks[row:row + HD, g % 2, j, :], part[HD * j:HD * j + HD, :]).then_inc(ks_in[g % 2], 16)

                load_w(0)
                load_ctx(0, 0)
                load_ctx(0, 1)
                load_w(1)
                sp.dma_start(x1[:, :, :], x.rearrange("b p d -> p b d")).then_inc(x_in, 16)
                load_w(2)
                for s in range(2, 8):
                    load_ctx(0, s)
                sp.dma_start(wo[:, :, :], woT.rearrange("(c p) d -> p c d", p=P)).then_inc(wo_in, 16)

                def body(b, last):
                    stack_q(b)
                    stack_k(b, 0)
                    stack_k(b, 1)
                    if not last:
                        load_ctx(b + 1, 0)
                        load_ctx(b + 1, 1)
                    stack_k(b, 2)
                    stack_k(b, 3)
                    if not last:
                        for s in range(2, 8):
                            load_ctx(b + 1, s)

                body(0, False)
                with sp.Fori(1, B - 1) as b:
                    body(b, False)
                body(B - 1, True)

            @block.gpsimd
            def _(gp):
                gp.memset(ks[QK:P, :, :, :], 1.0).then_inc(rows_set, 1)

                def load_weight(n, round_trip):
                    if round_trip == 0 and n >= 2:
                        gp.wait_ge(wq_seen, n - 1)
                    if round_trip == 1 and n < 2:
                        gp.wait_ge(wq_seen, WPIECES)
                    gp.dma_start(wq_f[:, n % 2, :], weight_piece(n)).then_inc(wq_in[n % 2], 16)

                def quantise_weight(n):
                    which = n // (3 * EC)
                    gp.wait_ge(wq_in[n % 2], 16 * (WPIECES // 2 + n // 2 + 1))
                    gp.tensor_scalar(wq_f[:, n % 2, :], wq_f[:, n % 2, :], wq_inv[:, which:which + 1], ROUND,
                                     ALU.mult, ALU.add).then_inc(wq_round, 1)
                    gp.wait_ge(wq_round, n + 1)
                    if n >= 2:
                        gp.wait_ge(wq_out[n % 2], 16 * (n // 2))
                    gp.tensor_scalar(wq_i[:, n % 2, :], wq_f[:, n % 2, :], -ROUND, 1.0, ALU.add, ALU.mult).then_inc(wq_int, 1)
                    gp.wait_ge(wq_int, n + 1)
                    gp.dma_start(weights_q[:, n // EC, n % EC, :], wq_i[:, n % 2, :]).then_inc(wq_out[n % 2], 16)
                    if n + 2 < WPIECES:
                        load_weight(n + 2, 1)

                def body(b, last):
                    for g in range(G):
                        e = 32 * b + UNITS * g
                        if first_batch(b):
                            load_weight(4 * g, 0)
                            load_weight(4 * g + 1, 0)
                        gp.wait_ge(e_ready, e + 4)
                        if not (isinstance(b, int) and b == 0 and g == 0):
                            gp.wait_ge(group_done, 4 * b + g)
                        gp.tensor_tensor(acc_g[:, :], probs[:, 2, :], probs[:, 3, :], ALU.add).then_inc(sum_g, 1)
                        if first_batch(b):
                            load_weight(4 * g + 2, 0)
                        gp.wait_ge(e_ready, e + 7)
                        gp.wait_ge(sum_g, 8 * b + 2 * g + 1)
                        gp.tensor_tensor(acc_g[:, :], acc_g[:, :], probs[:, 2, :], ALU.add).then_inc(sum_g, 1)
                        if first_batch(b):
                            load_weight(4 * g + 3, 0)
                        if last:
                            for n in range(*((0, 6), (6, 11), (11, WPIECES), (WPIECES, WPIECES))[g]):
                                quantise_weight(n)

                body(0, False)
                gp.wait_ge(wmax_ready, 1)
                gp.dma_start(wmax[:, :], wq_part[:, :]).then_inc(wmax_moved, 16)
                gp.wait_ge(wmax_moved, 16)
                gp.dma_start(wq_all[:, :, :], wmax.rearrange("(a p) w -> a p w", a=1).to_broadcast([P, P, 2])).then_inc(wmax_moved, 16)
                load_weight(0, 1)
                load_weight(1, 1)
                with gp.Fori(1, B - 1) as b:
                    body(b, False)
                gp.wait_ge(wq_scaled, 1)
                body(B - 1, True)
                for i in range(2):
                    gp.wait_ge(wq_out[i], 16 * (WPIECES // 2))

            @block.scalar
            def _(act):
                def split_w(i):
                    act.wait_ge(w_in[i], 16)
                    act.activation(w_hi[:, W_ORDER[i]], w_stage[i], ACT.Copy, scale=WSCALE).then_inc(w_hi_ready, 1)

                def split_ctx(b, s):
                    act.wait_ge(stage_in[s % 2], 16 * (4 * b + s // 2 + 1))
                    if not first_batch(b):
                        used = use_k(b - 1, 3, s // 2) if s < 6 else use_v(b - 1, 1, 7)
                        act.wait_ge(proj_ready, used + 1)
                    act.activation(ctx_hi[:, s // 2, 2 * (s % 2):2 * (s % 2) + 2, :], stage[:, s % 2], ACT.Copy).then_inc(stage_hi, 1)

                def copy_v(b, half, n):
                    act.wait_ge(proj_ready, use_v(b, half, n) + 1)
                    if not first_batch(b):
                        act.wait_ge(pv_done, 32 * b if half else 32 * b - 16)
                    elif n == 0 and half == 1:
                        act.wait_ge(w_lo_ready, 3)
                    act.activation(v_sb[:, half, 2 * n:2 * n + 2, :],
                                   proj[bank(USES.index(("v", half, n)))][:, :].rearrange("p (c d) -> p c d", c=2),
                                   ACT.Copy, scale=1.0 / WSCALE).then_inc(proj_act, 1)

                def split_k(b, g, kb):
                    act.wait_ge(proj_ready, use_k(b, g, kb) + 1)
                    if kb == 0:
                        wait_k_stacked(act, b, g)
                    act.activation(k_hi[:, 512 * kb:512 * kb + 512], proj[bank(USES.index(("k", g, kb)))][:, :], ACT.Copy,
                                   scale=1.0 / WSCALE).then_inc(proj_act, 1)

                def set_row(b, g):
                    act.wait_ge(row_ready, 4 * b + g + 1)
                    act.activation(qs[QK:QKM, 4 * g:4 * g + 4, :],
                                   misc[QK:QKM, :].rearrange("p (j t) -> p j t", j=GH), ACT.Copy).then_inc(row_set, 1)

                def exp(b, g, u):
                    e = 32 * b + UNITS * g + u
                    act.wait_ge(s_ready, e + 1)
                    if not (first_batch(b) and g == 0 and u < 4):
                        act.wait_ge(pv_done, e - 3)
                        k = 4 * g + 16 * b
                        m = 2 * g + 8 * b
                        who, val = {0: (sum_v, k - 2), 1: (sum_v, k - 1), 2: (sum_g, m), 3: (sum_v, k),
                                    4: (sum_v, k + 1), 5: (sum_v, k + 1), 6: (sum_g, m + 1), 7: (sum_g, m + 1)}[u]
                        act.wait_ge(who, val)
                    act.activation(probs[:, u % 4, :], sc[u % 2][:, :], ACT.Exp, scale=1.0 / sqrt(HD)).then_inc(e_ready, 1)

                def split_xt(b):
                    act.wait_ge(xt_ready, b + 1)
                    act.activation(xt_hi[:, :, :], misc[:, :].rearrange("p (c t) -> p c t", c=EC), ACT.Copy).then_inc(xt_split_hi, 1)

                def split_q(b):
                    act.wait_ge(q_ready, b + 1)
                    if not first_batch(b):
                        act.wait_ge(qs_in, 192 * b)
                    act.activation(q_hi[:, :, :], misc[:, :].rearrange("p (g t) -> p g t", g=G), ACT.Copy,
                                   scale=1.0 / WSCALE).then_inc(q_split_hi, 1)

                split_w(0)
                split_ctx(0, 0)
                split_ctx(0, 1)
                copy_v(0, 0, 0)
                split_w(1)
                split_ctx(0, 2)
                split_ctx(0, 3)
                copy_v(0, 0, 1)
                act.wait_ge(var_ready, 1)
                act.activation(tmp[:, :], var[:, :], ACT.Sqrt).then_inc(std_ready, 1)
                split_w(2)
                split_ctx(0, 4)
                split_ctx(0, 5)
                copy_v(0, 0, 2)
                copy_v(0, 0, 3)
                split_ctx(0, 6)
                split_ctx(0, 7)
                for n in range(4, 8):
                    copy_v(0, 0, n)
                split_xt(0)
                split_q(0)

                def body(b, last):
                    for kb in range(KB):
                        split_k(b, 0, kb)
                    for n in range(3):
                        copy_v(b, 1, n)
                    for g in range(G):
                        if g < 3:
                            for kb in range(KB):
                                split_k(b, g + 1, kb)
                        elif not last:
                            for n in range(5):
                                if n < 4:
                                    split_ctx(b + 1, 4 + n)
                                copy_v(b + 1, 0, n)
                        if g == 2 and not last:
                            split_ctx(b + 1, 0)
                            split_ctx(b + 1, 1)
                        set_row(b, g)
                        for u in range(-1, UNITS):
                            if u >= 0:
                                exp(b, g, u)
                            for half, piece in fill_after(g, u, last):
                                if piece % 2:
                                    copy_v(b if half else b + 1, half, piece // 2)
                            if not last:
                                if g == 2 and u == 3:
                                    split_xt(b + 1)
                                if g == 2 and u == 6:
                                    split_q(b + 1)
                                if g == 2 and u in (5, 7):
                                    split_ctx(b + 1, 2 + (u == 7))

                body(0, False)
                with act.Fori(1, B - 1) as b:
                    body(b, False)
                body(B - 1, True)

            @block.vector
            def _(dve):
                steps = Steps(dve, v_step)

                def split_w(i):
                    dve.wait_ge(w_hi_ready, i + 1)
                    dve.scalar_tensor_tensor(w_lo[:, W_ORDER[i]], w_stage[i], WSCALE, w_hi[:, W_ORDER[i]],
                                             ALU.mult, ALU.subtract).then_inc(w_lo_ready, 1)

                def split_ctx(b, s):
                    dve.wait_ge(stage_hi, 8 * b + s + 1)
                    at = (slice(None), s // 2, slice(2 * (s % 2), 2 * (s % 2) + 2))
                    dve.tensor_tensor(ctx_lo[at], stage[:, s % 2], ctx_hi[at], ALU.subtract).then_inc(stage_lo, 1)

                def split_k(b, g, kb):
                    dve.wait_ge(proj_act, use_k(b, g, kb) + 1)
                    dve.scalar_tensor_tensor(k_lo[:, 512 * kb:512 * kb + 512], proj[bank(USES.index(("k", g, kb)))][:, :], 1.0 / WSCALE,
                                             k_hi[:, 512 * kb:512 * kb + 512], ALU.mult, ALU.subtract).then_inc(k_low, 1)

                def normalise(b):
                    if not (isinstance(b, int) and b == 0):
                        dve.wait_ge(xt_ready, b)
                    dve.tensor_scalar(xn[:, :], x1[:, bass.ds(b, 1), :].rearrange("p a d -> p (a d)"),
                                      mv[:, bass.ds(b, 1), 0], rs[:, bass.ds(b, 1)],
                                      ALU.subtract, ALU.mult).then_inc(xn_ready, 1)

                def split_xt(b):
                    dve.wait_ge(xt_split_hi, b + 1)
                    dve.tensor_tensor(xt_lo[:, :, :], misc[:, :].rearrange("p (c t) -> p c t", c=EC), xt_hi[:, :, :],
                                      ALU.subtract).then_inc(xt_split_lo, 1)

                def split_q(b):
                    dve.wait_ge(q_split_hi, b + 1)
                    dve.scalar_tensor_tensor(q_lo[:, :, :], misc[:, :].rearrange("p (g t) -> p g t", g=G), 1.0 / WSCALE,
                                             q_hi[:, :, :], ALU.mult, ALU.subtract).then_inc(q_split_lo, 1)

                def maximum(b, g, u):
                    dve.wait_ge(m_ready, 32 * b + UNITS * g + u + 1)
                    dve.reduce_max(mx[:, u // 2, u % 2:u % 2 + 1], sc[u % 2][:, :], AX.X).then_inc(m_read, 1)

                def maxima_to_diag(b, g, steps):
                    dve.wait_ge(m_read, 32 * b + UNITS * g + UNITS)
                    steps.did(dve.tensor_reduce(nm[:, :], mx[:, :, :], AX.X, ALU.max, negate=True))
                    steps.wait()
                    if not (isinstance(b, int) and b == 0 and g == 0):
                        dve.wait_ge(row_ready, 4 * b + g)
                    dve.tensor_tensor(diag[:, :, :], nm[:, :].unsqueeze(2).to_broadcast([P, GH, T]),
                                      ident16[:, :].unsqueeze(1).to_broadcast([P, GH, T]),
                                      ALU.mult).then_inc(diag_ready, 1)

                def add_probs(b, g, part):
                    e = 32 * b + UNITS * g
                    dve.wait_ge(e_ready, e + (2, 5, 6, 8)[part])
                    if part == 0:
                        if not (isinstance(b, int) and b == 0 and g == 0):
                            dve.wait_ge(group_done, 4 * b + g)
                        dve.tensor_tensor(acc_v[:, :], probs[:, 0, :], probs[:, 1, :], ALU.add).then_inc(sum_v, 1)
                    else:
                        dve.wait_ge(sum_v, 16 * b + 4 * g + part)
                        dve.tensor_tensor(acc_v[:, :], acc_v[:, :], probs[:, (0, 0, 1, 3)[part], :],
                                          ALU.add).then_inc(sum_v, 1)

                def finish_group(b, g, steps):
                    dve.wait_ge(group_done, 4 * b + g + 1)
                    steps.did(dve.reciprocal(rden[:, :], po[:, T:2 * T]))
                    steps.wait()
                    if g == 0 and not (isinstance(b, int) and b == 0):
                        dve.wait_ge(o_ready, b)
                    dve.tensor_tensor(ot[:, g, :], po[:, 0:T], rden[:, :], ALU.mult).then_inc(ot_ready, 1)

                split_w(0)
                split_ctx(0, 0)
                split_ctx(0, 1)
                split_w(1)
                split_ctx(0, 2)
                split_ctx(0, 3)
                dve.wait_ge(x_in, 16)
                for b in range(B):
                    steps.did(dve.bn_stats(st[:, b, :], x1[:, b, :]))
                steps.wait()
                for b in range(B):
                    steps.did(dve.bn_aggr(mv[:, b, :], st[:, b, :]))
                steps.wait()
                dve.tensor_scalar(var[:, :], mv[:, :, 1], EPS, None, ALU.add).then_inc(var_ready, 1)
                dve.wait_ge(std_ready, 1)
                rsqrt_from_std(dve, steps, rs, tmp, var)
                LN_STEPS = steps.n
                normalise(0)
                split_w(2)
                for s in range(4, 8):
                    split_ctx(0, s)
                split_xt(0)
                split_q(0)
                PER = 2 * G

                def add_x(b):
                    dve.wait_ge(o_ready, b + 1)
                    x_b = x1[:, bass.ds(b, 1), :].rearrange("p a d -> p (a d)")
                    dve.tensor_tensor(x_b, misc[:, :], x_b, ALU.add).then_inc(x1_ready, 1)

                def body(b, last):
                    first = first_batch(b)
                    steps = Steps(dve, v_step, LN_STEPS if first else LN_STEPS + PER * b - 1)
                    for kb in range(KB):
                        split_k(b, 0, kb)
                        if kb == 1 and not first:
                            finish_group(b - 1, 3, steps)
                    if not last:
                        normalise(b + 1)
                    if not first:
                        add_x(b - 1)
                    for g in range(G):
                        for u in range(UNITS):
                            maximum(b, g, u)
                            if g < 3 and u in (2, 5):
                                split_k(b, g + 1, u // 3)
                            if g == 3 and not last and u % 2 == 0:
                                split_ctx(b + 1, 4 + u // 2)
                            if g and u == 4:
                                finish_group(b, g - 1, steps)
                        maxima_to_diag(b, g, steps)
                        if g < 3:
                            split_k(b, g + 1, 2)
                            split_k(b, g + 1, 3)
                        if g == 2 and not last:
                            split_ctx(b + 1, 0)
                            split_ctx(b + 1, 1)
                        for part in range(4):
                            add_probs(b, g, part)
                            if first:
                                largest_weight(4 * g + part)
                            if not last:
                                if g == 2 and part == 1:
                                    split_xt(b + 1)
                                if g == 2 and part == 3:
                                    split_q(b + 1)
                                if g == 2 and part >= 2:
                                    split_ctx(b + 1, part)
                    assert steps.n == PER - first

                def largest_weight(n):
                    dve.wait_ge(wq_in[n % 2], 16 * (n // 2 + 1))
                    dve.tensor_reduce(wq_max[:, n:n + 1], wq_f[:, n % 2, :], AX.X, ALU.max,
                                      apply_absolute_value=True).then_inc(wq_seen, 1)

                body(0, False)
                weight_steps = Steps(dve, wq_step)
                dve.wait_ge(wq_seen, WPIECES)
                weight_steps.did(dve.reduce_max(wq_part[:, 0:1], wq_max[:, 0:3 * EC], AX.X))
                weight_steps.wait()
                dve.reduce_max(wq_part[:, 1:2], wq_max[:, 3 * EC:WPIECES], AX.X).then_inc(wmax_ready, 1)
                with dve.Fori(1, B - 1) as b:
                    body(b, False)
                dve.wait_ge(wmax_moved, 32)
                weight_steps.did(dve.reduce_max(wscale[:, :], wq_all[:, :, :].rearrange("p q w -> p w q"), AX.X))
                weight_steps.wait()
                weight_steps.did(dve.tensor_scalar(wscale[:, :], wscale[:, :], 1.0 / QMAX, QFLOOR, ALU.mult, ALU.max))
                weight_steps.wait()
                dve.reciprocal(wq_inv[:, :], wscale[:, :]).then_inc(wq_scaled, 1)
                body(B - 1, True)
                finish_group(B - 1, 3, Steps(dve, v_step, LN_STEPS + PER * B - 1))
                add_x(B - 1)

            @block.tensor
            def _(pe):
                pe.wait_ge(rows_set, 1)

                def wait_bank(b, at):
                    pe.wait_ge(proj_act, 8 + 32 * b + at - 1)
                    before = at - 2
                    if before >= 0 or not first_batch(b):
                        kind, g, kb = USES[before]
                        if kind == "k":
                            pe.wait_ge(k_low, 16 * b + 4 * g + kb + 1 - (16 if before < 0 else 0))

                def project_v(b, half, piece):
                    n, c = piece // 2, piece % 2
                    at = USES.index(("v", half, n))
                    out = proj[bank(at)][:, 256 * c:256 * c + 256]
                    if c == 0:
                        if half:
                            wait_bank(b, at)
                        elif not first_batch(b):
                            wait_bank(b - 1, at)
                        elif n >= 2:
                            pe.wait_ge(proj_act, n - 1)
                        if not half and n % 2 == 0:
                            wait_each(pe, (stage_hi, 8 * b + n + 2), (stage_lo, 8 * b + n + 2))
                    kb, at = piece // 4, P * (piece % 4)
                    wv = slice(256 * half, 256 * half + 256)
                    n_mm = 0
                    for x_part, w_part in mm_terms(ctx_hi, ctx_lo, w_hi, w_lo):
                        for e in range(EC):
                            last = pe.matmul(out, x_part[:, kb, e, at:at + P], w_part[:, 2, e, wv],
                                             start=n_mm == 0, stop=n_mm == 3 * EC - 1)
                            n_mm += 1
                    if c == 1:
                        last.then_inc(proj_ready, 1)

                def project_k(b, g, piece):
                    kb, term = piece // 3, piece % 3
                    at = USES.index(("k", g, kb))
                    if term == 0:
                        wait_bank(b, at)
                    w_part, x_part = mm_terms(w_hi, w_lo, ctx_hi, ctx_lo)[term]
                    for e in range(EC):
                        last = pe.matmul(proj[bank(at)][:, :], w_part[:, 1, e, P * g:P * g + P], x_part[:, kb, e, :],
                                         start=term == 0 and e == 0, stop=term == 2 and e == EC - 1)
                    if term == 2:
                        last.then_inc(proj_ready, 1)

                def scores_for_max(b, g, u):
                    w = 32 * b + UNITS * g + u
                    if u == 0:
                        pe.wait_ge(ks_in[g % 2], 192 * (2 * b + g // 2 + 1))
                    if g == 0 and u == 0:
                        pe.wait_ge(qs_in, 192 * (b + 1))
                    if u >= 2:
                        pe.wait_ge(m_read, w - 1)
                    elif not (isinstance(b, int) and b == 0 and g == 0):
                        pe.wait_ge(e_ready, w - 1)
                    j = u // 2
                    for i in range(2):
                        at = 1024 * (u % 2) + 512 * i
                        last = pe.matmul(sc[u % 2][:, 512 * i:512 * i + 512], qs[0:QK, 4 * g + j, :],
                                         ks[0:QK, g % 2, j, at:at + 512], start=True, stop=True)
                    last.then_inc(m_ready, 1)

                def maxima_to_row(b, g, last):
                    pe.wait_ge(diag_ready, 4 * b + g + 1)
                    if g == 3 and not last:
                        pe.wait_ge(q_split_lo, b + 2)
                    elif g:
                        pe.wait_ge(row_set, 4 * b + g)
                    elif first_batch(b):
                        pe.wait_ge(q_split_lo, 1)
                    else:
                        pe.wait_ge(x1_ready, b)
                    pe.matmul(misc[QK:QKM, :], ones16[:, 0:1], diag[:, :, :].rearrange("p j t -> p (j t)"),
                              start=True, stop=True, tile_position=(0, QK)).then_inc(row_ready, 1)

                def scores_transposed(b, g, u):
                    w = 32 * b + UNITS * g + u
                    if u == 0:
                        pe.wait_ge(row_set, 4 * b + g + 1)
                    if u >= 2:
                        pe.wait_ge(e_ready, w - 1)
                    else:
                        pe.wait_ge(m_read, 32 * b + UNITS * g + UNITS - 1 + u)
                    for i in range(2):
                        ck = 2 * u + i
                        for j in range(GH):
                            last = pe.matmul(sc[u % 2][:, 512 * i + P * j:512 * i + P * j + P],
                                             ks[0:QKM, g % 2, j, P * ck:P * ck + P], qs[0:QKM, 4 * g + j, :],
                                             start=True, stop=True)
                    last.then_inc(s_ready, 1)

                def times_v(b, g, u):
                    w = 32 * b + UNITS * g + u
                    pe.wait_ge(e_ready, w + 1)
                    if u == 0:
                        if not (isinstance(b, int) and b == 0 and g == 0):
                            pe.wait_ge(ot_ready, 4 * b + g)
                    if u == 0 and g % 2 == 0:
                        pe.wait_ge(proj_act, use_v(b, g // 2, 7) + 1)
                    for i in range(2):
                        ck = 2 * u + i
                        for j in range(GH):
                            at = (4 * g + j) % 8 * HD
                            last = pe.matmul(po[HD * j:HD * j + HD, 0:T], v_sb[:, g // 2, ck, at:at + HD],
                                             probs[:, u % 4, 512 * i + P * j:512 * i + P * j + P],
                                             start=ck == 0, stop=ck == KC - 1, tile_position=(0, HD * j))
                    last.then_inc(pv_done, 1)

                def denominators(b, g):
                    pe.wait_ge(sum_v, 16 * b + 4 * g + 4)
                    pe.wait_ge(sum_g, 8 * b + 2 * g + 2)
                    parts = [(acc, 512 * i) for acc in (acc_v, acc_g) for i in range(2)]
                    for n, (acc, at) in enumerate(parts):
                        for j in range(GH):
                            last = pe.matmul(po[HD * j:HD * j + HD, T:2 * T], ones[:, 0:HD],
                                             acc[:, at + P * j:at + P * j + P], start=n == 0,
                                             stop=n == len(parts) - 1, tile_position=(0, HD * j))
                    last.then_inc(group_done, 1)

                def transpose_xn(b):
                    pe.wait_ge(xn_ready, b + 1)
                    if not (isinstance(b, int) and b == 0):
                        pe.wait_ge(row_set, 4 * b - 1)
                    for e in range(EC):
                        last = pe.transpose(misc[:, P * e:P * e + P], xn[:, P * e:P * e + P], ident[:, :])
                    last.then_inc(xt_ready, 1)

                def project_q(b):
                    pe.wait_ge(xt_split_lo, b + 1)
                    for g in range(G):
                        n_mm = 0
                        for w_part, x_part in mm_terms(w_hi, w_lo, xt_hi, xt_lo):
                            for e in range(EC):
                                last = pe.matmul(misc[:, P * g:P * g + P], w_part[:, 0, e, P * g:P * g + P],
                                                 x_part[:, e, :], start=n_mm == 0, stop=n_mm == 3 * EC - 1)
                                n_mm += 1
                    last.then_inc(q_ready, 1)

                def project_out(b):
                    pe.wait_ge(ot_ready, 4 * b + 4)
                    pe.wait_ge(row_set, 4 * b + 4)
                    for g in range(G):
                        last = pe.matmul(misc[:, :], ot[:, g, :], wo[:, g, :], start=g == 0, stop=g == G - 1)
                    last.then_inc(o_ready, 1)

                pe.wait_ge(w_lo_ready, 1)
                for piece in range(16):
                    project_v(0, 0, piece)
                transpose_xn(0)
                pe.wait_ge(w_lo_ready, 3)
                project_q(0)
                pe.wait_ge(wo_in, 16)

                def body(b, last):
                    first = first_batch(b)
                    for piece in range(12):
                        project_k(b, 0, piece)
                        if piece == 5 and not first:
                            denominators(b - 1, 3)
                    for piece in range(6):
                        project_v(b, 1, piece)
                    if not first:
                        project_out(b - 1)
                    for g in range(G):
                        for u in range(UNITS):
                            scores_for_max(b, g, u)
                            if g < 3:
                                project_k(b, g + 1, u)
                            elif not last:
                                project_v(b + 1, 0, u)
                            if g and u == 3:
                                denominators(b, g - 1)
                        if g < 3:
                            for piece in range(UNITS, 12):
                                project_k(b, g + 1, piece)
                        elif not last:
                            for piece in (8, 9):
                                project_v(b + 1, 0, piece)
                        maxima_to_row(b, g, last)
                        for u in range(-1, UNITS + 1):
                            if 0 <= u < UNITS:
                                scores_transposed(b, g, u)
                            for half, piece in fill_after(g, u, last):
                                project_v(b if half else b + 1, half, piece)
                            if u > 0:
                                times_v(b, g, u - 1)
                            if g == 2 and u == 2 and not last:
                                transpose_xn(b + 1)
                            if g == 2 and u == 5 and not last:
                                project_q(b + 1)

                body(0, False)
                with pe.Fori(1, B - 1) as b:
                    body(b, False)
                body(B - 1, True)
                denominators(B - 1, 3)
                project_out(B - 1)


def rsqrt_from_std(dve, steps, rs, std, var):
    steps.did(dve.reciprocal(rs[:, :], std[:, :]))
    steps.wait()
    steps.did(dve.tensor_tensor(std[:, :], rs[:, :], rs[:, :], ALU.mult))
    steps.wait()
    steps.did(dve.tensor_tensor(std[:, :], std[:, :], var[:, :], ALU.mult))
    steps.wait()
    steps.did(dve.tensor_scalar(std[:, :], std[:, :], -0.5, 1.5, ALU.mult, ALU.add))
    steps.wait()
    steps.did(dve.tensor_tensor(rs[:, :], rs[:, :], std[:, :], ALU.mult))
    steps.wait()


def constants(nc, ident, ident16, ones, ones16):
    with ExitStack() as c:
        zeroed = c.enter_context(nc.semaphore("zeroed"))
        made = c.enter_context(nc.semaphore("made"))
        with nc.Block() as block:

            @block.gpsimd
            def _(gp):
                gp.memset(ones[:, :], 1.0).then_inc(made, 1)
                gp.memset(ones16[:, :], 1.0).then_inc(made, 1)
                gp.memset(ident[:, :], 0.0).then_inc(zeroed, 1)
                gp.wait_ge(zeroed, 1)
                gp.affine_select(out=ident[:, :], in_=ident[:, :], compare_op=ALU.not_equal, fill=1.0, base=0,
                                 pattern=[[-1, P]], channel_multiplier=1).then_inc(zeroed, 1)
                gp.wait_ge(zeroed, 2)
                gp.tensor_copy(ident16[:, :], ident[:, :]).then_inc(made, 1)
                gp.wait_ge(made, 3)


E_, F = 8, 2048
TOPK = 2
CAP = int(1.25 * B * T * TOPK / E_) + 1
FQ = F // 512
CT = -(-CAP // P)
NST = 4
ORDER = [("a", 0), ("a", 1), ("b", 0), ("a", 2), ("b", 1), ("a", 3), ("b", 2), ("b", 3)]
SLOT = {item: s for s, item in enumerate(ORDER)}
ROWS = [min(P, CAP - P * i) for i in range(CT)]
EARLY = 4
DROPPED = 4096.0


def quarter(w1, w2, e, s):
    kind, q = ORDER[s]
    src = (w1 if kind == "a" else w2)[bass.ds(e, 1), :, :].rearrange("a r n -> (a r) n")
    if kind == "a":
        return src.rearrange("(c p) f -> p c f", p=P)[:, :, 512 * q:512 * q + 512]
    return src[512 * q:512 * q + 512, :].rearrange("(c p) h -> p c h", p=P)


def split_high(act, stage, stage_in, w_hi, stage_hi, e, s):
    act.wait_ge(stage_in[s % NST], 16 * (2 * e + s // NST + 1))
    act.activation(w_hi[:, s], stage[:, s % NST], ACT.Copy, scale=WSCALE).then_inc(stage_hi, 1)


def split_low(dve, stage, w_hi, w_lo, stage_hi, stage_lo, e, s):
    dve.wait_ge(stage_hi, 8 * e + s + 1)
    dve.scalar_tensor_tensor(w_lo[:, s], stage[:, s % NST], WSCALE, w_hi[:, s],
                             ALU.mult, ALU.subtract).then_inc(stage_lo, 1)


def quantised_self_attention(nc, weights_q, wscale, in_b, out_b, w1, w2, stage, stage_in, x1, ident, ident16):
    E3 = 3 * D
    PAIRS = B // 2
    HALF = B // 2
    with ExitStack() as c:
        def sb(name, shape, dt):
            return c.enter_context(nc.sbuf_tensor(name, shape, dt))

        def sem(name):
            return c.enter_context(nc.semaphore(name))

        wi_q = sb("wi_q", [P, 3, EC, D], f16)
        qo_q = sb("qo_q", [P, EC, D], f16)
        bi = sb("bi_sb", [P, E3], f32)
        bo = sb("bo_sb", [P, D], f32)
        xn = sb("xn2", [P, 2, D], f32)
        xt_hi = sb("xt2_hi", [P, 2, EC, T], f16)
        xt_lo = sb("xt2_lo", [P, 2, EC, T], f16)
        big = sb("big", [P, B, E3], f32)
        prod = stage[:, :, :, :].rearrange("p n c f -> p (n c f)").rearrange("p (i k d) -> p i k d", i=2, k=B)
        scores = sb("scores2", [P, B, B, H], f32)
        row = sb("row", [P, B, H], f32)
        q_val, k_val, v_val = (big[:, :, D * i:D * i + D] for i in range(3))
        heads = q_val
        y = k_val
        hq = sb("hq", [P, B, D], f16)
        ht = sb("ht", [P, 2, EC, T], f16)
        st = sb("st2", [P, B, 6], f32)
        mv = sb("mv2", [P, B, 2], f32)
        var = sb("var2", [P, B], f32)
        std = sb("std2", [P, B], f32)
        rs = sb("rs2", [P, B], f32)
        shift = sb("shift", [P, B], f32)
        tile_max = sb("tile_max", [P, 2, B], f32)
        part = sb("part", [P, 2], f32)
        wide = sb("wide", [P, 2, P], f32)
        scale = {n: sb(f"scale_{n}", [P, 1], f32) for n in ("x", "q", "qx", "xq", "h", "how", "y")}
        inv = {n: sb(f"inv_{n}", [P, 1], f32) for n in ("x", "q", "h", "y")}

        px = [c.enter_context(nc.psum_tensor(f"px{i}", [P, E3], f32)) for i in range(2)]
        pt = [c.enter_context(nc.psum_tensor(f"pt{i}", [P, 512], f32)) for i in range(2)]

        wi_in, wo_in, bias_in = sem("wi_in2"), sem("wo_in2"), sem("bias_in2")
        v_step = sem("v_step2")
        wide_ready = sem("wide_ready")
        wide_t = sem("wide_t")
        var_ready, std_ready, rs_ready = sem("var_ready2"), sem("std_ready2"), sem("rs_ready2")
        xn_ready = sem("xn_ready2")
        xt_ready, xt_hi_ready, xt_lo_ready = sem("xt_ready2"), sem("xt_hi_ready2"), sem("xt_lo_ready2")
        x_ready, x_read = sem("x_ready2"), sem("x_read2")
        x_scaled = sem("x_scaled")
        q_step, q_ready = sem("q_step"), sem("q_ready2")
        v_int_step, v_ready = sem("v_int_step"), sem("v_ready2")
        prod_ready = sem("prod_ready")
        prod_summed = sem("prod_summed")
        sum_read = sem("sum_read")
        diff_ready, exp_ready = sem("diff_ready2"), sem("exp_ready2")
        h_scaled, h_round = sem("h_scaled"), sem("h_round")
        hq_ready, ht_ready, ht_read, y_ready, y_read = (sem(n) for n in ("hq_ready", "ht_ready", "ht_read", "y_ready", "y_read"))
        y_scaled, y_step, y_int = sem("y_scaled"), sem("y_step"), sem("y_int")

        def sums_wait(eng, n):
            if not (isinstance(n, int) and n < 2):
                eng.wait_ge(sum_read, n - 1)

        with nc.Block() as block:

            @block.sync
            def _(sp):
                sp.dma_start(wi_q[:, :, :, :], weights_q[:, 0:3, :, :]).then_inc(wi_in, 16)
                sp.dma_start(bi[:, :], in_b.rearrange("(a d) -> a d", a=1).to_broadcast([P, E3])).then_inc(bias_in, 16)
                sp.dma_start(qo_q[:, :, :], weights_q[:, 3, :, :]).then_inc(wo_in, 16)
                sp.dma_start(bo[:, :], out_b.rearrange("(a d) -> a d", a=1).to_broadcast([P, D])).then_inc(bias_in, 16)
                sp.wait_ge(prod_summed, 2 * B)
                for s in range(NST):
                    sp.dma_start(stage[:, s], quarter(w1, w2, 0, s)).then_inc(stage_in[s], 16)

            @block.gpsimd
            def _(gp):
                gp.wait_ge(rs_ready, 1)
                for t in range(B):
                    if t >= 2:
                        gp.wait_ge(xt_ready, t - 1)
                    gp.tensor_scalar(xn[:, t % 2, :], x1[:, t, :], rs[:, t:t + 1], shift[:, t:t + 1],
                                     ALU.mult, ALU.add).then_inc(xn_ready, 1)

                gp.wait_ge(x_scaled, 1)

                def quantise_q(t):
                    q_t = q_val[:, t, :]
                    gp.tensor_scalar(q_t, q_t, inv["x"][:, :], ROUND, ALU.mult, ALU.add).then_inc(q_step, 1)
                    gp.wait_ge(q_step, 3 * t + 1)
                    gp.tensor_scalar(q_t, q_t, -ROUND, scale["xq"][:, :], ALU.add, ALU.mult).then_inc(q_step, 1)
                    gp.wait_ge(q_step, 3 * t + 2)
                    gp.tensor_scalar(q_t, q_t, 1.0, ROUND, ALU.mult, ALU.add).then_inc(q_step, 1)
                    gp.wait_ge(q_step, 3 * t + 3)
                    gp.tensor_scalar(q_t, q_t, -ROUND, 1.0, ALU.add, ALU.mult).then_inc(q_ready, 1)

                for t in range(B):
                    quantise_q(t)
                for t in range(B):
                    gp.tensor_scalar(v_val[:, t, :], v_val[:, t, :], inv["x"][:, :], ROUND, ALU.mult, ALU.add).then_inc(v_int_step, 1)
                for t in range(B):
                    gp.wait_ge(v_int_step, t + 1)
                    gp.tensor_scalar(v_val[:, t, :], v_val[:, t, :], -ROUND, 1.0, ALU.add, ALU.mult).then_inc(v_ready, 1)

                gp.wait_ge(h_scaled, 1)
                for t in range(B):
                    gp.tensor_scalar(heads[:, t, :], heads[:, t, :], inv["h"][:, :], ROUND, ALU.mult, ALU.add).then_inc(h_round, 1)
                gp.wait_ge(y_scaled, 1)
                for t in range(HALF, B):
                    gp.tensor_scalar(y[:, t, :], y[:, t, :], inv["y"][:, :], ROUND, ALU.mult, ALU.add).then_inc(y_step, 1)
                for t in range(HALF, B):
                    gp.wait_ge(y_step, t - HALF + 1)
                    gp.tensor_scalar(y[:, t, :], y[:, t, :], -ROUND, 1.0, ALU.add, ALU.mult).then_inc(y_int, 1)

            @block.scalar
            def _(act):
                act.wait_ge(var_ready, 1)
                act.activation(std[:, :], var[:, :], ACT.Sqrt).then_inc(std_ready, 1)
                for t in range(B):
                    act.wait_ge(xt_ready, t + 1)
                    if t >= 2:
                        act.wait_ge(x_ready, t - 1)
                    act.activation(xt_hi[:, t % 2], pt[t % 2][:, :].rearrange("p (c t) -> p c t", c=EC),
                                   ACT.Copy).then_inc(xt_hi_ready, 1)

                def read_scores(pair):
                    for i in range(2):
                        q = 2 * pair + i
                        act.wait_ge(prod_summed, q + 1)
                        act.activation(scores[:, bass.ds(q, 1), :, :].rearrange("p a k h -> p (a k h)"),
                                       px[i][:, 0:B * H], ACT.Copy).then_inc(sum_read, 1)

                def exp(half):
                    act.wait_ge(diff_ready, half + 1)
                    s_half = scores[:, HALF * half:HALF * half + HALF]
                    act.activation(s_half, s_half, ACT.Exp, scale=scale["qx"][:, :]).then_inc(exp_ready, 1)

                with act.Fori(0, PAIRS - 1) as pair:
                    read_scores(pair)
                exp(0)
                read_scores(PAIRS - 1)
                exp(1)

                def read_heads(pair):
                    for i in range(2):
                        q = 2 * pair + i
                        act.wait_ge(prod_summed, B + q + 1)
                        act.activation(heads[:, bass.ds(q, 1), :].rearrange("p a d -> p (a d)"),
                                       px[i][:, 0:D], ACT.Copy, scale=scale["x"][:, :]).then_inc(sum_read, 1)

                with act.Fori(0, PAIRS) as pair:
                    read_heads(pair)
                for t in range(B):
                    act.wait_ge(ht_ready, t + 1)
                    if t >= 2:
                        act.wait_ge(y_ready, t - 1)
                    act.activation(ht[:, t % 2], pt[t % 2][:, :].bitcast(f16)[:, 0:EC * T].rearrange("p (c t) -> p c t", c=EC),
                                   ACT.Copy).then_inc(ht_read, 1)

            @block.vector
            def _(dve):
                steps = Steps(dve, v_step)
                rounds = [0]

                def do(instruction):
                    steps.did(instruction)
                    steps.wait()

                def across_partitions(n):
                    dve.tensor_copy(wide[:, 0:n, :], part[:, 0:n].unsqueeze(2).to_broadcast([P, n, P])).then_inc(wide_ready, 1)
                    rounds[0] += 1
                    dve.wait_ge(wide_t, rounds[0])
                    do(dve.tensor_reduce(part[:, 0:n], pt[0][:, 0:P * n].rearrange("p (n q) -> p n q", n=n), AX.X, ALU.max))

                def scale_from_max(name, largest):
                    do(dve.tensor_scalar(scale[name][:, :], largest, 1.0 / QMAX, QFLOOR, ALU.mult, ALU.max))
                    do(dve.reciprocal(inv[name][:, :], scale[name][:, :]))

                def absmax(out, in_):
                    steps.did(dve.tensor_reduce(out, in_, AX.X, ALU.max, apply_absolute_value=True))

                for t in range(B):
                    steps.did(dve.bn_stats(st[:, t, :], x1[:, t, :]))
                steps.wait()
                for t in range(B):
                    steps.did(dve.bn_aggr(mv[:, t, :], st[:, t, :]))
                steps.wait()
                dve.tensor_scalar(var[:, :], mv[:, :, 1], EPS, None, ALU.add).then_inc(var_ready, 1)
                dve.wait_ge(std_ready, 1)
                rsqrt_from_std(dve, steps, rs, std, var)
                dve.scalar_tensor_tensor(shift[:, :], mv[:, :, 0], -1.0, rs[:, :], ALU.mult, ALU.mult).then_inc(rs_ready, 1)

                dve.wait_ge(bias_in, 32)
                for t in range(B):
                    dve.wait_ge(xt_hi_ready, t + 1)
                    dve.tensor_tensor(xt_lo[:, t % 2], pt[t % 2][:, :].rearrange("p (c t) -> p c t", c=EC),
                                      xt_hi[:, t % 2], ALU.subtract).then_inc(xt_lo_ready, 1)
                    if t:
                        dve.wait_ge(x_ready, t)
                        read_x = t - 1
                        dve.scalar_tensor_tensor(big[:, read_x, :], px[read_x % 2][:, :], wscale[:, 0:1], bi[:, :],
                                                 ALU.mult, ALU.add).then_inc(x_read, 1)
                        dve.wait_ge(x_read, t)
                        absmax(tile_max[:, 0, read_x:t], big[:, read_x, 0:D])
                        absmax(tile_max[:, 1, read_x:t], big[:, read_x, D:E3])
                dve.wait_ge(x_ready, B)
                dve.scalar_tensor_tensor(big[:, B - 1, :], px[(B - 1) % 2][:, :], wscale[:, 0:1], bi[:, :],
                                         ALU.mult, ALU.add).then_inc(x_read, 1)
                dve.wait_ge(x_read, B)
                absmax(tile_max[:, 0, B - 1:B], big[:, B - 1, 0:D])
                absmax(tile_max[:, 1, B - 1:B], big[:, B - 1, D:E3])
                steps.wait()
                do(dve.tensor_reduce(part[:, :], tile_max[:, :, :], AX.X, ALU.max))
                across_partitions(2)
                do(dve.tensor_tensor(part[:, 1:2], part[:, 0:1], part[:, 1:2], ALU.max))
                scale_from_max("x", part[:, 1:2])
                do(dve.tensor_scalar(part[:, 0:1], part[:, 0:1], inv["x"][:, :], ROUND, ALU.mult, ALU.add))
                do(dve.tensor_scalar(part[:, 0:1], part[:, 0:1], -ROUND, scale["x"][:, :], ALU.add, ALU.mult))
                do(dve.tensor_scalar(part[:, 0:1], part[:, 0:1], 1.0 / sqrt(HD), None, ALU.mult))
                scale_from_max("q", part[:, 0:1])
                do(dve.tensor_scalar(scale["xq"][:, :], scale["x"][:, :], 1.0 / sqrt(HD), inv["q"][:, :], ALU.mult, ALU.mult))
                dve.tensor_tensor(scale["qx"][:, :], scale["q"][:, :], scale["x"][:, :], ALU.mult).then_inc(x_scaled, 1)

                do(dve.tensor_scalar(k_val, k_val, inv["x"][:, :], ROUND, ALU.mult, ALU.add))
                do(dve.tensor_scalar(k_val, k_val, -ROUND, QMAX, ALU.add, ALU.min))

                def times_keys(pair):
                    for i in range(2):
                        q = 2 * pair + i
                        dve.wait_ge(q_ready, q + 1)
                        if not (isinstance(pair, int) and pair == 0):
                            dve.wait_ge(prod_summed, q - 1)
                        dve.tensor_tensor(prod[:, i], k_val, q_val[:, bass.ds(q, 1), :].to_broadcast([P, B, D]),
                                          ALU.mult).then_inc(prod_ready, 1)

                times_keys(0)
                with dve.Fori(1, PAIRS) as pair:
                    times_keys(pair)

                def softmax(half):
                    dve.wait_ge(sum_read, HALF * (half + 1))
                    s_q = scores[:, HALF * half:HALF * half + HALF]
                    s_h = s_q.rearrange("p q k h -> p q h k")
                    r = row[:, HALF * half:HALF * half + HALF, :]
                    r_q = r.unsqueeze(2).to_broadcast([P, HALF, B, H])
                    do(dve.tensor_reduce(r, s_h, AX.X, ALU.max))
                    dve.tensor_tensor(s_q, s_q, r_q, ALU.subtract).then_inc(diff_ready, 1)
                    dve.wait_ge(exp_ready, half + 1)
                    do(dve.tensor_reduce(r, s_h, AX.X, ALU.add))
                    do(dve.reciprocal(r, r))
                    do(dve.tensor_tensor(s_q, s_q, r_q, ALU.mult))

                def largest_head(q):
                    dve.wait_ge(sum_read, B + q + 1)
                    dve.tensor_reduce(tile_max[:, 0, bass.ds(q, 1)], heads[:, bass.ds(q, 1), :], AX.XY, ALU.max,
                                      apply_absolute_value=True).then_inc(v_step, 1)

                def times_values(pair):
                    for i in range(2):
                        q = 2 * pair + i
                        dve.wait_ge(prod_summed, B + q - 1)
                        p_q = scores[:, bass.ds(q, 1), :, :].rearrange("p a k h -> p (a k) h").unsqueeze(3)
                        dve.tensor_tensor(prod[:, i].rearrange("p k (h d) -> p k h d", h=H),
                                          v_val.rearrange("p k (h d) -> p k h d", h=H),
                                          p_q.to_broadcast([P, B, H, HD]), ALU.mult).then_inc(prod_ready, 1)
                        if not (isinstance(pair, int) and pair == 0):
                            largest_head(q - 2)

                softmax(0)
                dve.wait_ge(v_ready, B)
                times_values(0)
                softmax(1)
                with dve.Fori(1, PAIRS) as pair:
                    times_values(pair)
                for q in (B - 2, B - 1):
                    largest_head(q)
                steps.n += B
                steps.wait()

                do(dve.tensor_reduce(part[:, 0:1], tile_max[:, 0, :], AX.X, ALU.max))
                across_partitions(1)
                do(dve.tensor_scalar(scale["h"][:, :], part[:, 0:1], 1.0 / QMAX, QFLOOR, ALU.mult, ALU.max))
                dve.reciprocal(inv["h"][:, :], scale["h"][:, :]).then_inc(h_scaled, 1)
                do(dve.tensor_tensor(scale["how"][:, :], scale["h"][:, :], wscale[:, 1:2], ALU.mult))

                def integers_of_heads(t):
                    dve.wait_ge(h_round, t + 1)
                    dve.tensor_scalar(hq[:, t, :], heads[:, t, :], -ROUND, QMAX, ALU.add, ALU.min).then_inc(hq_ready, 1)

                integers_of_heads(0)
                integers_of_heads(1)
                for t in range(B):
                    if t + 2 < B:
                        integers_of_heads(t + 2)
                    dve.wait_ge(y_ready, t + 1)
                    dve.scalar_tensor_tensor(y[:, t, :], px[t % 2][:, 0:D], scale["how"][:, :], bo[:, :],
                                             ALU.mult, ALU.add).then_inc(y_read, 1)
                    dve.wait_ge(y_read, t + 1)
                    absmax(tile_max[:, 0, t:t + 1], y[:, t, :])
                steps.wait()
                do(dve.tensor_reduce(part[:, 0:1], tile_max[:, 0, :], AX.X, ALU.max))
                across_partitions(1)
                do(dve.tensor_scalar(scale["y"][:, :], part[:, 0:1], 1.0 / QMAX, QFLOOR, ALU.mult, ALU.max))
                dve.reciprocal(inv["y"][:, :], scale["y"][:, :]).then_inc(y_scaled, 1)
                dve.wait_ge(y_scaled, 1)
                first, second = y[:, 0:HALF, :], y[:, HALF:B, :]
                do(dve.tensor_scalar(first, first, inv["y"][:, :], ROUND, ALU.mult, ALU.add))
                do(dve.tensor_scalar(first, first, -ROUND, QMAX, ALU.add, ALU.min))
                dve.scalar_tensor_tensor(x1[:, 0:HALF, :], first, scale["y"][:, :], x1[:, 0:HALF, :], ALU.mult, ALU.add)
                dve.wait_ge(y_int, B - HALF)
                dve.scalar_tensor_tensor(x1[:, HALF:B, :], second, scale["y"][:, :], x1[:, HALF:B, :], ALU.mult, ALU.add)

            @block.tensor
            def _(pe):
                rounds = [0]

                def transpose_wide(n):
                    rounds[0] += 1
                    pe.wait_ge(wide_ready, rounds[0])
                    for i in range(n):
                        last = pe.transpose(pt[0][:, P * i:P * i + P], wide[:, i, :], ident[:, :])
                    last.then_inc(wide_t, 1)

                def transpose_xn(t):
                    pe.wait_ge(xn_ready, t + 1)
                    if t >= 2:
                        pe.wait_ge(xt_lo_ready, t - 1)
                    for e in range(EC):
                        last = pe.transpose(pt[t % 2][:, P * e:P * e + P], xn[:, t % 2, P * e:P * e + P], ident[:, :])
                    last.then_inc(xt_ready, 1)

                transpose_xn(0)
                pe.wait_ge(wi_in, 16)
                for t in range(B):
                    if t + 1 < B:
                        transpose_xn(t + 1)
                    pe.wait_ge(xt_lo_ready, t + 1)
                    if t >= 2:
                        pe.wait_ge(x_read, t - 1)
                    for n in range(3):
                        n_mm = 0
                        for x_part in (xt_hi, xt_lo):
                            for e in range(EC):
                                last = pe.matmul(px[t % 2][:, D * n:D * n + D], x_part[:, t % 2, e, :],
                                                 wi_q[:, n, e, :], start=n_mm == 0, stop=n_mm == 2 * EC - 1)
                                n_mm += 1
                    last.then_inc(x_ready, 1)
                transpose_wide(2)

                def add_over_dims(pair):
                    for i in range(2):
                        q = 2 * pair + i
                        pe.wait_ge(prod_ready, q + 1)
                        if not (isinstance(pair, int) and pair == 0):
                            pe.wait_ge(sum_read, q - 1)
                        by_dim = prod[:, i].rearrange("p k (h d) -> p d k h", h=H)
                        for d in range(HD):
                            last = pe.matmul(px[i][:, 0:B * H].rearrange("p (k h) -> p k h", k=B), ident[:, :], by_dim[:, d],
                                             start=d == 0, stop=d == HD - 1)
                        last.then_inc(prod_summed, 1)

                add_over_dims(0)
                with pe.Fori(1, PAIRS) as pair:
                    add_over_dims(pair)

                def add_over_keys(pair):
                    for i in range(2):
                        q = 2 * pair + i
                        pe.wait_ge(prod_ready, B + q + 1)
                        pe.wait_ge(sum_read, B + q - 1)
                        for k in range(B):
                            last = pe.matmul(px[i][:, 0:D], ident[:, :], prod[:, i, k, :], start=k == 0, stop=k == B - 1)
                        last.then_inc(prod_summed, 1)

                with pe.Fori(0, PAIRS) as pair:
                    add_over_keys(pair)
                transpose_wide(1)

                def transpose_heads(t):
                    pe.wait_ge(hq_ready, t + 1)
                    if t >= 2:
                        pe.wait_ge(ht_read, t - 1)
                    for e in range(EC):
                        last = pe.transpose(pt[t % 2][:, :].bitcast(f16)[:, P * e:P * e + P], hq[:, t, P * e:P * e + P], ident16[:, :])
                    last.then_inc(ht_ready, 1)

                transpose_heads(0)
                pe.wait_ge(wo_in, 16)
                for t in range(B):
                    if t + 1 < B:
                        transpose_heads(t + 1)
                    pe.wait_ge(ht_read, t + 1)
                    if t >= 2:
                        pe.wait_ge(y_read, t - 1)
                    for e in range(EC):
                        last = pe.matmul(px[t % 2][:, 0:D], ht[:, t % 2, e, :], qo_q[:, e, :], start=e == 0, stop=e == EC - 1)
                    last.then_inc(y_ready, 1)
                transpose_wide(1)


def route(nc, rwT, w1, w2, stage, w_hi, w_lo, stage_in, stage_hi, stage_lo, x1, slot_i, gates, xbuf, ident):
    with ExitStack() as c:
        def sb(name, shape, dt):
            return c.enter_context(nc.sbuf_tensor(name, shape, dt))

        def sem(name):
            return c.enter_context(nc.semaphore(name))

        rw = sb("rw", [P, EC, E_], f32)
        xn3 = sb("xn3", [P, B, D], f32)
        zeros = sb("zeros", [P, D], f32)
        xt = sb("xt3", [P, 2, EC, T], f32)
        st = sb("st3", [P, B, 6], f32)
        mv = sb("mv3", [P, B, 2], f32)
        var = sb("var3", [P, B], f32)
        std = sb("std3", [P, B], f32)
        rs = sb("rs3", [P, B], f32)
        upper = sb("upper", [P, P], f16)
        ones_sq = sb("ones_sq", [P, P], f16)
        expert_i = sb("expert_i", [P, E_], i32)
        expert_f = sb("expert_f", [P, E_], f32)
        logits = sb("logits", [P, B, E_], f32)
        top = sb("top", [P, B, 8], f32)
        top_i = sb("top_i", [P, B, 8], u32)
        chosen = sb("chosen", [P, TOPK, B], f32)
        hot = sb("hot", [P, TOPK, B, E_], f32)
        both = sb("both", [P, B, E_], f16)
        before = sb("before", [P, B, E_], f16)
        rank_e = sb("rank_e", [P, B, E_], f32)
        masked = sb("masked", [P, TOPK, B, E_], f32)
        rank = sb("rank", [P, TOPK, B], f32)
        keep = sb("keep", [P, TOPK, B], f32)
        slot = sb("slot", [P, TOPK, B], f32)
        send = sb("send", [P, TOPK, B], f32)
        send_i = sb("send_i", [P, TOPK, B], i32)
        gap = sb("gap", [P, B], f32)
        e2 = sb("e2", [P, B], f32)

        pt = [c.enter_context(nc.psum_tensor(f"pt3_{i}", [P, 512], f32)) for i in range(2)]
        pl = c.enter_context(nc.psum_tensor("pl", [P, B * E_], f32))
        pr = c.enter_context(nc.psum_tensor("pr", [P, B * E_], f32))

        rw_in, zeroed, filled = sem("rw_in"), sem("zeroed3"), sem("filled")
        made = sem("made3")
        v_step = sem("v_step3")
        var_ready, std_ready = sem("var_ready3"), sem("std_ready3")
        xn_ready, xt_ready, xt_read, logit_ready = (sem(n) for n in ("xn_ready3", "xt_ready3", "xt_read3", "logit_ready"))
        before_ready = sem("before_ready")
        both_ready, rank_ready, gap_ready, exp_ready, send_ready, sent = (
            sem(n) for n in ("both_ready", "rank_ready", "gap_ready", "exp_ready3", "send_ready", "sent"))

        with nc.Block() as block:

            @block.sync
            def _(sp):
                sp.dma_start(rw[:, :, :], rwT.rearrange("(c p) e -> p c e", p=P)).then_inc(rw_in, 16)
                sp.wait_ge(zeroed, 1)
                rows = E_ * CAP
                for r in range(0, rows, P):
                    n = min(P, rows - r)
                    sp.dma_start(xbuf[r:r + n, :], zeros[0:n, :]).then_inc(filled, 16)
                for s in range(NST, NST + EARLY):
                    sp.wait_ge(stage_hi, s - NST + 1)
                    sp.wait_ge(stage_lo, s - NST + 1)
                    sp.dma_start(stage[:, s % NST], quarter(w1, w2, 0, s)).then_inc(stage_in[s % NST], 16)

            @block.gpsimd
            def _(gp):
                gp.memset(zeros[:, :], 0.0).then_inc(zeroed, 1)
                gp.memset(ones_sq[:, :], 1.0).then_inc(made, 1)
                gp.iota(expert_i[:, :], [[1, E_]], base=0, channel_multiplier=0).then_inc(made, 1)
                gp.wait_ge(made, 2)
                gp.affine_select(out=upper[:, :], in_=ones_sq[:, :], compare_op=ALU.is_gt, fill=0.0, base=0,
                                 pattern=[[1, P]], channel_multiplier=-1).then_inc(made, 1)
                gp.wait_ge(send_ready, 1)
                gp.wait_ge(filled, 16 * (-(-E_ * CAP // P)))
                for t in range(B):
                    for k in range(TOPK):
                        gp.indirect_dma_start(xbuf, bass.IndirectOffsetOnAxis(ap=send_i[:, k, t:t + 1], axis=0),
                                              xn3[:, t, :], None, bounds_check=E_ * CAP - 1, oob_is_err=False).then_inc(sent, 16)
                gp.wait_ge(sent, 16 * B * TOPK)

            @block.scalar
            def _(act):
                act.wait_ge(var_ready, 1)
                act.activation(std[:, :], var[:, :], ACT.Sqrt).then_inc(std_ready, 1)
                for t in range(B):
                    act.wait_ge(xt_ready, t + 1)
                    if t >= 2:
                        act.wait_ge(logit_ready, t - 1)
                    act.activation(xt[:, t % 2], pt[t % 2][:, :].rearrange("p (c t) -> p c t", c=EC), ACT.Copy).then_inc(xt_read, 1)
                for s in range(2):
                    split_high(act, stage, stage_in, w_hi, stage_hi, 0, s)
                act.wait_ge(gap_ready, 1)
                act.activation(e2[:, :], gap[:, :], ACT.Exp).then_inc(exp_ready, 1)
                for s in range(2, EARLY):
                    split_high(act, stage, stage_in, w_hi, stage_hi, 0, s)

            @block.vector
            def _(dve):
                steps = Steps(dve, v_step)

                def do(instruction):
                    steps.did(instruction)
                    steps.wait()

                for t in range(B):
                    steps.did(dve.bn_stats(st[:, t, :], x1[:, t, :]))
                steps.wait()
                for t in range(B):
                    steps.did(dve.bn_aggr(mv[:, t, :], st[:, t, :]))
                steps.wait()
                dve.tensor_scalar(var[:, :], mv[:, :, 1], EPS, None, ALU.add).then_inc(var_ready, 1)
                dve.wait_ge(std_ready, 1)
                rsqrt_from_std(dve, steps, rs, std, var)
                for t in range(B):
                    dve.tensor_scalar(xn3[:, t, :], x1[:, t, :], mv[:, t, 0:1], rs[:, t:t + 1],
                                      ALU.subtract, ALU.mult).then_inc(xn_ready, 1)
                dve.wait_ge(xn_ready, B)
                do(dve.tensor_tensor(x1[:, :, :], x1[:, :, :], xn3[:, :, :], ALU.add))
                dve.wait_ge(made, 3)
                do(dve.tensor_copy(expert_f[:, :], expert_i[:, :]))
                dve.wait_ge(logit_ready, B)
                do(dve.tensor_copy(logits[:, :, :], pl[:, :].rearrange("p (t e) -> p t e", t=B)))
                for t in range(B):
                    steps.did(dve.max(top[:, t, :], logits[:, t, :]))
                steps.wait()
                for t in range(B):
                    steps.did(dve.max_index(top_i[:, t, :], top[:, t, :], logits[:, t, :]))
                dve.tensor_tensor(gap[:, :], top[:, :, 1], top[:, :, 0], ALU.subtract).then_inc(gap_ready, 1)
                steps.wait()
                do(dve.tensor_copy(chosen[:, :, :].rearrange("p k t -> p t k"), top_i[:, :, 0:TOPK]))
                for k in range(TOPK):
                    steps.did(dve.tensor_tensor(hot[:, k], chosen[:, k, :].unsqueeze(2).to_broadcast([P, B, E_]),
                                                expert_f[:, :].unsqueeze(1).to_broadcast([P, B, E_]), ALU.is_equal))
                steps.wait()
                dve.tensor_tensor(both[:, :, :], hot[:, 0], hot[:, 1], ALU.add).then_inc(both_ready, 1)
                do(dve.memset(before[:, 0, :], 0.0))
                dve.wait_ge(both_ready, 1)
                for t in range(1, B):
                    dve.tensor_tensor(before[:, t, :], before[:, t - 1, :], both[:, t - 1, :], ALU.add).then_inc(before_ready, 1)
                    dve.wait_ge(before_ready, t)
                dve.wait_ge(exp_ready, 1)
                do(dve.tensor_scalar(gates[:, 0, :], e2[:, :], 1.0, None, ALU.add))
                do(dve.reciprocal(gates[:, 0, :], gates[:, 0, :]))
                do(dve.tensor_tensor(gates[:, 1, :], gates[:, 0, :], e2[:, :], ALU.mult))
                dve.wait_ge(rank_ready, 1)
                do(dve.tensor_copy(rank_e[:, :, :], pr[:, :].rearrange("p (t e) -> p t e", t=B)))
                for k in range(TOPK):
                    steps.did(dve.tensor_tensor(masked[:, k], hot[:, k], rank_e[:, :, :], ALU.mult))
                steps.wait()
                do(dve.tensor_reduce(rank[:, :, :], masked[:, :, :, :], AX.X, ALU.add))
                do(dve.tensor_scalar(keep[:, :, :], rank[:, :, :], float(CAP), None, ALU.is_lt))
                do(dve.tensor_scalar(slot[:, :, :], rank[:, :, :], float(CAP - 1), None, ALU.min))
                do(dve.scalar_tensor_tensor(slot[:, :, :], chosen[:, :, :], float(CAP), slot[:, :, :], ALU.mult, ALU.add))
                do(dve.tensor_scalar(send[:, :, :], keep[:, :, :], -DROPPED, DROPPED, ALU.mult, ALU.add))
                do(dve.tensor_tensor(send[:, :, :], send[:, :, :], slot[:, :, :], ALU.add))
                dve.tensor_copy(send_i[:, :, :], send[:, :, :]).then_inc(send_ready, 1)
                dve.tensor_copy(slot_i[:, :, :], slot[:, :, :])
                dve.tensor_tensor(gates[:, :, :], gates[:, :, :], keep[:, :, :], ALU.mult)
                for s in range(EARLY):
                    split_low(dve, stage, w_hi, w_lo, stage_hi, stage_lo, 0, s)

            @block.tensor
            def _(pe):
                pe.wait_ge(rw_in, 16)

                def transpose_xn(t):
                    pe.wait_ge(xn_ready, t + 1)
                    if t >= 2:
                        pe.wait_ge(xt_read, t - 1)
                    for e in range(EC):
                        last = pe.transpose(pt[t % 2][:, P * e:P * e + P], xn3[:, t, P * e:P * e + P], ident[:, :])
                    last.then_inc(xt_ready, 1)

                transpose_xn(0)
                for t in range(B):
                    if t + 1 < B:
                        transpose_xn(t + 1)
                    pe.wait_ge(xt_read, t + 1)
                    for e in range(EC):
                        last = pe.matmul(pl[:, E_ * t:E_ * t + E_], xt[:, t % 2, e, :], rw[:, e, :], start=e == 0, stop=e == EC - 1)
                    last.then_inc(logit_ready, 1)
                pe.wait_ge(both_ready, 1)
                pe.wait_ge(made, 3)
                pe.matmul(pr[:, :], upper[:, :], both[:, :, :].rearrange("p t e -> p (t e)"), start=True, stop=False)
                pe.wait_ge(before_ready, B - 1)
                pe.matmul(pr[:, :], ones_sq[:, :], before[:, :, :].rearrange("p t e -> p (t e)"),
                          start=False, stop=True).then_inc(rank_ready, 1)


def experts(nc, w1, w2, stage, w_hi, w_lo, stage_in, stage_hi, stage_lo, xbuf, obuf, ident):
    with ExitStack() as c:
        def sb(name, shape, dt):
            return c.enter_context(nc.sbuf_tensor(name, shape, dt))

        def sem(name):
            return c.enter_context(nc.semaphore(name))

        xg = sb("xg", [P, CT, D], f32)
        xt_hi = sb("xt3_hi", [P, EC, CAP], f16)
        xt_lo = sb("xt3_lo", [P, EC, CAP], f16)
        hf = sb("hf", [P, 2, CAP], f32)
        h_hi = sb("h_hi", [P, 8, CAP], f16)
        h_lo = sb("h_lo", [P, 8, CAP], f16)
        o_sb = sb("o_sb", [P, CT, D], f32)

        ph = [c.enter_context(nc.psum_tensor(f"ph{i}", [P, 512], f32)) for i in range(2)]
        po = [c.enter_context(nc.psum_tensor(f"po3_{i}", [P, 512], f32)) for i in range(CT)]
        pt = [c.enter_context(nc.psum_tensor(f"ptx{i}", [P, 512], f32)) for i in range(3)]

        xg_in = sem("xg_in")
        xt_ready, xt_hi_ready, xt_lo_ready = sem("xg_t_ready"), sem("xg_hi_ready"), sem("xg_lo_ready")
        a_ready = sem("a_ready")
        a_done = sem("a_done")
        h_step, h_ready = sem("h_step"), sem("h_ready")
        b_done = sem("b_done")
        o_ready, o_stored = sem("o_sb_ready"), sem("o_stored")

        def wait_used(eng, e, s):
            kind, q = ORDER[s]
            if kind == "a":
                eng.wait_ge(a_ready, 16 * (e - 1) + 4 * q + 4)
            else:
                eng.wait_ge(b_done, 4 * (e - 1) + q + 1)

        with nc.Block() as block:

            @block.sync
            def _(sp):
                def load(e, s):
                    if not isinstance(e, int):
                        sp.compute_val(e * (D * F) * 4)
                    wait_each(sp, (stage_hi, 8 * e + s - NST + 1), (stage_lo, 8 * e + s - NST + 1))
                    sp.dma_start(stage[:, s % NST], quarter(w1, w2, e, s)).then_inc(stage_in[s % NST], 16)

                for s in range(NST + EARLY, 8):
                    load(0, s)
                with sp.Fori(1, E_) as e:
                    for s in range(8):
                        load(e, s)

            @block.gpsimd
            def _(gp):
                def load_x(e):
                    for i in range(CT):
                        row = e * CAP + P * i
                        gp.dma_start(xg[0:ROWS[i], i, :], xbuf[bass.ds(row, ROWS[i]), :]).then_inc(xg_in, 16)

                def store(e):
                    gp.wait_ge(o_ready, CT * e + CT)
                    for i in range(CT):
                        row = e * CAP + P * i
                        gp.dma_start(obuf[bass.ds(row, ROWS[i]), :], o_sb[0:ROWS[i], i, :]).then_inc(o_stored, 16)

                load_x(0)

                def body(e):
                    gp.wait_ge(xt_ready, EC * e + EC)
                    load_x(e + 1)
                    store(e)

                body(0)
                with gp.Fori(1, E_ - 1) as e:
                    body(e)
                store(E_ - 1)
                gp.wait_ge(o_stored, 16 * CT * E_)

            @block.scalar
            def _(act):
                def split(e, s):
                    if not (isinstance(e, int) and e == 0):
                        wait_used(act, e, s)
                    split_high(act, stage, stage_in, w_hi, stage_hi, e, s)

                def silu(e, q):
                    for f in range(4):
                        n = 16 * e + 4 * q + f
                        act.wait_ge(a_ready, n + 1)
                        if not (isinstance(e, int) and e == 0 and q == 0 and f < 2):
                            act.wait_ge(h_ready, n - 1)
                        act.activation(hf[:, f % 2, :], ph[f % 2][:, 0:CAP], ACT.Silu, scale=1.0 / WSCALE).then_inc(a_done, 1)

                def split_x(e, chunks):
                    for i in chunks:
                        act.wait_ge(xt_ready, EC * e + i + 1)
                        act.activation(xt_hi[:, i, :], pt[i % 3][:, 0:CAP], ACT.Copy).then_inc(xt_hi_ready, 1)

                split_x(0, range(EC))
                for s in range(EARLY, 7):
                    split(0, s)

                def body(e, last):
                    silu(e, 0)
                    split(e, 7)
                    silu(e, 1)
                    if not last:
                        split(e + 1, 0)
                        split(e + 1, 1)
                    silu(e, 2)
                    if not last:
                        split(e + 1, 2)
                    silu(e, 3)
                    if not last:
                        for s in (3, 4, 5):
                            split(e + 1, s)
                        split_x(e + 1, range(EC))
                        split(e + 1, 6)

                body(0, False)
                with act.Fori(1, E_ - 1) as e:
                    body(e, False)
                body(E_ - 1, True)

            @block.vector
            def _(dve):
                def split(e, s):
                    split_low(dve, stage, w_hi, w_lo, stage_hi, stage_lo, e, s)

                def split_h(e, q):
                    if not (isinstance(e, int) and e == 0 and q < 2):
                        dve.wait_ge(b_done, 4 * e + q - 1)
                    for f in range(4):
                        n = 16 * e + 4 * q + f
                        at = 4 * (q % 2) + f
                        dve.wait_ge(a_done, n + 1)
                        dve.tensor_copy(h_hi[:, at, :], hf[:, f % 2, :]).then_inc(h_step, 1)
                        dve.wait_ge(h_step, n + 1)
                        dve.tensor_tensor(h_lo[:, at, :], hf[:, f % 2, :], h_hi[:, at, :], ALU.subtract).then_inc(h_ready, 1)

                def split_x(e, chunks):
                    for i in chunks:
                        dve.wait_ge(xt_hi_ready, EC * e + i + 1)
                        dve.tensor_tensor(xt_lo[:, i, :], pt[i % 3][:, 0:CAP], xt_hi[:, i, :], ALU.subtract).then_inc(xt_lo_ready, 1)

                def read_out(e):
                    dve.wait_ge(b_done, 4 * e + 4)
                    if not (isinstance(e, int) and e == 0):
                        dve.wait_ge(o_stored, 16 * CT * e)
                    for i in range(CT):
                        dve.tensor_scalar(o_sb[0:ROWS[i], i, :], po[i][0:ROWS[i], :], 1.0 / WSCALE, None, ALU.mult).then_inc(o_ready, 1)

                split_x(0, range(EC))
                for s in range(EARLY, 7):
                    split(0, s)

                def body(e, last):
                    split_h(e, 0)
                    split(e, 7)
                    split_h(e, 1)
                    if not last:
                        split(e + 1, 0)
                        split(e + 1, 1)
                    split_h(e, 2)
                    if not last:
                        split(e + 1, 2)
                    split_h(e, 3)
                    if not last:
                        for s in (3, 4, 5):
                            split(e + 1, s)
                        split_x(e + 1, range(EC))
                        split(e + 1, 6)
                    read_out(e)

                body(0, False)
                with dve.Fori(1, E_ - 1) as e:
                    body(e, False)
                body(E_ - 1, True)

            @block.tensor
            def _(pe):
                def wait_split(e, s):
                    wait_each(pe, (stage_hi, 8 * e + s + 1), (stage_lo, 8 * e + s + 1))

                def transpose_x(e, chunks):
                    for i in chunks:
                        if i == 0:
                            pe.wait_ge(xg_in, 16 * CT * (e + 1))
                            if not (isinstance(e, int) and e == 0):
                                pe.wait_ge(xt_lo_ready, EC * e)
                        if i == 3:
                            pe.wait_ge(xt_lo_ready, EC * e + 1)
                        for j in range(CT):
                            last = pe.transpose(pt[i % 3][:, P * j:P * j + ROWS[j]], xg[0:ROWS[j], j, P * i:P * i + P],
                                                ident[0:ROWS[j], 0:ROWS[j]])
                        last.then_inc(xt_ready, 1)

                def hidden(e, q):
                    wait_split(e, SLOT["a", q])
                    if q == 0:
                        pe.wait_ge(xt_lo_ready, EC * e + EC)
                    s = SLOT["a", q]
                    for f in range(4):
                        n = 16 * e + 4 * q + f
                        if not (isinstance(e, int) and e == 0 and q == 0 and f < 2):
                            pe.wait_ge(a_done, n - 1)
                        n_mm = 0
                        for w_part, x_part in mm_terms(w_hi, w_lo, xt_hi, xt_lo):
                            for i in range(EC):
                                last = pe.matmul(ph[f % 2][:, 0:CAP], w_part[:, s, i, P * f:P * f + P], x_part[:, i, :],
                                                 start=n_mm == 0, stop=n_mm == 3 * EC - 1)
                                n_mm += 1
                        last.then_inc(a_ready, 1)

                def output(e, q, chunks):
                    s = SLOT["b", q]
                    if 0 in chunks:
                        wait_split(e, s)
                        if q == 0 and not (isinstance(e, int) and e == 0):
                            pe.wait_ge(o_ready, CT * e)
                    for f in chunks:
                        pe.wait_ge(h_ready, 16 * e + 4 * q + f + 1)
                        at = 4 * (q % 2) + f
                        for i in range(CT):
                            rows = slice(P * i, P * i + ROWS[i])
                            for n, (h_part, w_part) in enumerate(mm_terms(h_hi, h_lo, w_hi, w_lo)):
                                last = pe.matmul(po[i][0:ROWS[i], :], h_part[:, at, rows], w_part[:, s, f, :],
                                                 start=q == 0 and f == 0 and n == 0, stop=q == FQ - 1 and f == 3 and n == 2)
                    if 3 in chunks:
                        last.then_inc(b_done, 1)

                transpose_x(0, range(EC))

                def body(e, last):
                    hidden(e, 0)
                    hidden(e, 1)
                    output(e, 0, range(4))
                    hidden(e, 2)
                    output(e, 1, range(4))
                    hidden(e, 3)
                    output(e, 2, range(4))
                    if not last:
                        transpose_x(e + 1, range(3))
                    output(e, 3, range(2))
                    if not last:
                        transpose_x(e + 1, range(3, 4))
                    output(e, 3, range(2, 4))

                body(0, False)
                with pe.Fori(1, E_ - 1) as e:
                    body(e, False)
                body(E_ - 1, True)


def combine(nc, x1, slot_i, gates, obuf, out):
    with ExitStack() as c:
        pair = c.enter_context(nc.sbuf_tensor("pair", [P, B, TOPK, D], f32))
        got = [c.enter_context(nc.semaphore(f"got{t}")) for t in range(B)]
        step, summed, stored = (c.enter_context(nc.semaphore(n)) for n in ("step5", "summed", "stored"))
        with nc.Block() as block:

            @block.gpsimd
            def _(gp):
                for t in range(B):
                    for k in range(TOPK):
                        gp.indirect_dma_start(pair[:, t, k, :], None, obuf,
                                              bass.IndirectOffsetOnAxis(ap=slot_i[:, k, t:t + 1], axis=0)).then_inc(got[t], 16)

            @block.vector
            def _(dve):
                for t in range(B):
                    dve.wait_ge(got[t], 16 * TOPK)
                    dve.scalar_tensor_tensor(x1[:, t, :], pair[:, t, 0, :], gates[:, 0, t:t + 1], x1[:, t, :],
                                             ALU.mult, ALU.add).then_inc(step, 1)
                    dve.wait_ge(step, t + 1)
                    dve.scalar_tensor_tensor(x1[:, t, :], pair[:, t, 1, :], gates[:, 1, t:t + 1], x1[:, t, :],
                                             ALU.mult, ALU.add).then_inc(summed, 1)

            @block.sync
            def _(sp):
                for t in range(B):
                    sp.wait_ge(summed, t + 1)
                    sp.dma_start(out[t], x1[:, t, :]).then_inc(stored, 16)
                sp.wait_ge(stored, 16 * B)


def build_block(nc, x, ctxT, wqT, wkT, wvT, woT, wiT, in_b, qoT, out_b, rwT, w1, w2, out):
    xbuf = nc.dram_tensor("xbuf", [E_ * CAP, D], f32).ap()
    obuf = nc.dram_tensor("obuf", [E_ * CAP, D], f32).ap()
    weights_q = nc.dram_tensor("weights_q", [P, 4, EC, 512], f16).ap()
    wmax = nc.dram_tensor("wmax", [P, 2], f32).ap()
    with ExitStack() as c:
        def sb(name, shape, dt):
            return c.enter_context(nc.sbuf_tensor(name, shape, dt))

        x1 = sb("x1", [P, B, D], f32)
        ident = sb("ident", [P, P], f32)
        ident16 = sb("ident16", [P, P], f16)
        ones = sb("ones", [P, HD], f32)
        ones16 = sb("ones16", [P, 1], f16)
        slot_i = sb("slot_i", [P, TOPK, B], i32)
        gates = sb("gates", [P, TOPK, B], f32)
        constants(nc, ident, ident16, ones, ones16)
        wscale = sb("wscale", [P, 2], f32)
        cross_attention(nc, x, ctxT, wqT, wkT, wvT, woT, wiT, qoT, weights_q, wmax, wscale, x1, ident, ident16, ones, ones16)
        stage_in = [c.enter_context(nc.semaphore(f"w_in{i}")) for i in range(NST)]
        stage_hi, stage_lo = (c.enter_context(nc.semaphore(n)) for n in ("w_hi_ready", "w_lo_ready"))
        with nc.sbuf_tensor("stage_w", [P, NST, EC, 512], f32) as stage:
            quantised_self_attention(nc, weights_q, wscale, in_b, out_b, w1, w2, stage, stage_in, x1, ident, ident16)
            with nc.sbuf_tensor("w_hi3", [P, 8, EC, 512], f16) as w_hi, nc.sbuf_tensor("w_lo3", [P, 8, EC, 512], f16) as w_lo:
                split = (stage, w_hi, w_lo, stage_in, stage_hi, stage_lo)
                route(nc, rwT, w1, w2, *split, x1, slot_i, gates, xbuf, ident)
                experts(nc, w1, w2, *split, xbuf, obuf, ident)
        combine(nc, x1, slot_i, gates, obuf, out)


def kernel(x, ctx_1024, L0_xattn_Wq, L0_xattn_Wk, L0_xattn_Wv, L0_xattn_Wo, L0_attn_key, L0_attn_value,
           L0_attn_in_w, L0_attn_in_b, L0_attn_out_w, L0_attn_out_b, L0_ffn_router_w, L0_ffn_w1, L0_ffn_w2):
    import numpy as np
    import concourse.bacc as bacc
    from concourse.bass_utils import run_bass_kernel_spmd

    arrays = {
        "x": x, "ctxT": np.asarray(ctx_1024).transpose(0, 2, 1), "wqT": np.asarray(L0_xattn_Wq).T,
        "wkT": np.asarray(L0_xattn_Wk).T, "wvT": np.asarray(L0_xattn_Wv).T, "woT": np.asarray(L0_xattn_Wo).T,
        "wiT": np.asarray(L0_attn_in_w).T, "in_b": L0_attn_in_b, "qoT": np.asarray(L0_attn_out_w).T,
        "out_b": L0_attn_out_b, "rwT": np.asarray(L0_ffn_router_w).T, "w1": L0_ffn_w1, "w2": L0_ffn_w2,
    }
    arrays = {f"in_{n}": np.ascontiguousarray(a) for n, a in arrays.items()}
    nc = bacc.Bacc("TRN2", target_bir_lowering=False, num_devices=1)
    args = [nc.dram_tensor(n, a.shape, mybir.dt.from_np(a.dtype), kind="ExternalInput").ap() for n, a in arrays.items()]
    args.append(nc.dram_tensor("out_x", (B, T, D), f32, kind="ExternalOutput").ap())
    build_block(nc, *args)
    return run_bass_kernel_spmd(nc, [arrays], core_ids=[0]).results[0]["out_x"]
```

```python
import concourse.bass as bass
from concourse import mybir
from contextlib import ExitStack
from math import sqrt

f32 = mybir.dt.float32
f16 = mybir.dt.float16
i32 = mybir.dt.int32
u32 = mybir.dt.uint32
ALU = mybir.AluOpType
ACT = mybir.ActivationFunctionType
AX = mybir.AxisListType

P = 128
B, T, D = 8, 128, 512
S = 2048
H, HD = 16, 32
EC = D // P
GH = P // HD
G = H // GH
KB = S // 512
KC = S // P
UNITS = 8
WSCALE = 1024.0
EPS = 1e-5
QMAX, QFLOOR = 127.0, 1e-8
ROUND = 1.5 * 2.0 ** 23
QK = 3 * HD
WPIECES = 4 * EC
QKM = QK + 1


def mm_terms(hi_l, lo_l, hi_r, lo_r):
    return ((hi_l, hi_r), (lo_l, hi_r), (hi_l, lo_r))


class Steps:

    def __init__(self, eng, sem, base=0):
        self.eng, self.sem, self.base, self.n = eng, sem, base, 0

    def did(self, instruction):
        instruction.then_inc(self.sem, 1)
        self.n += 1

    def wait(self):
        self.eng.wait_ge(self.sem, self.base + self.n)


def wait_each(eng, *waits):
    for _, value in waits:
        if not isinstance(value, int):
            eng.compute_val(value)
    for sem, value in waits:
        eng.wait_ge(sem, value)


def cross_attention(nc, x, ctxT, wqT, wkT, wvT, woT, wiT, qoT, weights_q, wmax, wscale, x1, x1_stats, ident, ident16, ones, ones16):
    with ExitStack() as c:
        def sb(name, shape, dt):
            return c.enter_context(nc.sbuf_tensor(name, shape, dt))

        def sem(name):
            return c.enter_context(nc.semaphore(name))

        stage = sb("stage", [P, 2, 2, 512], f32)
        ctx_hi = sb("ctx_hi", [P, KB, EC, 512], f16)
        ctx_lo = sb("ctx_lo", [P, KB, EC, 512], f16)
        w_hi = sb("w_hi", [P, 3, EC, D], f16)
        w_lo = sb("w_lo", [P, 3, EC, D], f16)
        wo = sb("wo_sb", [P, EC, D], f32)
        v_sb = sb("v_sb", [P, 2, KC, 256], f32)
        k_hi = sb("k_hi", [P, S], f16)
        k_lo = sb("k_lo", [P, S], f16)
        ks = sb("ks", [P, 2, GH, S], f16)
        q_hi = sb("q_hi", [P, G, T], f16)
        q_lo = sb("q_lo", [P, G, T], f16)
        qs = sb("qs", [P, H, T], f16)
        xn = sb("xn", [P, D], f32)
        xt_hi = sb("xt_hi", [P, EC, T], f16)
        xt_lo = sb("xt_lo", [P, EC, T], f16)
        probs = sb("probs", [P, 4, 1024], f32)
        acc_v = sb("acc_v", [P, 1024], f32)
        acc_g = sb("acc_g", [P, 1024], f32)
        mx = sb("mx", [P, GH, 2], f32)
        nm = sb("nm", [P, GH], f32)
        diag = sb("diag", [P, GH, T], f16)
        rden = sb("rden", [P, T], f32)
        ot = sb("ot", [P, G, T], f32)
        st = sb("st", [P, B, 6], f32)
        mv = sb("mv", [P, B, 2], f32)
        var = sb("var", [P, B], f32)
        rs = sb("rs", [P, B], f32)
        tmp = sb("tmp", [P, B], f32)

        wq_f = sb("wq_f", [P, 2, 512], f32)
        wq_i = sb("wq_i", [P, 2, 512], f16)
        wq_max = sb("wq_max", [P, WPIECES], f32)
        wq_part = sb("wq_part", [P, 2], f32)
        wq_all = sb("wq_all", [P, P, 2], f32)
        wq_inv = sb("wq_inv", [P, 2], f32)

        proj = [c.enter_context(nc.psum_tensor(f"proj{i}", [P, 512], f32)) for i in range(2)]
        sc = [c.enter_context(nc.psum_tensor(f"sc{i}", [P, 1024], f32)) for i in range(2)]
        po = c.enter_context(nc.psum_tensor("po", [P, 512], f32))
        misc = c.enter_context(nc.psum_tensor("misc", [P, 512], f32))

        x_in = sem("x_in")
        wo_in = sem("wo_in")
        w_in = [sem(f"w_in{i}") for i in range(3)]
        w_hi_ready = sem("w_hi_ready")
        w_lo_ready = sem("w_lo_ready")
        stage_in = [sem(f"stage_in{i}") for i in range(2)]
        stage_hi = sem("stage_hi")
        stage_lo = sem("stage_lo")
        rows_set = sem("rows_set")
        var_ready = sem("var_ready")
        std_ready = sem("std_ready")
        xn_ready = sem("xn_ready")
        xt_ready = sem("xt_ready")
        xt_split_hi = sem("xt_split_hi")
        xt_split_lo = sem("xt_split_lo")
        q_ready = sem("q_ready")
        q_split_hi = sem("q_split_hi")
        q_split_lo = sem("q_split_lo")
        qs_in = sem("qs_in")
        first_qs_in = sem("first_qs_in")
        proj_ready = sem("proj_ready")
        proj_act = sem("proj_act")
        k_low = sem("k_low")
        ks_in = [sem(f"ks_in{i}") for i in range(2)]
        m_ready = sem("m_ready")
        m_read = sem("m_read")
        diag_ready = sem("diag_ready")
        row_ready = sem("row_ready")
        row_set = sem("row_set")
        s_ready = sem("s_ready")
        e_ready = sem("e_ready")
        pv_done = sem("pv_done")
        stage_hi_v = sem("stage_hi_v")
        sum_v = sem("sum_v")
        sum_g = sem("sum_g")
        group_done = sem("group_done")
        ot_ready = sem("ot_ready")
        o_ready = sem("o_ready")
        x1_ready = sem("x1_ready")
        v_step = sem("v_step")
        wq_in = [sem(f"wq_in{i}") for i in range(2)]
        wq_seen = sem("wq_seen")
        wq_step = sem("wq_step")
        wmax_ready, wmax_moved = sem("wmax_ready"), sem("wmax_moved")
        wq_scaled = sem("wq_scaled")
        wq_round, wq_int = sem("wq_round"), sem("wq_int")
        wq_out = [sem(f"wq_out{i}") for i in range(2)]

        ctx_v = ctxT.rearrange("b (c p) s -> b p c s", p=P)
        W_ORDER = (2, 1, 0)
        w_stage = [probs[:, 0:2, :], probs[:, 2:4, :], v_sb[:, 1, 0:8, :]]
        w_stage = [w.rearrange("p a n -> p (a n)").rearrange("p (c d) -> p c d", c=EC) for w in w_stage]

        USES = ([("k", 0, i) for i in range(KB)] + [("v", 1, i) for i in (0, 1, 2)]
                + [("k", 1, i) for i in range(KB)] + [("v", 1, 3)]
                + [("k", 2, i) for i in range(KB)] + [("v", 1, i) for i in (4, 5)]
                + [("k", 3, i) for i in range(KB)] + [("v", 1, i) for i in (6, 7)] + [("v", 0, i) for i in range(8)])
        FILL = {0: [(1, i) for i in (6, 7)], 1: [(1, i) for i in range(8, 12)],
                2: [(1, i) for i in range(12, 16)], 3: [(0, i) for i in range(10, 16)]}

        def weight_piece(n):
            third, e = n // EC, n % EC
            src = wiT[:, 512 * third:512 * third + 512] if third < 3 else qoT
            return src[P * e:P * e + P, :]

        def stacked_q():
            return [(qs[row:row + HD, j:H:GH, :], part[HD * j:HD * j + HD, :, :])
                    for row, part in ((0, q_hi), (HD, q_hi), (2 * HD, q_lo)) for j in range(GH)]

        def use_k(b, g, kb):
            return 8 + 32 * b + USES.index(("k", g, kb))

        def use_v(b, half, n):
            at = USES.index(("v", half, n))
            return 8 + 32 * b + at if half else 32 * b + at - 24

        def bank(use_in_body):
            return use_in_body % 2

        DVE_HIGH = (2, 3)

        def high_parts_done(b, s):
            if first_batch(b):
                return stage_hi, s + 1
            if s in DVE_HIGH:
                return stage_hi_v, 2 * (b - 1) + DVE_HIGH.index(s) + 1
            return stage_hi, 8 + 6 * (b - 1) + (s if s > 3 else s + 2) - 1

        def first_batch(b):
            return isinstance(b, int) and b == 0

        def fill_after(g, unit, last):
            pieces = FILL[g] if not (last and g == 3) else []
            thirds = [(half, piece, term) for half, piece in pieces for term in range(3)]
            if unit < 0:
                return thirds[0:3]
            rest = thirds[3:]
            return rest[unit * len(rest) // UNITS:(unit + 1) * len(rest) // UNITS] if unit < UNITS else []

        def wait_k_stacked(eng, b, g):
            if isinstance(b, int) and b == 0 and g == 0:
                return
            n = 2 * b + (g - 1) // 2 + 1 if g else 2 * b
            eng.wait_ge(ks_in[(g - 1) % 2], 192 * n)

        with nc.Block() as block:

            @block.sync
            def _(sp):
                def load_w(i):
                    w = (wqT, wkT, wvT)[W_ORDER[i]].rearrange("(c p) d -> p c d", p=P)
                    sp.dma_start(w_stage[i], w).then_inc(w_in[i], 16)

                def load_ctx(b, s):
                    n = 8 * b + s
                    if not isinstance(b, int):
                        sp.compute_val(b * (D * S) * 4)
                    if not (first_batch(b) and s < 2):
                        wait_each(sp, (stage_lo, n - 1))
                    src = ctx_v[bass.ds(b, 1), :, 2 * (s % 2):2 * (s % 2) + 2, 512 * (s // 2):512 * (s // 2) + 512]
                    sp.dma_start(stage[:, s % 2], src.rearrange("a p c s -> (a p) c s")).then_inc(stage_in[s % 2], 16)

                def stack_q(b):
                    wait_each(sp, (q_split_hi, b + 1), (q_split_lo, b + 1), (s_ready, 32 * b))
                    for to, part in stacked_q():
                        sp.dma_start(to, part).then_inc(qs_in, 16)

                def stack_k(b, g):
                    waits = [(proj_act, use_k(b, g, KB - 1) + 1), (k_low, 16 * b + 4 * g + KB)]
                    if g >= 2 or not first_batch(b):
                        waits.append((s_ready, 8 * (4 * b + g - 1)))
                    wait_each(sp, *waits)
                    for row, part in ((0, k_hi), (HD, k_lo), (2 * HD, k_hi)):
                        for j in range(GH):
                            sp.dma_start(ks[row:row + HD, g % 2, j, :], part[HD * j:HD * j + HD, :]).then_inc(ks_in[g % 2], 16)

                load_w(0)
                load_ctx(0, 0)
                load_ctx(0, 1)
                load_w(1)
                load_ctx(0, 2)
                for s in range(3, 8):
                    load_ctx(0, s)
                sp.dma_start(x1[:, :, :], x.rearrange("b p d -> p b d")).then_inc(x_in, 16)
                load_w(2)
                sp.dma_start(wo[:, :, :], woT.rearrange("(c p) d -> p c d", p=P)).then_inc(wo_in, 16)

                def body(b, last):
                    if not first_batch(b):
                        stack_q(b)
                    stack_k(b, 0)
                    stack_k(b, 1)
                    if not last:
                        load_ctx(b + 1, 0)
                        load_ctx(b + 1, 1)
                    stack_k(b, 2)
                    stack_k(b, 3)
                    if not last:
                        for s in range(2, 8):
                            load_ctx(b + 1, s)

                body(0, False)
                with sp.Fori(1, B - 1) as b:
                    body(b, False)
                body(B - 1, True)

            @block.gpsimd
            def _(gp):
                gp.memset(ks[QK:P, :, :, :], 1.0).then_inc(rows_set, 1)

                def load_weight(n, round_trip):
                    if round_trip == 0 and n >= 2:
                        gp.wait_ge(wq_seen, n - 1)
                    if round_trip == 1 and n < 2:
                        gp.wait_ge(wq_seen, WPIECES)
                    gp.dma_start(wq_f[:, n % 2, :], weight_piece(n)).then_inc(wq_in[n % 2], 16)

                def quantise_weight(n):
                    which = n // (3 * EC)
                    gp.wait_ge(wq_in[n % 2], 16 * (WPIECES // 2 + n // 2 + 1))
                    gp.tensor_scalar(wq_f[:, n % 2, :], wq_f[:, n % 2, :], wq_inv[:, which:which + 1], ROUND,
                                     ALU.mult, ALU.add).then_inc(wq_round, 1)
                    gp.wait_ge(wq_round, n + 1)
                    if n >= 2:
                        gp.wait_ge(wq_out[n % 2], 16 * (n // 2))
                    gp.tensor_scalar(wq_i[:, n % 2, :], wq_f[:, n % 2, :], -ROUND, 1.0, ALU.add, ALU.mult).then_inc(wq_int, 1)
                    gp.wait_ge(wq_int, n + 1)
                    gp.dma_start(weights_q[:, n // EC, n % EC, :], wq_i[:, n % 2, :]).then_inc(wq_out[n % 2], 16)
                    if n + 2 < WPIECES:
                        load_weight(n + 2, 1)

                def body(b, last):
                    for g in range(G):
                        e = 32 * b + UNITS * g
                        if first_batch(b) and g:
                            load_weight(4 * g, 0)
                            load_weight(4 * g + 1, 0)
                        gp.wait_ge(e_ready, e + 4)
                        if not (isinstance(b, int) and b == 0 and g == 0):
                            gp.wait_ge(group_done, 4 * b + g)
                        gp.tensor_tensor(acc_g[:, :], probs[:, 2, :], probs[:, 3, :], ALU.add).then_inc(sum_g, 1)
                        if first_batch(b):
                            load_weight(4 * g + 2, 0)
                        gp.wait_ge(e_ready, e + 7)
                        gp.wait_ge(sum_g, 8 * b + 2 * g + 1)
                        gp.tensor_tensor(acc_g[:, :], acc_g[:, :], probs[:, 2, :], ALU.add).then_inc(sum_g, 1)
                        if first_batch(b):
                            load_weight(4 * g + 3, 0)
                        if last:
                            for n in range(*((0, 6), (6, 11), (11, WPIECES), (WPIECES, WPIECES))[g]):
                                quantise_weight(n)

                gp.wait_ge(x_in, 16)
                load_weight(0, 0)
                load_weight(1, 0)
                gp.wait_ge(q_split_hi, 1)
                gp.wait_ge(q_split_lo, 1)
                for to, part in stacked_q():
                    gp.dma_start(to, part).then_inc(first_qs_in, 16)
                body(0, False)
                gp.wait_ge(wmax_ready, 1)
                gp.dma_start(wmax[:, :], wq_part[:, :]).then_inc(wmax_moved, 16)
                gp.wait_ge(wmax_moved, 16)
                gp.dma_start(wq_all[:, :, :], wmax.rearrange("(a p) w -> a p w", a=1).to_broadcast([P, P, 2])).then_inc(wmax_moved, 16)
                load_weight(0, 1)
                load_weight(1, 1)
                with gp.Fori(1, B - 1) as b:
                    body(b, False)
                gp.wait_ge(wq_scaled, 1)
                body(B - 1, True)
                for i in range(2):
                    gp.wait_ge(wq_out[i], 16 * (WPIECES // 2))

            @block.scalar
            def _(act):
                def split_w(i):
                    act.wait_ge(w_in[i], 16)
                    act.activation(w_hi[:, W_ORDER[i]], w_stage[i], ACT.Copy, scale=WSCALE).then_inc(w_hi_ready, 1)

                def split_ctx(b, s):
                    act.wait_ge(stage_in[s % 2], 16 * (4 * b + s // 2 + 1))
                    if not first_batch(b):
                        used = use_k(b - 1, 3, s // 2) if s < 6 else use_v(b - 1, 1, 7)
                        act.wait_ge(proj_ready, used + 1)
                    act.activation(ctx_hi[:, s // 2, 2 * (s % 2):2 * (s % 2) + 2, :], stage[:, s % 2], ACT.Copy).then_inc(stage_hi, 1)

                def copy_v(b, half, n):
                    act.wait_ge(proj_ready, use_v(b, half, n) + 1)
                    if not first_batch(b):
                        act.wait_ge(pv_done, 32 * b if half else 32 * b - 16)
                    elif n == 0 and half == 1:
                        act.wait_ge(w_lo_ready, 3)
                    act.activation(v_sb[:, half, 2 * n:2 * n + 2, :],
                                   proj[bank(USES.index(("v", half, n)))][:, :].rearrange("p (c d) -> p c d", c=2),
                                   ACT.Copy, scale=1.0 / WSCALE).then_inc(proj_act, 1)

                def split_k(b, g, kb):
                    act.wait_ge(proj_ready, use_k(b, g, kb) + 1)
                    if kb == 0:
                        wait_k_stacked(act, b, g)
                    act.activation(k_hi[:, 512 * kb:512 * kb + 512], proj[bank(USES.index(("k", g, kb)))][:, :], ACT.Copy,
                                   scale=1.0 / WSCALE).then_inc(proj_act, 1)

                def set_row(b, g):
                    act.wait_ge(row_ready, 4 * b + g + 1)
                    act.activation(qs[QK:QKM, 4 * g:4 * g + 4, :],
                                   misc[QK:QKM, :].rearrange("p (j t) -> p j t", j=GH), ACT.Copy).then_inc(row_set, 1)

                def exp(b, g, u):
                    e = 32 * b + UNITS * g + u
                    act.wait_ge(s_ready, e + 1)
                    if not (first_batch(b) and g == 0 and u < 4):
                        act.wait_ge(pv_done, e - 3)
                        k = 4 * g + 16 * b
                        m = 2 * g + 8 * b
                        who, val = {0: (sum_v, k - 2), 1: (sum_v, k - 1), 2: (sum_g, m), 3: (sum_v, k),
                                    4: (sum_v, k + 1), 5: (sum_v, k + 1), 6: (sum_g, m + 1), 7: (sum_g, m + 1)}[u]
                        act.wait_ge(who, val)
                    act.activation(probs[:, u % 4, :], sc[u % 2][:, :], ACT.Exp, scale=1.0 / sqrt(HD)).then_inc(e_ready, 1)

                def split_xt(b):
                    act.wait_ge(xt_ready, b + 1)
                    act.activation(xt_hi[:, :, :], misc[:, :].rearrange("p (c t) -> p c t", c=EC), ACT.Copy).then_inc(xt_split_hi, 1)

                def split_q(b):
                    act.wait_ge(q_ready, b + 1)
                    if isinstance(b, int) and b == 1:
                        act.wait_ge(first_qs_in, 192)
                    elif not first_batch(b):
                        act.wait_ge(qs_in, 192 * (b - 1))
                    act.activation(q_hi[:, :, :], misc[:, :].rearrange("p (g t) -> p g t", g=G), ACT.Copy,
                                   scale=1.0 / WSCALE).then_inc(q_split_hi, 1)

                split_w(0)
                split_ctx(0, 0)
                split_ctx(0, 1)
                split_ctx(0, 2)
                split_ctx(0, 3)
                copy_v(0, 0, 0)
                split_w(1)
                copy_v(0, 0, 1)
                copy_v(0, 0, 2)
                split_ctx(0, 4)
                split_ctx(0, 5)
                copy_v(0, 0, 3)
                split_ctx(0, 6)
                split_ctx(0, 7)
                copy_v(0, 0, 4)
                copy_v(0, 0, 5)
                copy_v(0, 0, 6)
                copy_v(0, 0, 7)
                split_w(2)
                act.wait_ge(var_ready, 1)
                act.activation(tmp[:, :], var[:, :], ACT.Sqrt).then_inc(std_ready, 1)

                def body(b, last):
                    for kb in range(KB):
                        split_k(b, 0, kb)
                        if kb == 1 and first_batch(b):
                            split_xt(0)
                            split_q(0)
                    for n in range(3):
                        copy_v(b, 1, n)
                    for g in range(G):
                        if g < 3:
                            for kb in range(KB):
                                split_k(b, g + 1, kb)
                                if g == 2 and kb == 1 and not last:
                                    split_ctx(b + 1, 0)
                                    split_ctx(b + 1, 1)
                        elif not last:
                            for n in range(5):
                                if n < 4:
                                    split_ctx(b + 1, 4 + n)
                                copy_v(b + 1, 0, n)
                        set_row(b, g)
                        for u in range(-1, UNITS):
                            if u >= 0:
                                exp(b, g, u)
                            for half, piece, term in fill_after(g, u, last):
                                if piece % 2 and term == 2:
                                    copy_v(b if half else b + 1, half, piece // 2)
                            if not last:
                                if g == 2 and u == 3:
                                    split_xt(b + 1)
                                if g == 2 and u == 7:
                                    split_q(b + 1)

                body(0, False)
                with act.Fori(1, B - 1) as b:
                    body(b, False)
                body(B - 1, True)

            @block.vector
            def _(dve):
                steps = Steps(dve, v_step)

                def split_w(i):
                    dve.wait_ge(w_hi_ready, i + 1)
                    dve.scalar_tensor_tensor(w_lo[:, W_ORDER[i]], w_stage[i], WSCALE, w_hi[:, W_ORDER[i]],
                                             ALU.mult, ALU.subtract).then_inc(w_lo_ready, 1)

                def ctx_high(b, s):
                    dve.wait_ge(stage_in[s % 2], 16 * (4 * b + s // 2 + 1))
                    dve.wait_ge(proj_ready, use_k(b - 1, 3, s // 2) + 1)
                    dve.tensor_copy(ctx_hi[:, s // 2, 2 * (s % 2):2 * (s % 2) + 2, :], stage[:, s % 2]).then_inc(stage_hi_v, 1)

                def split_ctx(b, s):
                    if s in DVE_HIGH and not first_batch(b):
                        ctx_high(b, s)
                    dve.wait_ge(*high_parts_done(b, s))
                    at = (slice(None), s // 2, slice(2 * (s % 2), 2 * (s % 2) + 2))
                    dve.tensor_tensor(ctx_lo[at], stage[:, s % 2], ctx_hi[at], ALU.subtract).then_inc(stage_lo, 1)

                def split_k(b, g, kb):
                    dve.wait_ge(proj_act, use_k(b, g, kb) + 1)
                    dve.scalar_tensor_tensor(k_lo[:, 512 * kb:512 * kb + 512], proj[bank(USES.index(("k", g, kb)))][:, :], 1.0 / WSCALE,
                                             k_hi[:, 512 * kb:512 * kb + 512], ALU.mult, ALU.subtract).then_inc(k_low, 1)

                def normalise(b):
                    if not (isinstance(b, int) and b == 0):
                        dve.wait_ge(xt_ready, b)
                    dve.tensor_scalar(xn[:, :], x1[:, bass.ds(b, 1), :].rearrange("p a d -> p (a d)"),
                                      mv[:, bass.ds(b, 1), 0], rs[:, bass.ds(b, 1)],
                                      ALU.subtract, ALU.mult).then_inc(xn_ready, 1)

                def split_xt(b):
                    dve.wait_ge(xt_split_hi, b + 1)
                    dve.tensor_tensor(xt_lo[:, :, :], misc[:, :].rearrange("p (c t) -> p c t", c=EC), xt_hi[:, :, :],
                                      ALU.subtract).then_inc(xt_split_lo, 1)

                def split_q(b):
                    dve.wait_ge(q_split_hi, b + 1)
                    dve.scalar_tensor_tensor(q_lo[:, :, :], misc[:, :].rearrange("p (g t) -> p g t", g=G), 1.0 / WSCALE,
                                             q_hi[:, :, :], ALU.mult, ALU.subtract).then_inc(q_split_lo, 1)

                def maximum(b, g, u):
                    dve.wait_ge(m_ready, 32 * b + UNITS * g + u + 1)
                    dve.reduce_max(mx[:, u // 2, u % 2:u % 2 + 1], sc[u % 2][:, :], AX.X).then_inc(m_read, 1)

                def maxima_to_diag(b, g, steps):
                    dve.wait_ge(m_read, 32 * b + UNITS * g + UNITS)
                    steps.did(dve.tensor_reduce(nm[:, :], mx[:, :, :], AX.X, ALU.max, negate=True))
                    steps.wait()
                    if not (isinstance(b, int) and b == 0 and g == 0):
                        dve.wait_ge(row_ready, 4 * b + g)
                    dve.tensor_tensor(diag[:, :, :], nm[:, :].unsqueeze(2).to_broadcast([P, GH, T]),
                                      ident16[:, :].unsqueeze(1).to_broadcast([P, GH, T]),
                                      ALU.mult).then_inc(diag_ready, 1)

                def add_probs(b, g, part):
                    e = 32 * b + UNITS * g
                    dve.wait_ge(e_ready, e + (2, 5, 6, 8)[part])
                    if part == 0:
                        if not (isinstance(b, int) and b == 0 and g == 0):
                            dve.wait_ge(group_done, 4 * b + g)
                        dve.tensor_tensor(acc_v[:, :], probs[:, 0, :], probs[:, 1, :], ALU.add).then_inc(sum_v, 1)
                    else:
                        dve.wait_ge(sum_v, 16 * b + 4 * g + part)
                        dve.tensor_tensor(acc_v[:, :], acc_v[:, :], probs[:, (0, 0, 1, 3)[part], :],
                                          ALU.add).then_inc(sum_v, 1)

                def finish_group(b, g, steps):
                    dve.wait_ge(group_done, 4 * b + g + 1)
                    steps.did(dve.reciprocal(rden[:, :], po[:, T:2 * T]))
                    steps.wait()
                    if g == 0 and not (isinstance(b, int) and b == 0):
                        dve.wait_ge(o_ready, b)
                    dve.tensor_tensor(ot[:, g, :], po[:, 0:T], rden[:, :], ALU.mult).then_inc(ot_ready, 1)

                split_w(0)
                for s in range(4):
                    split_ctx(0, s)
                split_w(1)
                for s in range(4, 8):
                    split_ctx(0, s)
                dve.wait_ge(x_in, 16)
                for b in range(B):
                    steps.did(dve.bn_stats(st[:, b, :], x1[:, b, :]))
                steps.wait()
                for b in range(B):
                    steps.did(dve.bn_aggr(mv[:, b, :], st[:, b, :]))
                steps.wait()
                dve.tensor_scalar(var[:, :], mv[:, :, 1], EPS, None, ALU.add).then_inc(var_ready, 1)
                split_w(2)
                dve.wait_ge(std_ready, 1)
                rsqrt_from_std(dve, steps, rs, tmp, var)
                LN_STEPS = steps.n
                normalise(0)
                PER = 2 * G

                def add_x(b):
                    dve.wait_ge(o_ready, b + 1)
                    x_b = x1[:, bass.ds(b, 1), :].rearrange("p a d -> p (a d)")
                    dve.tensor_tensor(x_b, misc[:, :], x_b, ALU.add).then_inc(x1_ready, 1)

                def body(b, last):
                    first = first_batch(b)
                    steps = Steps(dve, v_step, LN_STEPS if first else LN_STEPS + PER * b - 1)
                    for kb in range(KB):
                        split_k(b, 0, kb)
                        if kb == 1 and not first:
                            finish_group(b - 1, 3, steps)
                        if kb == 1 and first:
                            split_xt(0)
                            split_q(0)
                    if not last:
                        normalise(b + 1)
                    if not first:
                        add_x(b - 1)
                    for g in range(G):
                        for u in range(UNITS):
                            maximum(b, g, u)
                            if g < 3 and u in (2, 5):
                                split_k(b, g + 1, u // 3)
                            if g == 3 and not last and u % 2 == 0:
                                split_ctx(b + 1, 4 + u // 2)
                            if g and u == 4:
                                finish_group(b, g - 1, steps)
                        maxima_to_diag(b, g, steps)
                        if g < 3:
                            split_k(b, g + 1, 2)
                            split_k(b, g + 1, 3)
                        if g == 2 and not last:
                            split_ctx(b + 1, 0)
                            split_ctx(b + 1, 1)
                        for part in range(4):
                            add_probs(b, g, part)
                            if last and 4 * g + part < B - 1:
                                done = 4 * g + part
                                dve.wait_ge(x1_ready, done + 1)
                                dve.bn_stats(x1_stats[:, done, :], x1[:, done, :])
                            if first and g + part:
                                largest_weight(4 * g + part - 1)
                            if not last:
                                if g == 2 and part == 1:
                                    split_xt(b + 1)
                                if g == 2 and part == 3:
                                    split_q(b + 1)
                                if g == 2 and part >= 2:
                                    split_ctx(b + 1, part)
                    assert steps.n == PER - first

                def largest_weight(n):
                    dve.wait_ge(wq_in[n % 2], 16 * (n // 2 + 1))
                    dve.tensor_reduce(wq_max[:, n:n + 1], wq_f[:, n % 2, :], AX.X, ALU.max,
                                      apply_absolute_value=True).then_inc(wq_seen, 1)

                body(0, False)
                largest_weight(WPIECES - 1)
                weight_steps = Steps(dve, wq_step)
                dve.wait_ge(wq_seen, WPIECES)
                weight_steps.did(dve.reduce_max(wq_part[:, 0:1], wq_max[:, 0:3 * EC], AX.X))
                weight_steps.wait()
                dve.reduce_max(wq_part[:, 1:2], wq_max[:, 3 * EC:WPIECES], AX.X).then_inc(wmax_ready, 1)
                with dve.Fori(1, B - 1) as b:
                    body(b, False)
                dve.wait_ge(wmax_moved, 32)
                weight_steps.did(dve.reduce_max(wscale[:, :], wq_all[:, :, :].rearrange("p q w -> p w q"), AX.X))
                weight_steps.wait()
                weight_steps.did(dve.tensor_scalar(wscale[:, :], wscale[:, :], 1.0 / QMAX, QFLOOR, ALU.mult, ALU.max))
                weight_steps.wait()
                dve.reciprocal(wq_inv[:, :], wscale[:, :]).then_inc(wq_scaled, 1)
                body(B - 1, True)
                finish_group(B - 1, 3, Steps(dve, v_step, LN_STEPS + PER * B - 1))
                add_x(B - 1)

            @block.tensor
            def _(pe):
                def wait_bank(b, at):
                    pe.wait_ge(proj_act, 8 + 32 * b + at - 1)
                    before = at - 2
                    if before >= 0 or not first_batch(b):
                        kind, g, kb = USES[before]
                        if kind == "k":
                            pe.wait_ge(k_low, 16 * b + 4 * g + kb + 1 - (16 if before < 0 else 0))

                def project_v(b, half, piece, terms=range(3)):
                    n, c = piece // 2, piece % 2
                    at = USES.index(("v", half, n))
                    out = proj[bank(at)][:, 256 * c:256 * c + 256]
                    if c == 0 and 0 in terms:
                        if half:
                            wait_bank(b, at)
                        elif not first_batch(b):
                            wait_bank(b - 1, at)
                        elif n >= 2:
                            pe.wait_ge(proj_act, n - 1)
                        if not half and n % 2 == 0:
                            pe.wait_ge(stage_lo, 8 * b + n + 2)
                    kb, at = piece // 4, P * (piece % 4)
                    wv = slice(256 * half, 256 * half + 256)
                    for term in terms:
                        x_part, w_part = mm_terms(ctx_hi, ctx_lo, w_hi, w_lo)[term]
                        for e in range(EC):
                            last = pe.matmul(out, x_part[:, kb, e, at:at + P], w_part[:, 2, e, wv],
                                             start=term == 0 and e == 0, stop=term == 2 and e == EC - 1)
                    if c == 1 and 2 in terms:
                        last.then_inc(proj_ready, 1)

                def project_k(b, g, piece):
                    kb, term = piece // 3, piece % 3
                    at = USES.index(("k", g, kb))
                    if term == 0:
                        wait_bank(b, at)
                    w_part, x_part = mm_terms(w_hi, w_lo, ctx_hi, ctx_lo)[term]
                    for e in range(EC):
                        last = pe.matmul(proj[bank(at)][:, :], w_part[:, 1, e, P * g:P * g + P], x_part[:, kb, e, :],
                                         start=term == 0 and e == 0, stop=term == 2 and e == EC - 1)
                    if term == 2:
                        last.then_inc(proj_ready, 1)

                def scores_for_max(b, g, u):
                    w = 32 * b + UNITS * g + u
                    if u == 0:
                        pe.wait_ge(ks_in[g % 2], 192 * (2 * b + g // 2 + 1))
                    if g == 0 and u == 0:
                        if first_batch(b):
                            pe.wait_ge(first_qs_in, 192)
                        else:
                            pe.wait_ge(qs_in, 192 * b)
                    if u >= 2:
                        pe.wait_ge(m_read, w - 1)
                    elif not (isinstance(b, int) and b == 0 and g == 0):
                        pe.wait_ge(e_ready, w - 1)
                    j = u // 2
                    for i in range(2):
                        at = 1024 * (u % 2) + 512 * i
                        last = pe.matmul(sc[u % 2][:, 512 * i:512 * i + 512], qs[0:QK, 4 * g + j, :],
                                         ks[0:QK, g % 2, j, at:at + 512], start=True, stop=True)
                    last.then_inc(m_ready, 1)

                def maxima_to_row(b, g, last):
                    pe.wait_ge(diag_ready, 4 * b + g + 1)
                    if g == 3 and not last:
                        pe.wait_ge(q_split_lo, b + 2)
                    elif g:
                        pe.wait_ge(row_set, 4 * b + g)
                    elif first_batch(b):
                        pe.wait_ge(q_split_lo, 1)
                    else:
                        pe.wait_ge(x1_ready, b)
                    pe.matmul(misc[QK:QKM, :], ones16[:, 0:1], diag[:, :, :].rearrange("p j t -> p (j t)"),
                              start=True, stop=True, tile_position=(0, QK)).then_inc(row_ready, 1)

                def scores_transposed(b, g, u):
                    w = 32 * b + UNITS * g + u
                    if u == 0:
                        pe.wait_ge(row_set, 4 * b + g + 1)
                    if u >= 2:
                        pe.wait_ge(e_ready, w - 1)
                    else:
                        pe.wait_ge(m_read, 32 * b + UNITS * g + UNITS - 1 + u)
                    for i in range(2):
                        ck = 2 * u + i
                        for j in range(GH):
                            last = pe.matmul(sc[u % 2][:, 512 * i + P * j:512 * i + P * j + P],
                                             ks[0:QKM, g % 2, j, P * ck:P * ck + P], qs[0:QKM, 4 * g + j, :],
                                             start=True, stop=True)
                    last.then_inc(s_ready, 1)

                def times_v(b, g, u):
                    w = 32 * b + UNITS * g + u
                    pe.wait_ge(e_ready, w + 1)
                    if u == 0:
                        if not (isinstance(b, int) and b == 0 and g == 0):
                            pe.wait_ge(ot_ready, 4 * b + g)
                    if g % 2 == 0:
                        pe.wait_ge(proj_act, use_v(b, g // 2, u) + 1)
                    for i in range(2):
                        ck = 2 * u + i
                        for j in range(GH):
                            at = (4 * g + j) % 8 * HD
                            last = pe.matmul(po[HD * j:HD * j + HD, 0:T], v_sb[:, g // 2, ck, at:at + HD],
                                             probs[:, u % 4, 512 * i + P * j:512 * i + P * j + P],
                                             start=ck == 0, stop=ck == KC - 1, tile_position=(0, HD * j))
                    last.then_inc(pv_done, 1)

                def denominators(b, g):
                    pe.wait_ge(sum_v, 16 * b + 4 * g + 4)
                    pe.wait_ge(sum_g, 8 * b + 2 * g + 2)
                    parts = [(acc, 512 * i) for acc in (acc_v, acc_g) for i in range(2)]
                    for n, (acc, at) in enumerate(parts):
                        for j in range(GH):
                            last = pe.matmul(po[HD * j:HD * j + HD, T:2 * T], ones[:, 0:HD],
                                             acc[:, at + P * j:at + P * j + P], start=n == 0,
                                             stop=n == len(parts) - 1, tile_position=(0, HD * j))
                    last.then_inc(group_done, 1)

                def transpose_xn(b):
                    pe.wait_ge(xn_ready, b + 1)
                    if not (isinstance(b, int) and b == 0):
                        pe.wait_ge(row_set, 4 * b - 1)
                    for e in range(EC):
                        last = pe.transpose(misc[:, P * e:P * e + P], xn[:, P * e:P * e + P], ident[:, :])
                    last.then_inc(xt_ready, 1)

                def project_q(b):
                    if first_batch(b):
                        pe.wait_ge(w_lo_ready, 3)
                    pe.wait_ge(xt_split_lo, b + 1)
                    for g in range(G):
                        n_mm = 0
                        for w_part, x_part in mm_terms(w_hi, w_lo, xt_hi, xt_lo):
                            for e in range(EC):
                                last = pe.matmul(misc[:, P * g:P * g + P], w_part[:, 0, e, P * g:P * g + P],
                                                 x_part[:, e, :], start=n_mm == 0, stop=n_mm == 3 * EC - 1)
                                n_mm += 1
                    last.then_inc(q_ready, 1)

                def project_out(b):
                    pe.wait_ge(ot_ready, 4 * b + 4)
                    pe.wait_ge(row_set, 4 * b + 4)
                    for g in range(G):
                        last = pe.matmul(misc[:, :], ot[:, g, :], wo[:, g, :], start=g == 0, stop=g == G - 1)
                    last.then_inc(o_ready, 1)

                pe.wait_ge(w_lo_ready, 1)
                for piece in range(16):
                    project_v(0, 0, piece)
                pe.wait_ge(w_lo_ready, 2)
                pe.wait_ge(rows_set, 1)

                def body(b, last):
                    first = first_batch(b)
                    for piece in range(12):
                        project_k(b, 0, piece)
                        if piece == 5 and not first:
                            denominators(b - 1, 3)
                        if piece == 5 and first:
                            transpose_xn(0)
                        if piece == 8 and first:
                            project_q(0)
                    for piece in range(6):
                        project_v(b, 1, piece)
                    if not first:
                        project_out(b - 1)
                    for g in range(G):
                        for u in range(UNITS):
                            scores_for_max(b, g, u)
                            if g < 3:
                                project_k(b, g + 1, u)
                            elif not last:
                                project_v(b + 1, 0, u)
                            if g and u == 3:
                                denominators(b, g - 1)
                        if g < 3:
                            for piece in range(UNITS, 12):
                                project_k(b, g + 1, piece)
                        elif not last:
                            for piece in (8, 9):
                                project_v(b + 1, 0, piece)
                        maxima_to_row(b, g, last)
                        for u in range(-1, UNITS + 1):
                            if 0 <= u < UNITS:
                                scores_transposed(b, g, u)
                            for half, piece, term in fill_after(g, u, last):
                                project_v(b if half else b + 1, half, piece, (term,))
                            if u > 0:
                                times_v(b, g, u - 1)
                            if g == 2 and u == 2 and not last:
                                transpose_xn(b + 1)
                            if g == 2 and u == 6 and not last:
                                project_q(b + 1)

                body(0, False)
                pe.wait_ge(wo_in, 16)
                with pe.Fori(1, B - 1) as b:
                    body(b, False)
                body(B - 1, True)
                denominators(B - 1, 3)
                project_out(B - 1)


def rsqrt_from_std(dve, steps, rs, std, var):
    steps.did(dve.reciprocal(rs[:, :], std[:, :]))
    steps.wait()
    steps.did(dve.tensor_tensor(std[:, :], rs[:, :], rs[:, :], ALU.mult))
    steps.wait()
    steps.did(dve.tensor_tensor(std[:, :], std[:, :], var[:, :], ALU.mult))
    steps.wait()
    steps.did(dve.tensor_scalar(std[:, :], std[:, :], -0.5, 1.5, ALU.mult, ALU.add))
    steps.wait()
    steps.did(dve.tensor_tensor(rs[:, :], rs[:, :], std[:, :], ALU.mult))
    steps.wait()


def constants(nc, ident, ident16, ones, ones16):
    with ExitStack() as c:
        zeroed = c.enter_context(nc.semaphore("zeroed"))
        made = c.enter_context(nc.semaphore("made"))
        with nc.Block() as block:

            @block.gpsimd
            def _(gp):
                gp.memset(ones[:, :], 1.0).then_inc(made, 1)
                gp.memset(ones16[:, :], 1.0).then_inc(made, 1)
                gp.memset(ident[:, :], 0.0).then_inc(zeroed, 1)
                gp.wait_ge(zeroed, 1)
                gp.affine_select(out=ident[:, :], in_=ident[:, :], compare_op=ALU.not_equal, fill=1.0, base=0,
                                 pattern=[[-1, P]], channel_multiplier=1).then_inc(zeroed, 1)
                gp.wait_ge(zeroed, 2)
                gp.tensor_copy(ident16[:, :], ident[:, :]).then_inc(made, 1)
                gp.wait_ge(made, 3)


E_, F = 8, 2048
TOPK = 2
CAP = int(1.25 * B * T * TOPK / E_) + 1
FQ = F // 512
CT = -(-CAP // P)
NST = 4
ORDER = [("a", 0), ("a", 1), ("b", 0), ("a", 2), ("b", 1), ("a", 3), ("b", 2), ("b", 3)]
SLOT = {item: s for s, item in enumerate(ORDER)}
ROWS = [min(P, CAP - P * i) for i in range(CT)]
EARLY = 4
LOADED = 1
DROPPED = 4096.0


def quarter(w1, w2, e, s):
    kind, q = ORDER[s]
    src = (w1 if kind == "a" else w2)[bass.ds(e, 1), :, :].rearrange("a r n -> (a r) n")
    if kind == "a":
        return src.rearrange("(c p) f -> p c f", p=P)[:, :, 512 * q:512 * q + 512]
    return src[512 * q:512 * q + 512, :].rearrange("(c p) h -> p c h", p=P)


def split_high(act, stage, stage_in, w_hi, stage_hi, e, s):
    act.wait_ge(stage_in[s % NST], 16 * (2 * e + s // NST + 1))
    act.activation(w_hi[:, s], stage[:, s % NST], ACT.Copy, scale=WSCALE).then_inc(stage_hi, 1)


def split_low(dve, stage, w_hi, w_lo, stage_hi, stage_lo, e, s):
    dve.wait_ge(stage_hi, 8 * e + s + 1)
    dve.scalar_tensor_tensor(w_lo[:, s], stage[:, s % NST], WSCALE, w_hi[:, s],
                             ALU.mult, ALU.subtract).then_inc(stage_lo, 1)


def quantised_self_attention(nc, weights_q, wscale, in_b, out_b, w1, w2, stage, stage_in, x1, x1_stats, ident, ident16):
    E3 = 3 * D
    PAIRS = B // 2
    HALF = B // 2
    FOLD = 6
    with ExitStack() as c:
        def sb(name, shape, dt):
            return c.enter_context(nc.sbuf_tensor(name, shape, dt))

        def sem(name):
            return c.enter_context(nc.semaphore(name))

        wi_q = sb("wi_q", [P, 3, EC, D], f16)
        qo_q = sb("qo_q", [P, EC, D], f16)
        bi = sb("bi_sb", [P, E3], f32)
        bo = sb("bo_sb", [P, D], f32)
        xn = sb("xn2", [P, 2, D], f32)
        xt_hi = sb("xt2_hi", [P, 2, EC, T], f16)
        xt_lo = sb("xt2_lo", [P, 2, EC, T], f16)
        big = sb("big", [P, B, E3], f32)
        prod = stage[:, :, :, :].rearrange("p n c f -> p (n c f)").rearrange("p (i k d) -> p i k d", i=2, k=B)
        scores = sb("scores2", [P, B, B, H], f32)
        row = sb("row", [P, B, H], f32)
        q_val, k_val, v_val = (big[:, :, D * i:D * i + D] for i in range(3))
        heads = q_val
        y = k_val
        hq = sb("hq", [P, B, D], f16)
        ht = sb("ht", [P, 2, EC, T], f16)
        mv = sb("mv2", [P, B, 2], f32)
        var = sb("var2", [P, B], f32)
        std = sb("std2", [P, B], f32)
        rs = sb("rs2", [P, B], f32)
        shift = sb("shift", [P, B], f32)
        tile_max = sb("tile_max", [P, 2, B], f32)
        part = sb("part", [P, 2], f32)
        wide = sb("wide", [P, 2, P], f32)
        scale = {n: sb(f"scale_{n}", [P, 1], f32) for n in ("x", "q", "qx", "xq", "h", "how", "y")}
        inv = {n: sb(f"inv_{n}", [P, 1], f32) for n in ("x", "q", "h", "y")}

        px = [c.enter_context(nc.psum_tensor(f"px{i}", [P, E3], f32)) for i in range(2)]
        pt = [c.enter_context(nc.psum_tensor(f"pt{i}", [P, 512], f32)) for i in range(2)]

        wi_in, wo_in, bias_in = sem("wi_in2"), sem("wo_in2"), sem("bias_in2")
        v_step = sem("v_step2")
        wide_ready = sem("wide_ready")
        wide_t = sem("wide_t")
        var_ready, std_ready, rs_ready = sem("var_ready2"), sem("std_ready2"), sem("rs_ready2")
        xn_ready = sem("xn_ready2")
        xt_ready, xt_hi_ready, xt_lo_ready = sem("xt_ready2"), sem("xt_hi_ready2"), sem("xt_lo_ready2")
        x_ready, x_read = sem("x_ready2"), sem("x_read2")
        x_scaled = sem("x_scaled")
        q_step, q_ready = sem("q_step"), sem("q_ready2")
        v_int_step, v_ready = sem("v_int_step"), sem("v_ready2")
        prod_ready = sem("prod_ready")
        folded = sem("folded")
        prod_summed = sem("prod_summed")
        sum_read = sem("sum_read")
        diff_ready, exp_ready = sem("diff_ready2"), sem("exp_ready2")
        h_scaled, h_round = sem("h_scaled"), sem("h_round")
        hq_ready, ht_ready, ht_read, y_ready, y_read = (sem(n) for n in ("hq_ready", "ht_ready", "ht_read", "y_ready", "y_read"))
        y_scaled, y_step, y_int = sem("y_scaled"), sem("y_step"), sem("y_int")

        def sums_wait(eng, n):
            if not (isinstance(n, int) and n < 2):
                eng.wait_ge(sum_read, n - 1)

        with nc.Block() as block:

            @block.sync
            def _(sp):
                sp.dma_start(wi_q[:, :, :, :], weights_q[:, 0:3, :, :]).then_inc(wi_in, 16)
                sp.dma_start(bi[:, :], in_b.rearrange("(a d) -> a d", a=1).to_broadcast([P, E3])).then_inc(bias_in, 16)
                sp.dma_start(qo_q[:, :, :], weights_q[:, 3, :, :]).then_inc(wo_in, 16)
                sp.dma_start(bo[:, :], out_b.rearrange("(a d) -> a d", a=1).to_broadcast([P, D])).then_inc(bias_in, 16)
                sp.wait_ge(prod_summed, 2 * B)
                for s in range(NST):
                    sp.dma_start(stage[:, s], quarter(w1, w2, 0, s)).then_inc(stage_in[s], 16)

            @block.gpsimd
            def _(gp):
                gp.wait_ge(rs_ready, 1)
                for t in range(B):
                    if t >= 2:
                        gp.wait_ge(xt_ready, t - 1)
                    gp.tensor_scalar(xn[:, t % 2, :], x1[:, t, :], rs[:, t:t + 1], shift[:, t:t + 1],
                                     ALU.mult, ALU.add).then_inc(xn_ready, 1)

                gp.wait_ge(x_scaled, 1)

                def quantise_q(t):
                    q_t = q_val[:, t, :]
                    gp.tensor_scalar(q_t, q_t, inv["x"][:, :], ROUND, ALU.mult, ALU.add).then_inc(q_step, 1)
                    gp.wait_ge(q_step, 3 * t + 1)
                    gp.tensor_scalar(q_t, q_t, -ROUND, scale["xq"][:, :], ALU.add, ALU.mult).then_inc(q_step, 1)
                    gp.wait_ge(q_step, 3 * t + 2)
                    gp.tensor_scalar(q_t, q_t, 1.0, ROUND, ALU.mult, ALU.add).then_inc(q_step, 1)
                    gp.wait_ge(q_step, 3 * t + 3)
                    gp.tensor_scalar(q_t, q_t, -ROUND, 1.0, ALU.add, ALU.mult).then_inc(q_ready, 1)

                quantise_q(0)
                quantise_q(1)
                for q in range(B):
                    gp.tensor_scalar(v_val[:, q, :], v_val[:, q, :], inv["x"][:, :], ROUND, ALU.mult, ALU.add).then_inc(v_int_step, 1)
                    gp.wait_ge(v_int_step, q + 1)
                    gp.tensor_scalar(v_val[:, q, :], v_val[:, q, :], -ROUND, 1.0, ALU.add, ALU.mult).then_inc(v_ready, 1)
                    gp.wait_ge(prod_ready, q + 1)
                    by_dim = prod[:, q % 2].rearrange("p k (h d) -> p (k h) d", h=H)
                    kept = by_dim[:, :, HD - 2 * FOLD:HD - FOLD]
                    gp.tensor_tensor(kept, kept, by_dim[:, :, HD - FOLD:HD], ALU.add).then_inc(folded, 1)
                    if q + 2 < B:
                        quantise_q(q + 2)
                for q in range(B):
                    gp.wait_ge(prod_ready, B + q + 1)
                    gp.tensor_tensor(prod[:, q % 2, B - 2, :], prod[:, q % 2, B - 2, :], prod[:, q % 2, B - 1, :],
                                     ALU.add).then_inc(folded, 1)

                gp.wait_ge(h_scaled, 1)
                for t in range(B):
                    gp.tensor_scalar(heads[:, t, :], heads[:, t, :], inv["h"][:, :], ROUND, ALU.mult, ALU.add).then_inc(h_round, 1)
                    gp.wait_ge(h_round, t + 1)
                    gp.tensor_scalar(hq[:, t, :], heads[:, t, :], -ROUND, 1.0, ALU.add, ALU.mult).then_inc(hq_ready, 1)
                gp.wait_ge(y_scaled, 1)
                for t in range(HALF, B):
                    gp.tensor_scalar(y[:, t, :], y[:, t, :], inv["y"][:, :], ROUND, ALU.mult, ALU.add).then_inc(y_step, 1)
                for t in range(HALF, B):
                    gp.wait_ge(y_step, t - HALF + 1)
                    gp.tensor_scalar(y[:, t, :], y[:, t, :], -ROUND, 1.0, ALU.add, ALU.mult).then_inc(y_int, 1)

            @block.scalar
            def _(act):
                act.wait_ge(var_ready, 1)
                act.activation(std[:, :], var[:, :], ACT.Sqrt).then_inc(std_ready, 1)
                for t in range(B):
                    act.wait_ge(xt_ready, t + 1)
                    if t >= 2:
                        act.wait_ge(x_ready, t - 1)
                    act.activation(xt_hi[:, t % 2], pt[t % 2][:, :].rearrange("p (c t) -> p c t", c=EC),
                                   ACT.Copy).then_inc(xt_hi_ready, 1)

                def read_scores(pair):
                    for i in range(2):
                        q = 2 * pair + i
                        act.wait_ge(prod_summed, q + 1)
                        act.activation(scores[:, bass.ds(q, 1), :, :].rearrange("p a k h -> p (a k h)"),
                                       px[i][:, 0:B * H], ACT.Copy).then_inc(sum_read, 1)

                def exp(half):
                    act.wait_ge(diff_ready, half + 1)
                    s_half = scores[:, HALF * half:HALF * half + HALF]
                    act.activation(s_half, s_half, ACT.Exp, scale=scale["qx"][:, :]).then_inc(exp_ready, 1)

                with act.Fori(0, PAIRS - 1) as pair:
                    read_scores(pair)
                exp(0)
                read_scores(PAIRS - 1)
                exp(1)

                def read_heads(pair):
                    for i in range(2):
                        q = 2 * pair + i
                        act.wait_ge(prod_summed, B + q + 1)
                        act.activation(heads[:, bass.ds(q, 1), :].rearrange("p a d -> p (a d)"),
                                       px[i][:, 0:D], ACT.Copy, scale=scale["x"][:, :]).then_inc(sum_read, 1)

                with act.Fori(0, PAIRS) as pair:
                    read_heads(pair)
                for t in range(B):
                    act.wait_ge(ht_ready, t + 1)
                    if t >= 2:
                        act.wait_ge(y_ready, t - 1)
                    act.activation(ht[:, t % 2], pt[t % 2][:, :].bitcast(f16)[:, 0:EC * T].rearrange("p (c t) -> p c t", c=EC),
                                   ACT.Copy).then_inc(ht_read, 1)

            @block.vector
            def _(dve):
                steps = Steps(dve, v_step)
                rounds = [0]

                def do(instruction):
                    steps.did(instruction)
                    steps.wait()

                def across_partitions(n):
                    dve.tensor_copy(wide[:, 0:n, :], part[:, 0:n].unsqueeze(2).to_broadcast([P, n, P])).then_inc(wide_ready, 1)
                    rounds[0] += 1
                    dve.wait_ge(wide_t, rounds[0])
                    do(dve.tensor_reduce(part[:, 0:n], pt[0][:, 0:P * n].rearrange("p (n q) -> p n q", n=n), AX.X, ALU.max))

                def scale_from_max(name, largest):
                    do(dve.tensor_scalar(scale[name][:, :], largest, 1.0 / QMAX, QFLOOR, ALU.mult, ALU.max))
                    do(dve.reciprocal(inv[name][:, :], scale[name][:, :]))

                def absmax(out, in_):
                    steps.did(dve.tensor_reduce(out, in_, AX.X, ALU.max, apply_absolute_value=True))

                for t in range(B - 1):
                    steps.did(dve.bn_aggr(mv[:, t, :], x1_stats[:, t, :]))
                steps.did(dve.bn_stats(x1_stats[:, B - 1, :], x1[:, B - 1, :]))
                steps.wait()
                steps.did(dve.bn_aggr(mv[:, B - 1, :], x1_stats[:, B - 1, :]))
                steps.wait()
                dve.tensor_scalar(var[:, :], mv[:, :, 1], EPS, None, ALU.add).then_inc(var_ready, 1)
                dve.wait_ge(std_ready, 1)
                rsqrt_from_std(dve, steps, rs, std, var)
                dve.scalar_tensor_tensor(shift[:, :], mv[:, :, 0], -1.0, rs[:, :], ALU.mult, ALU.mult).then_inc(rs_ready, 1)

                for t in range(B):
                    dve.wait_ge(xt_hi_ready, t + 1)
                    dve.tensor_tensor(xt_lo[:, t % 2], pt[t % 2][:, :].rearrange("p (c t) -> p c t", c=EC),
                                      xt_hi[:, t % 2], ALU.subtract).then_inc(xt_lo_ready, 1)
                    if t == 1:
                        dve.wait_ge(bias_in, 32)
                    if t:
                        dve.wait_ge(x_ready, t)
                        read_x = t - 1
                        dve.scalar_tensor_tensor(big[:, read_x, :], px[read_x % 2][:, :], wscale[:, 0:1], bi[:, :],
                                                 ALU.mult, ALU.add).then_inc(x_read, 1)
                        dve.wait_ge(x_read, t)
                        absmax(tile_max[:, 0, read_x:t], big[:, read_x, 0:D])
                        absmax(tile_max[:, 1, read_x:t], big[:, read_x, D:E3])
                dve.wait_ge(x_ready, B)
                dve.scalar_tensor_tensor(big[:, B - 1, :], px[(B - 1) % 2][:, :], wscale[:, 0:1], bi[:, :],
                                         ALU.mult, ALU.add).then_inc(x_read, 1)
                dve.wait_ge(x_read, B)
                absmax(tile_max[:, 0, B - 1:B], big[:, B - 1, 0:D])
                absmax(tile_max[:, 1, B - 1:B], big[:, B - 1, D:E3])
                steps.wait()
                do(dve.tensor_reduce(part[:, :], tile_max[:, :, :], AX.X, ALU.max))
                across_partitions(2)
                do(dve.tensor_tensor(part[:, 1:2], part[:, 0:1], part[:, 1:2], ALU.max))
                scale_from_max("x", part[:, 1:2])
                do(dve.tensor_scalar(part[:, 0:1], part[:, 0:1], inv["x"][:, :], ROUND, ALU.mult, ALU.add))
                do(dve.tensor_scalar(part[:, 0:1], part[:, 0:1], -ROUND, scale["x"][:, :], ALU.add, ALU.mult))
                do(dve.tensor_scalar(part[:, 0:1], part[:, 0:1], 1.0 / sqrt(HD), None, ALU.mult))
                scale_from_max("q", part[:, 0:1])
                do(dve.tensor_scalar(scale["xq"][:, :], scale["x"][:, :], 1.0 / sqrt(HD), inv["q"][:, :], ALU.mult, ALU.mult))
                dve.tensor_tensor(scale["qx"][:, :], scale["q"][:, :], scale["x"][:, :], ALU.mult).then_inc(x_scaled, 1)

                do(dve.tensor_scalar(k_val, k_val, inv["x"][:, :], ROUND, ALU.mult, ALU.add))
                do(dve.tensor_scalar(k_val, k_val, -ROUND, QMAX, ALU.add, ALU.min))

                def times_keys(pair):
                    for i in range(2):
                        q = 2 * pair + i
                        dve.wait_ge(q_ready, q + 1)
                        if not (isinstance(pair, int) and pair == 0):
                            dve.wait_ge(prod_summed, q - 1)
                        dve.tensor_tensor(prod[:, i], k_val, q_val[:, bass.ds(q, 1), :].to_broadcast([P, B, D]),
                                          ALU.mult).then_inc(prod_ready, 1)

                times_keys(0)
                with dve.Fori(1, PAIRS) as pair:
                    times_keys(pair)

                def softmax(half):
                    dve.wait_ge(sum_read, HALF * (half + 1))
                    s_q = scores[:, HALF * half:HALF * half + HALF]
                    s_h = s_q.rearrange("p q k h -> p q h k")
                    r = row[:, HALF * half:HALF * half + HALF, :]
                    r_q = r.unsqueeze(2).to_broadcast([P, HALF, B, H])
                    do(dve.tensor_reduce(r, s_h, AX.X, ALU.max))
                    dve.tensor_tensor(s_q, s_q, r_q, ALU.subtract).then_inc(diff_ready, 1)
                    dve.wait_ge(exp_ready, half + 1)
                    do(dve.tensor_reduce(r, s_h, AX.X, ALU.add))
                    do(dve.reciprocal(r, r))
                    do(dve.tensor_tensor(s_q, s_q, r_q, ALU.mult))

                def largest_head(q):
                    dve.wait_ge(sum_read, B + q + 1)
                    dve.tensor_reduce(tile_max[:, 0, bass.ds(q, 1)], heads[:, bass.ds(q, 1), :], AX.XY, ALU.max,
                                      apply_absolute_value=True).then_inc(v_step, 1)

                def times_values(pair):
                    for i in range(2):
                        q = 2 * pair + i
                        dve.wait_ge(prod_summed, B + q - 1)
                        p_q = scores[:, bass.ds(q, 1), :, :].rearrange("p a k h -> p (a k) h").unsqueeze(3)
                        dve.tensor_tensor(prod[:, i].rearrange("p k (h d) -> p k h d", h=H),
                                          v_val.rearrange("p k (h d) -> p k h d", h=H),
                                          p_q.to_broadcast([P, B, H, HD]), ALU.mult).then_inc(prod_ready, 1)
                        if not (isinstance(pair, int) and pair == 0):
                            largest_head(q - 2)

                softmax(0)
                dve.wait_ge(v_ready, B)
                times_values(0)
                softmax(1)
                with dve.Fori(1, PAIRS) as pair:
                    times_values(pair)
                for q in (B - 2, B - 1):
                    largest_head(q)
                steps.n += B
                steps.wait()

                do(dve.tensor_reduce(part[:, 0:1], tile_max[:, 0, :], AX.X, ALU.max))
                across_partitions(1)
                do(dve.tensor_scalar(scale["h"][:, :], part[:, 0:1], 1.0 / QMAX, QFLOOR, ALU.mult, ALU.max))
                dve.reciprocal(inv["h"][:, :], scale["h"][:, :]).then_inc(h_scaled, 1)
                do(dve.tensor_tensor(scale["how"][:, :], scale["h"][:, :], wscale[:, 1:2], ALU.mult))

                for t in range(B):
                    dve.wait_ge(y_ready, t + 1)
                    dve.scalar_tensor_tensor(y[:, t, :], px[t % 2][:, 0:D], scale["how"][:, :], bo[:, :],
                                             ALU.mult, ALU.add).then_inc(y_read, 1)
                    dve.wait_ge(y_read, t + 1)
                    absmax(tile_max[:, 0, t:t + 1], y[:, t, :])
                steps.wait()
                do(dve.tensor_reduce(part[:, 0:1], tile_max[:, 0, :], AX.X, ALU.max))
                across_partitions(1)
                do(dve.tensor_scalar(scale["y"][:, :], part[:, 0:1], 1.0 / QMAX, QFLOOR, ALU.mult, ALU.max))
                dve.reciprocal(inv["y"][:, :], scale["y"][:, :]).then_inc(y_scaled, 1)
                dve.wait_ge(y_scaled, 1)
                first, second = y[:, 0:HALF, :], y[:, HALF:B, :]
                do(dve.tensor_scalar(first, first, inv["y"][:, :], ROUND, ALU.mult, ALU.add))
                do(dve.tensor_scalar(first, first, -ROUND, QMAX, ALU.add, ALU.min))
                dve.scalar_tensor_tensor(x1[:, 0:HALF, :], first, scale["y"][:, :], x1[:, 0:HALF, :], ALU.mult, ALU.add)
                dve.wait_ge(y_int, B - HALF)
                dve.scalar_tensor_tensor(x1[:, HALF:B, :], second, scale["y"][:, :], x1[:, HALF:B, :], ALU.mult, ALU.add)

            @block.tensor
            def _(pe):
                rounds = [0]

                def transpose_wide(n):
                    rounds[0] += 1
                    pe.wait_ge(wide_ready, rounds[0])
                    for i in range(n):
                        last = pe.transpose(pt[0][:, P * i:P * i + P], wide[:, i, :], ident[:, :])
                    last.then_inc(wide_t, 1)

                def transpose_xn(t):
                    pe.wait_ge(xn_ready, t + 1)
                    if t >= 2:
                        pe.wait_ge(xt_lo_ready, t - 1)
                    for e in range(EC):
                        last = pe.transpose(pt[t % 2][:, P * e:P * e + P], xn[:, t % 2, P * e:P * e + P], ident[:, :])
                    last.then_inc(xt_ready, 1)

                transpose_xn(0)
                pe.wait_ge(wi_in, 16)
                for t in range(B):
                    if t + 1 < B:
                        transpose_xn(t + 1)
                    pe.wait_ge(xt_lo_ready, t + 1)
                    if t >= 2:
                        pe.wait_ge(x_read, t - 1)
                    for n in range(3):
                        n_mm = 0
                        for x_part in (xt_hi, xt_lo):
                            for e in range(EC):
                                last = pe.matmul(px[t % 2][:, D * n:D * n + D], x_part[:, t % 2, e, :],
                                                 wi_q[:, n, e, :], start=n_mm == 0, stop=n_mm == 2 * EC - 1)
                                n_mm += 1
                    last.then_inc(x_ready, 1)
                transpose_wide(2)

                def add_over_dims(pair):
                    for i in range(2):
                        q = 2 * pair + i
                        pe.wait_ge(prod_ready, q + 1)
                        if not (isinstance(pair, int) and pair == 0):
                            pe.wait_ge(sum_read, q - 1)
                        by_dim = prod[:, i].rearrange("p k (h d) -> p d k h", h=H)
                        for d in range(HD - FOLD):
                            if d == HD - 2 * FOLD:
                                pe.wait_ge(folded, q + 1)
                            last = pe.matmul(px[i][:, 0:B * H].rearrange("p (k h) -> p k h", k=B), ident[:, :], by_dim[:, d],
                                             start=d == 0, stop=d == HD - FOLD - 1)
                        last.then_inc(prod_summed, 1)

                add_over_dims(0)
                with pe.Fori(1, PAIRS) as pair:
                    add_over_dims(pair)

                def add_over_keys(pair):
                    for i in range(2):
                        q = 2 * pair + i
                        pe.wait_ge(prod_ready, B + q + 1)
                        pe.wait_ge(sum_read, B + q - 1)
                        for k in range(B - 1):
                            if k == B - 2:
                                pe.wait_ge(folded, B + q + 1)
                            last = pe.matmul(px[i][:, 0:D], ident[:, :], prod[:, i, k, :], start=k == 0, stop=k == B - 2)
                        last.then_inc(prod_summed, 1)

                with pe.Fori(0, PAIRS) as pair:
                    add_over_keys(pair)
                transpose_wide(1)

                def transpose_heads(t):
                    pe.wait_ge(hq_ready, t + 1)
                    if t >= 2:
                        pe.wait_ge(ht_read, t - 1)
                    for e in range(EC):
                        last = pe.transpose(pt[t % 2][:, :].bitcast(f16)[:, P * e:P * e + P], hq[:, t, P * e:P * e + P], ident16[:, :])
                    last.then_inc(ht_ready, 1)

                transpose_heads(0)
                pe.wait_ge(wo_in, 16)
                for t in range(B):
                    if t + 1 < B:
                        transpose_heads(t + 1)
                    pe.wait_ge(ht_read, t + 1)
                    if t >= 2:
                        pe.wait_ge(y_read, t - 1)
                    for e in range(EC):
                        last = pe.matmul(px[t % 2][:, 0:D], ht[:, t % 2, e, :], qo_q[:, e, :], start=e == 0, stop=e == EC - 1)
                    last.then_inc(y_ready, 1)
                transpose_wide(1)


def route(nc, rwT, w1, w2, stage, w_hi, w_lo, stage_in, stage_hi, stage_lo, x1, slot_i, gates, xbuf, ident):
    TH = B // 2
    with ExitStack() as c:
        def sb(name, shape, dt):
            return c.enter_context(nc.sbuf_tensor(name, shape, dt))

        def sem(name):
            return c.enter_context(nc.semaphore(name))

        rw = sb("rw", [P, EC, HD], f32)
        fold = sb("fold", [P, E_], f32)
        shares = sb("shares", [P, B, T], f32)
        xn3 = sb("xn3", [P, B, D], f32)
        zeros = sb("zeros", [P, D], f32)
        xt = sb("xt3", [P, 2, EC, T], f32)
        st = sb("st3", [P, B, 6], f32)
        mv = sb("mv3", [P, B, 2], f32)
        var = sb("var3", [P, B], f32)
        std = sb("std3", [P, B], f32)
        rs = sb("rs3", [P, B], f32)
        upper = sb("upper", [P, P], f16)
        ones_sq = sb("ones_sq", [P, P], f16)
        expert_i = sb("expert_i", [P, E_], i32)
        expert_f = sb("expert_f", [P, E_], f32)
        logits = sb("logits", [P, B, E_], f32)
        top = sb("top", [P, B, 8], f32)
        top_i = sb("top_i", [P, B, 8], u32)
        chosen = sb("chosen", [P, TOPK, B], f32)
        hot = sb("hot", [P, TOPK, B, E_], f32)
        both = sb("both", [P, B, E_], f16)
        before = sb("before", [P, B, E_], f16)
        rank_e = sb("rank_e", [P, B, E_], f32)
        masked = sb("masked", [P, TOPK, B, E_], f32)
        rank = sb("rank", [P, TOPK, B], f32)
        keep = sb("keep", [P, TOPK, B], f32)
        slot = sb("slot", [P, TOPK, B], f32)
        send = sb("send", [P, TOPK, B], f32)
        send_i = sb("send_i", [P, TOPK, B], i32)
        gap = sb("gap", [P, B], f32)
        e2 = sb("e2", [P, B], f32)

        pt = [c.enter_context(nc.psum_tensor(f"pt3_{i}", [P, 512], f32)) for i in range(2)]
        ps = [c.enter_context(nc.psum_tensor(f"ps{i}", [P, 512], f32)) for i in range(2)]
        pl = c.enter_context(nc.psum_tensor("pl", [P, B * E_], f32))
        pr = c.enter_context(nc.psum_tensor("pr", [P, B * E_], f32))

        rw_zeroed, fold_ready = sem("rw_zeroed"), sem("fold_ready")
        share_ready = sem("share_ready")
        share_read = sem("share_read")
        rw_in, zeroed, filled = sem("rw_in"), sem("zeroed3"), sem("filled")
        made = sem("made3")
        v_step = sem("v_step3")
        var_ready, std_ready = sem("var_ready3"), sem("std_ready3")
        xn_ready, xt_ready, xt_read, logit_ready = (sem(n) for n in ("xn_ready3", "xt_ready3", "xt_read3", "logit_ready"))
        before_ready = sem("before_ready")
        both_ready, rank_ready, gap_ready, exp_ready, send_ready, sent = (
            sem(n) for n in ("both_ready", "rank_ready", "gap_ready", "exp_ready3", "send_ready", "sent"))

        with nc.Block() as block:

            @block.sync
            def _(sp):
                sp.wait_ge(rw_zeroed, 1)
                sp.dma_start(rw[:, :, 0:E_], rwT.rearrange("(c p) e -> p c e", p=P)).then_inc(rw_in, 16)
                sp.wait_ge(zeroed, 1)
                rows = E_ * CAP
                for r in range(0, rows, P):
                    n = min(P, rows - r)
                    sp.dma_start(xbuf[r:r + n, :], zeros[0:n, :]).then_inc(filled, 16)
                for s in range(NST, NST + LOADED):
                    sp.wait_ge(stage_hi, s - NST + 1)
                    sp.wait_ge(stage_lo, s - NST + 1)
                    sp.dma_start(stage[:, s % NST], quarter(w1, w2, 0, s)).then_inc(stage_in[s % NST], 16)

            @block.gpsimd
            def _(gp):
                gp.memset(rw[:, :, :], 0.0).then_inc(rw_zeroed, 1)
                gp.memset(zeros[:, :], 0.0).then_inc(zeroed, 1)
                gp.memset(ones_sq[:, :], 1.0).then_inc(made, 1)
                gp.iota(expert_i[:, :], [[1, E_]], base=0, channel_multiplier=0).then_inc(made, 1)
                gp.wait_ge(made, 2)
                gp.affine_select(out=upper[:, :], in_=ones_sq[:, :], compare_op=ALU.is_gt, fill=0.0, base=0,
                                 pattern=[[1, P]], channel_multiplier=-1).then_inc(made, 1)
                gp.wait_ge(filled, 16 * (-(-E_ * CAP // P)))
                for t in range(B):
                    if t % TH == 0:
                        gp.wait_ge(send_ready, t // TH + 1)
                    for k in range(TOPK):
                        gp.indirect_dma_start(xbuf, bass.IndirectOffsetOnAxis(ap=send_i[:, k, t:t + 1], axis=0),
                                              xn3[:, t, :], None, bounds_check=E_ * CAP - 1, oob_is_err=False).then_inc(sent, 16)
                gp.wait_ge(sent, 16 * B * TOPK)

            @block.scalar
            def _(act):
                def read_shares(half):
                    act.wait_ge(share_ready, TH * half + TH)
                    act.activation(shares[:, TH * half:TH * half + TH, :], ps[half][:, :].rearrange("p (t n) -> p t n", t=TH),
                                   ACT.Copy).then_inc(share_read, 1)

                for s in range(2):
                    split_high(act, stage, stage_in, w_hi, stage_hi, 0, s)
                act.wait_ge(var_ready, 1)
                act.activation(std[:, :], var[:, :], ACT.Sqrt).then_inc(std_ready, 1)
                for t in range(B):
                    act.wait_ge(xt_ready, t + 1)
                    if t >= 2:
                        act.wait_ge(share_ready, t - 1)
                    act.activation(xt[:, t % 2], pt[t % 2][:, :].rearrange("p (c t) -> p c t", c=EC), ACT.Copy).then_inc(xt_read, 1)
                    if t == TH:
                        read_shares(0)
                read_shares(1)
                act.wait_ge(gap_ready, 2)
                act.activation(e2[:, :], gap[:, :], ACT.Exp).then_inc(exp_ready, 1)
                for s in range(2, EARLY):
                    split_high(act, stage, stage_in, w_hi, stage_hi, 0, s)

            @block.vector
            def _(dve):
                steps = Steps(dve, v_step)

                def do(instruction):
                    steps.did(instruction)
                    steps.wait()

                do(dve.tensor_tensor(fold[:, :], ident[:, 0:E_], ident[:, HD:HD + E_], ALU.add))
                do(dve.tensor_tensor(fold[:, :], fold[:, :], ident[:, 2 * HD:2 * HD + E_], ALU.add))
                dve.tensor_tensor(fold[:, :], fold[:, :], ident[:, 3 * HD:3 * HD + E_], ALU.add).then_inc(fold_ready, 1)
                for t in range(B):
                    steps.did(dve.bn_stats(st[:, t, :], x1[:, t, :]))
                steps.wait()
                for t in range(B):
                    steps.did(dve.bn_aggr(mv[:, t, :], st[:, t, :]))
                steps.wait()
                dve.tensor_scalar(var[:, :], mv[:, :, 1], EPS, None, ALU.add).then_inc(var_ready, 1)
                dve.wait_ge(std_ready, 1)
                rsqrt_from_std(dve, steps, rs, std, var)
                for t in range(B):
                    dve.tensor_scalar(xn3[:, t, :], x1[:, t, :], mv[:, t, 0:1], rs[:, t:t + 1],
                                      ALU.subtract, ALU.mult).then_inc(xn_ready, 1)
                dve.wait_ge(made, 3)
                do(dve.tensor_copy(expert_f[:, :], expert_i[:, :]))
                do(dve.memset(before[:, 0, :], 0.0))
                for half in range(2):
                    tiles = range(TH * half, TH * half + TH)
                    ts = slice(TH * half, TH * half + TH)
                    dve.wait_ge(logit_ready, half + 1)
                    do(dve.tensor_copy(logits[:, ts, :], pl[:, TH * E_ * half:TH * E_ * half + TH * E_].rearrange("p (t e) -> p t e", t=TH)))
                    for t in tiles:
                        steps.did(dve.max(top[:, t, :], logits[:, t, :]))
                    steps.wait()
                    for t in tiles:
                        steps.did(dve.max_index(top_i[:, t, :], top[:, t, :], logits[:, t, :]))
                    dve.tensor_tensor(gap[:, ts], top[:, ts, 1], top[:, ts, 0], ALU.subtract).then_inc(gap_ready, 1)
                    steps.wait()
                    do(dve.tensor_copy(chosen[:, :, ts].rearrange("p k t -> p t k"), top_i[:, ts, 0:TOPK]))
                    for k in range(TOPK):
                        steps.did(dve.tensor_tensor(hot[:, k, ts, :], chosen[:, k, ts].unsqueeze(2).to_broadcast([P, TH, E_]),
                                                    expert_f[:, :].unsqueeze(1).to_broadcast([P, TH, E_]), ALU.is_equal))
                    steps.wait()
                    dve.tensor_tensor(both[:, ts, :], hot[:, 0, ts, :], hot[:, 1, ts, :], ALU.add).then_inc(both_ready, 1)
                    dve.wait_ge(both_ready, half + 1)
                    for t in tiles:
                        if t:
                            dve.tensor_tensor(before[:, t, :], before[:, t - 1, :], both[:, t - 1, :], ALU.add).then_inc(before_ready, 1)
                            dve.wait_ge(before_ready, t)
                    dve.wait_ge(rank_ready, half + 1)
                    do(dve.tensor_copy(rank_e[:, ts, :], pr[:, TH * E_ * half:TH * E_ * half + TH * E_].rearrange("p (t e) -> p t e", t=TH)))
                    for k in range(TOPK):
                        steps.did(dve.tensor_tensor(masked[:, k, ts, :], hot[:, k, ts, :], rank_e[:, ts, :], ALU.mult))
                    steps.wait()
                    do(dve.tensor_reduce(rank[:, :, ts], masked[:, :, ts, :], AX.X, ALU.add))
                    do(dve.tensor_scalar(keep[:, :, ts], rank[:, :, ts], float(CAP), None, ALU.is_lt))
                    do(dve.tensor_scalar(slot[:, :, ts], rank[:, :, ts], float(CAP - 1), None, ALU.min))
                    do(dve.scalar_tensor_tensor(slot[:, :, ts], chosen[:, :, ts], float(CAP), slot[:, :, ts], ALU.mult, ALU.add))
                    do(dve.tensor_scalar(send[:, :, ts], keep[:, :, ts], -DROPPED, DROPPED, ALU.mult, ALU.add))
                    do(dve.tensor_tensor(send[:, :, ts], send[:, :, ts], slot[:, :, ts], ALU.add))
                    dve.tensor_copy(send_i[:, :, ts], send[:, :, ts]).then_inc(send_ready, 1)
                dve.wait_ge(exp_ready, 1)
                do(dve.tensor_scalar(gates[:, 0, :], e2[:, :], 1.0, None, ALU.add))
                do(dve.reciprocal(gates[:, 0, :], gates[:, 0, :]))
                do(dve.tensor_tensor(gates[:, 1, :], gates[:, 0, :], e2[:, :], ALU.mult))
                dve.tensor_copy(slot_i[:, :, :], slot[:, :, :])
                dve.tensor_tensor(gates[:, :, :], gates[:, :, :], keep[:, :, :], ALU.mult)
                for s in range(EARLY):
                    split_low(dve, stage, w_hi, w_lo, stage_hi, stage_lo, 0, s)
                dve.wait_ge(xn_ready, B)
                dve.tensor_tensor(x1[:, :, :], x1[:, :, :], xn3[:, :, :], ALU.add)

            @block.tensor
            def _(pe):
                pe.wait_ge(rw_in, 16)

                def transpose_xn(t):
                    pe.wait_ge(xn_ready, t + 1)
                    if t >= 2:
                        pe.wait_ge(xt_read, t - 1)
                    for e in range(EC):
                        last = pe.transpose(pt[t % 2][:, P * e:P * e + P], xn3[:, t, P * e:P * e + P], ident[:, :])
                    last.then_inc(xt_ready, 1)

                def add_shares(half):
                    pe.wait_ge(share_read, half + 1)
                    for t in range(TH * half, TH * half + TH):
                        last = pe.matmul(pl[:, E_ * t:E_ * t + E_], shares[:, t, :], fold[:, :], start=True, stop=True)
                    last.then_inc(logit_ready, 1)

                def rank_tokens(half):
                    tiles = slice(TH * half, TH * half + TH)
                    out = pr[:, TH * E_ * half:TH * E_ * half + TH * E_]
                    pe.wait_ge(both_ready, half + 1)
                    pe.wait_ge(made, 3)
                    pe.matmul(out, upper[:, :], both[:, tiles, :].rearrange("p t e -> p (t e)"), start=True, stop=False)
                    pe.wait_ge(before_ready, TH * half + TH - 1)
                    pe.matmul(out, ones_sq[:, :], before[:, tiles, :].rearrange("p t e -> p (t e)"),
                              start=False, stop=True).then_inc(rank_ready, 1)

                transpose_xn(0)
                for t in range(B):
                    if t + 1 < B:
                        transpose_xn(t + 1)
                    pe.wait_ge(xt_read, t + 1)
                    for e in range(EC):
                        last = pe.matmul(ps[t // TH][HD * e:HD * e + HD, T * (t % TH):T * (t % TH) + T], rw[:, e, :], xt[:, t % 2, e, :],
                                         start=True, stop=True, tile_position=(0, HD * e))
                    last.then_inc(share_ready, 1)
                    if t == TH + 1:
                        pe.wait_ge(fold_ready, 1)
                        add_shares(0)
                rank_tokens(0)
                add_shares(1)
                rank_tokens(1)


def experts(nc, w1, w2, stage, w_hi, w_lo, stage_in, stage_hi, stage_lo, xbuf, obuf, ident):
    with ExitStack() as c:
        def sb(name, shape, dt):
            return c.enter_context(nc.sbuf_tensor(name, shape, dt))

        def sem(name):
            return c.enter_context(nc.semaphore(name))

        xg = sb("xg", [P, CT, D], f32)
        xt_hi = sb("xt3_hi", [P, EC, CAP], f16)
        xt_lo = sb("xt3_lo", [P, EC, CAP], f16)
        hf = sb("hf", [P, 2, CAP], f32)
        h_hi = sb("h_hi", [P, 8, CAP], f16)
        h_lo = sb("h_lo", [P, 8, CAP], f16)
        ot_sb = sb("ot_sb", [P, EC, CAP], f32)
        o_sb = sb("o_sb", [P, CT, D], f32)

        ph = [c.enter_context(nc.psum_tensor(f"ph{i}", [P, 512], f32)) for i in range(2)]
        po = [c.enter_context(nc.psum_tensor(f"po3_{i}", [P, 512], f32)) for i in range(EC)]
        pt = [c.enter_context(nc.psum_tensor(f"ptx{i}", [P, 512], f32)) for i in range(2)]

        xg_first_in, xg_in = sem("xg_first_in"), sem("xg_in")
        xt_ready, xt_hi_ready, xt_lo_ready = sem("xg_t_ready"), sem("xg_hi_ready"), sem("xg_lo_ready")
        a_ready = sem("a_ready")
        a_done = sem("a_done")
        h_step, h_ready = sem("h_step"), sem("h_ready")
        b_done = sem("b_done")
        ot_ready = sem("ot_sb_ready")
        o_turned = sem("o_turned")
        o_ready, o_stored = sem("o_sb_ready"), sem("o_stored")

        def wait_used(eng, e, s):
            kind, q = ORDER[s]
            if kind == "a":
                eng.wait_ge(a_ready, 16 * (e - 1) + 4 * q + 4)
            else:
                eng.wait_ge(b_done, 4 * (e - 1) + q + 1)

        with nc.Block() as block:

            @block.sync
            def _(sp):
                def load(e, s):
                    if not isinstance(e, int):
                        sp.compute_val(e * (D * F) * 4)
                    wait_each(sp, (stage_hi, 8 * e + s - NST + 1), (stage_lo, 8 * e + s - NST + 1))
                    sp.dma_start(stage[:, s % NST], quarter(w1, w2, e, s)).then_inc(stage_in[s % NST], 16)

                for i in range(CT):
                    sp.dma_start(xg[0:ROWS[i], i, :], xbuf[P * i:P * i + ROWS[i], :]).then_inc(xg_first_in, 16)
                sp.wait_ge(xg_first_in, 16 * CT)
                for s in range(NST + LOADED, 8):
                    load(0, s)
                with sp.Fori(1, E_) as e:
                    for s in range(8):
                        load(e, s)

            @block.gpsimd
            def _(gp):
                def load_x(e):
                    for i in range(CT):
                        row = e * CAP + P * i
                        gp.dma_start(xg[0:ROWS[i], i, :], xbuf[bass.ds(row, ROWS[i]), :]).then_inc(xg_in, 16)

                def store(e):
                    gp.wait_ge(o_ready, CT * e + CT)
                    for i in range(CT):
                        row = e * CAP + P * i
                        gp.dma_start(obuf[bass.ds(row, ROWS[i]), :], o_sb[0:ROWS[i], i, :]).then_inc(o_stored, 16)

                def body(e):
                    gp.wait_ge(xt_ready, EC * e + EC)
                    load_x(e + 1)
                    store(e)

                body(0)
                with gp.Fori(1, E_ - 1) as e:
                    body(e)
                store(E_ - 1)
                gp.wait_ge(o_stored, 16 * CT * E_)

            @block.scalar
            def _(act):
                def split(e, s):
                    if not (isinstance(e, int) and e == 0):
                        wait_used(act, e, s)
                    split_high(act, stage, stage_in, w_hi, stage_hi, e, s)

                def silu(e, q, chunks=range(4)):
                    for f in chunks:
                        n = 16 * e + 4 * q + f
                        act.wait_ge(a_ready, n + 1)
                        if not (isinstance(e, int) and e == 0 and q == 0 and f < 2):
                            act.wait_ge(h_ready, n - 1)
                        act.activation(hf[:, f % 2, :], ph[f % 2][:, 0:CAP], ACT.Silu, scale=1.0 / WSCALE).then_inc(a_done, 1)

                def split_x(e, chunks):
                    for i in chunks:
                        act.wait_ge(xt_ready, EC * e + i + 1)
                        act.activation(xt_hi[:, i, :], pt[i % 2][:, 0:CAP], ACT.Copy).then_inc(xt_hi_ready, 1)

                def read_out(e, i):
                    act.wait_ge(o_turned, CT * e + i + 1)
                    if i == 0 and not (isinstance(e, int) and e == 0):
                        act.wait_ge(o_stored, 16 * CT * e)
                    act.activation(o_sb[0:ROWS[i], i, :], pt[i % 2][0:ROWS[i], :], ACT.Copy).then_inc(o_ready, 1)

                split_x(0, range(EC))
                for s in range(EARLY, 7):
                    split(0, s)

                def body(e, last):
                    first = isinstance(e, int) and e == 0
                    silu(e, 0)
                    if not first:
                        read_out(e - 1, 0)
                        read_out(e - 1, 1)
                    split(e, 7)
                    silu(e, 1, range(1))
                    if not first:
                        read_out(e - 1, 2)
                    silu(e, 1, range(1, 4))
                    if not last:
                        split(e + 1, 0)
                        split(e + 1, 1)
                    silu(e, 2)
                    if not last:
                        split(e + 1, 2)
                    silu(e, 3)
                    if not last:
                        for s in (3, 4, 5):
                            split(e + 1, s)
                        split_x(e + 1, range(EC))
                        split(e + 1, 6)

                body(0, False)
                with act.Fori(1, E_ - 1) as e:
                    body(e, False)
                body(E_ - 1, True)
                for i in range(CT):
                    read_out(E_ - 1, i)

            @block.vector
            def _(dve):
                def split(e, s):
                    split_low(dve, stage, w_hi, w_lo, stage_hi, stage_lo, e, s)

                def split_h(e, q):
                    if not (isinstance(e, int) and e == 0 and q < 2):
                        dve.wait_ge(b_done, 4 * e + q - 1)
                    for f in range(4):
                        n = 16 * e + 4 * q + f
                        at = 4 * (q % 2) + f
                        dve.wait_ge(a_done, n + 1)
                        dve.tensor_copy(h_hi[:, at, :], hf[:, f % 2, :]).then_inc(h_step, 1)
                        dve.wait_ge(h_step, n + 1)
                        dve.tensor_tensor(h_lo[:, at, :], hf[:, f % 2, :], h_hi[:, at, :], ALU.subtract).then_inc(h_ready, 1)

                def split_x(e, chunks):
                    for i in chunks:
                        dve.wait_ge(xt_hi_ready, EC * e + i + 1)
                        dve.tensor_tensor(xt_lo[:, i, :], pt[i % 2][:, 0:CAP], xt_hi[:, i, :], ALU.subtract).then_inc(xt_lo_ready, 1)

                def read_out(e):
                    dve.wait_ge(b_done, 4 * e + 4)
                    if not (isinstance(e, int) and e == 0):
                        dve.wait_ge(o_turned, CT * e)
                    for i in range(EC):
                        dve.tensor_scalar(ot_sb[:, i, :], po[i][:, 0:CAP], 1.0 / WSCALE, None, ALU.mult).then_inc(ot_ready, 1)

                split_x(0, range(EC))
                for s in range(EARLY, 7):
                    split(0, s)

                def body(e, last):
                    split_h(e, 0)
                    split(e, 7)
                    split_h(e, 1)
                    if not last:
                        split(e + 1, 0)
                        split(e + 1, 1)
                    split_h(e, 2)
                    if not last:
                        split(e + 1, 2)
                    split_h(e, 3)
                    if not last:
                        for s in (3, 4, 5):
                            split(e + 1, s)
                        split_x(e + 1, range(EC))
                        split(e + 1, 6)
                    read_out(e)

                body(0, False)
                with dve.Fori(1, E_ - 1) as e:
                    body(e, False)
                body(E_ - 1, True)

            @block.tensor
            def _(pe):
                def wait_split(e, s):
                    wait_each(pe, (stage_hi, 8 * e + s + 1), (stage_lo, 8 * e + s + 1))

                def transpose_x(e, chunks):
                    for i in chunks:
                        if i == 0:
                            if isinstance(e, int) and e == 0:
                                pe.wait_ge(xg_first_in, 16 * CT)
                            else:
                                pe.wait_ge(xg_in, 16 * CT * e)
                            if not (isinstance(e, int) and e < 2):
                                pe.wait_ge(o_ready, CT * (e - 1))
                            elif e == 1:
                                pe.wait_ge(xt_lo_ready, EC)
                        if i >= 2:
                            pe.wait_ge(xt_lo_ready, EC * e + i - 1)
                        for j in range(CT):
                            last = pe.transpose(pt[i % 2][:, P * j:P * j + ROWS[j]], xg[0:ROWS[j], j, P * i:P * i + P],
                                                ident[0:ROWS[j], 0:ROWS[j]])
                        last.then_inc(xt_ready, 1)

                def transpose_out(e, i):
                    if i == 0:
                        pe.wait_ge(ot_ready, EC * e + EC)
                    if i == 2:
                        pe.wait_ge(o_ready, CT * e + 1)
                    for j in range(EC):
                        last = pe.transpose(pt[i % 2][0:ROWS[i], P * j:P * j + P], ot_sb[:, j, P * i:P * i + ROWS[i]], ident[:, :])
                    last.then_inc(o_turned, 1)

                def hidden(e, q, chunks=range(4)):
                    s = SLOT["a", q]
                    if 0 in chunks:
                        wait_split(e, s)
                        if q == 0:
                            pe.wait_ge(xt_lo_ready, EC * e + EC)
                    for f in chunks:
                        n = 16 * e + 4 * q + f
                        if not (isinstance(e, int) and e == 0 and q == 0 and f < 2):
                            pe.wait_ge(a_done, n - 1)
                        n_mm = 0
                        for w_part, x_part in mm_terms(w_hi, w_lo, xt_hi, xt_lo):
                            for i in range(EC):
                                last = pe.matmul(ph[f % 2][:, 0:CAP], w_part[:, s, i, P * f:P * f + P], x_part[:, i, :],
                                                 start=n_mm == 0, stop=n_mm == 3 * EC - 1)
                                n_mm += 1
                        last.then_inc(a_ready, 1)

                def output(e, q, chunks):
                    s = SLOT["b", q]
                    if 0 in chunks:
                        wait_split(e, s)
                        if q == 0 and not (isinstance(e, int) and e == 0):
                            pe.wait_ge(ot_ready, EC * e)
                    for f in chunks:
                        pe.wait_ge(h_ready, 16 * e + 4 * q + f + 1)
                        at = 4 * (q % 2) + f
                        for i in range(EC):
                            for n, (w_part, h_part) in enumerate(mm_terms(w_hi, w_lo, h_hi, h_lo)):
                                last = pe.matmul(po[i][:, 0:CAP], w_part[:, s, f, P * i:P * i + P], h_part[:, at, :],
                                                 start=q == 0 and f == 0 and n == 0, stop=q == FQ - 1 and f == 3 and n == 2)
                    if 3 in chunks:
                        last.then_inc(b_done, 1)

                transpose_x(0, range(EC))

                def body(e, last):
                    first = isinstance(e, int) and e == 0
                    hidden(e, 0, range(2))
                    if not first:
                        transpose_out(e - 1, 0)
                        transpose_out(e - 1, 1)
                    hidden(e, 0, range(2, 4))
                    hidden(e, 1, range(1))
                    if not first:
                        transpose_out(e - 1, 2)
                    hidden(e, 1, range(1, 4))
                    output(e, 0, range(4))
                    hidden(e, 2)
                    output(e, 1, range(4))
                    hidden(e, 3)
                    output(e, 2, range(4))
                    if not last:
                        transpose_x(e + 1, range(2))
                    output(e, 3, range(2))
                    if not last:
                        transpose_x(e + 1, range(2, 4))
                    output(e, 3, range(2, 4))

                body(0, False)
                with pe.Fori(1, E_ - 1) as e:
                    body(e, False)
                body(E_ - 1, True)
                for i in range(CT):
                    transpose_out(E_ - 1, i)


def combine(nc, x1, slot_i, gates, obuf, out):
    with ExitStack() as c:
        pair = c.enter_context(nc.sbuf_tensor("pair", [P, B, TOPK, D], f32))
        got = [c.enter_context(nc.semaphore(f"got{t}")) for t in range(B)]
        step, summed, stored = (c.enter_context(nc.semaphore(n)) for n in ("step5", "summed", "stored"))
        with nc.Block() as block:

            @block.gpsimd
            def _(gp):
                for t in range(B):
                    for k in range(TOPK):
                        gp.indirect_dma_start(pair[:, t, k, :], None, obuf,
                                              bass.IndirectOffsetOnAxis(ap=slot_i[:, k, t:t + 1], axis=0)).then_inc(got[t], 16)

            @block.vector
            def _(dve):
                for t in range(B):
                    dve.wait_ge(got[t], 16 * TOPK)
                    dve.scalar_tensor_tensor(x1[:, t, :], pair[:, t, 0, :], gates[:, 0, t:t + 1], x1[:, t, :],
                                             ALU.mult, ALU.add).then_inc(step, 1)
                    dve.wait_ge(step, t + 1)
                    dve.scalar_tensor_tensor(x1[:, t, :], pair[:, t, 1, :], gates[:, 1, t:t + 1], x1[:, t, :],
                                             ALU.mult, ALU.add).then_inc(summed, 1)

            @block.sync
            def _(sp):
                for t in range(B):
                    sp.wait_ge(summed, t + 1)
                    sp.dma_start(out[t], x1[:, t, :]).then_inc(stored, 16)
                sp.wait_ge(stored, 16 * B)


def build_block(nc, x, ctxT, wqT, wkT, wvT, woT, wiT, in_b, qoT, out_b, rwT, w1, w2, out):
    xbuf = nc.dram_tensor("xbuf", [E_ * CAP, D], f32).ap()
    obuf = nc.dram_tensor("obuf", [E_ * CAP, D], f32).ap()
    weights_q = nc.dram_tensor("weights_q", [P, 4, EC, 512], f16).ap()
    wmax = nc.dram_tensor("wmax", [P, 2], f32).ap()
    with ExitStack() as c:
        def sb(name, shape, dt):
            return c.enter_context(nc.sbuf_tensor(name, shape, dt))

        x1 = sb("x1", [P, B, D], f32)
        ident = sb("ident", [P, P], f32)
        ident16 = sb("ident16", [P, P], f16)
        ones = sb("ones", [P, HD], f32)
        ones16 = sb("ones16", [P, 1], f16)
        slot_i = sb("slot_i", [P, TOPK, B], i32)
        gates = sb("gates", [P, TOPK, B], f32)
        constants(nc, ident, ident16, ones, ones16)
        x1_stats = sb("x1_stats", [P, B, 6], f32)
        wscale = sb("wscale", [P, 2], f32)
        cross_attention(nc, x, ctxT, wqT, wkT, wvT, woT, wiT, qoT, weights_q, wmax, wscale, x1, x1_stats,
                        ident, ident16, ones, ones16)
        stage_in = [c.enter_context(nc.semaphore(f"w_in{i}")) for i in range(NST)]
        stage_hi, stage_lo = (c.enter_context(nc.semaphore(n)) for n in ("w_hi_ready", "w_lo_ready"))
        with nc.sbuf_tensor("stage_w", [P, NST, EC, 512], f32) as stage:
            quantised_self_attention(nc, weights_q, wscale, in_b, out_b, w1, w2, stage, stage_in, x1, x1_stats,
                                     ident, ident16)
            with nc.sbuf_tensor("w_hi3", [P, 8, EC, 512], f16) as w_hi, nc.sbuf_tensor("w_lo3", [P, 8, EC, 512], f16) as w_lo:
                split = (stage, w_hi, w_lo, stage_in, stage_hi, stage_lo)
                route(nc, rwT, w1, w2, *split, x1, slot_i, gates, xbuf, ident)
                experts(nc, w1, w2, *split, xbuf, obuf, ident)
        combine(nc, x1, slot_i, gates, obuf, out)


def kernel(x, ctx_1024, L0_xattn_Wq, L0_xattn_Wk, L0_xattn_Wv, L0_xattn_Wo, L0_attn_key, L0_attn_value,
           L0_attn_in_w, L0_attn_in_b, L0_attn_out_w, L0_attn_out_b, L0_ffn_router_w, L0_ffn_w1, L0_ffn_w2):
    import numpy as np
    import concourse.bacc as bacc
    from concourse.bass_utils import run_bass_kernel_spmd

    arrays = {
        "x": x, "ctxT": np.asarray(ctx_1024).transpose(0, 2, 1), "wqT": np.asarray(L0_xattn_Wq).T,
        "wkT": np.asarray(L0_xattn_Wk).T, "wvT": np.asarray(L0_xattn_Wv).T, "woT": np.asarray(L0_xattn_Wo).T,
        "wiT": np.asarray(L0_attn_in_w).T, "in_b": L0_attn_in_b, "qoT": np.asarray(L0_attn_out_w).T,
        "out_b": L0_attn_out_b, "rwT": np.asarray(L0_ffn_router_w).T, "w1": L0_ffn_w1, "w2": L0_ffn_w2,
    }
    arrays = {f"in_{n}": np.ascontiguousarray(a) for n, a in arrays.items()}
    nc = bacc.Bacc("TRN2", target_bir_lowering=False, num_devices=1)
    args = [nc.dram_tensor(n, a.shape, mybir.dt.from_np(a.dtype), kind="ExternalInput").ap() for n, a in arrays.items()]
    args.append(nc.dram_tensor("out_x", (B, T, D), f32, kind="ExternalOutput").ap())
    build_block(nc, *args)
    return run_bass_kernel_spmd(nc, [arrays], core_ids=[0]).results[0]["out_x"]
```
